# Optimizing a Trainium2 kernel written in Bass

```python
import numpy as np
import jax
import jax.numpy as jnp

def _softmax(x, axis=-1):
    return jax.nn.softmax(x, axis=axis)

def _gelu(x):
    return jax.nn.gelu(x, approximate=True)

def _silu(x):
    return jax.nn.silu(x)

def _sigmoid(x):
    return jax.nn.sigmoid(x)

def _layernorm(x, axis=-1, eps=1e-05):
    m = jnp.mean(x, axis=axis, keepdims=True)
    v = jnp.var(x, axis=axis, keepdims=True)
    return (x - m) / jnp.sqrt(v + eps)

def _scatter_add(tgt, idx, src, axis=0):
    return tgt.at[idx].add(src)

def _segment_sum(src, seg, n):
    return jax.ops.segment_sum(src, seg, n)
kernel_name = 'mk_seq_postln_d2_jaxref_r8_02b5e2'

def setup_inputs(seed: int=0):
    np.random.seed(seed)
    _w = jnp.asarray

    def _L0_attn_setup():
        import jax, jax.numpy as jnp
        import numpy as np
        H = 16
        CHUNK = 64
        EPS = 1e-05

        def _forward(x, wq, wk, wv, wo, fq1_w, fq1_b, fq2_w, fq2_b, fk1_w, fk1_b, fk2_w, fk2_b, norm_w):
            B, L, D = x.shape
            dk = D // H

            def proj(w):
                return (x @ w.T).reshape(B, L, H, dk).transpose(0, 2, 1, 3)
            q, k, v = (proj(wq), proj(wk), proj(wv))
            q = (q @ fq1_w.T + fq1_b) * (q @ fq2_w.T + fq2_b)
            k = (k @ fk1_w.T + fk1_b) * (k @ fk2_w.T + fk2_b)
            scale = dk ** (-0.5)
            n = L // CHUNK
            qc = q.reshape(B, H, n, CHUNK, dk) * scale
            kc = k.reshape(B, H, n, CHUNK, dk)
            vc = v.reshape(B, H, n, CHUNK, dk)
            kv = jnp.einsum('bhncd,bhnce->bhnde', kc, vc)
            kv = jnp.cumsum(kv, axis=2)
            kv = jnp.concatenate([jnp.zeros_like(kv[:, :, :1]), kv[:, :, :-1]], axis=2)
            inter = jnp.einsum('bhncd,bhnde->bhnce', qc, kv)
            s = jnp.einsum('bhncd,bhnmd->bhncm', qc, kc)
            mask = jnp.tril(jnp.ones((CHUNK, CHUNK), bool))
            s = jnp.where(mask, s, 0.0)
            intra = jnp.einsum('bhncm,bhnmd->bhncd', s, vc)
            o = (inter + intra).reshape(B, H, L, dk)
            o = o * jax.lax.rsqrt(jnp.mean(o * o, axis=-1, keepdims=True) + EPS) * norm_w
            o = o.transpose(0, 2, 1, 3).reshape(B, L, D)
            return o @ wo.T
        key = jax.random.key(seed)
        ks = jax.random.split(key, 16)
        B, L, D = (2, 512, 256)
        dk = D // H
        g = 2 ** (-2.5)

        def xav(k, n):
            lim = g * np.sqrt(6.0 / (2 * n))
            return jax.random.uniform(k, (n, n), jnp.float32, -lim, lim)
        return {'x': jax.random.normal(ks[0], (B, L, D), jnp.float32), 'wq': xav(ks[1], D), 'wk': xav(ks[2], D), 'wv': xav(ks[3], D), 'wo': xav(ks[4], D), 'fq1_w': xav(ks[5], dk), 'fq1_b': jnp.zeros((dk,), jnp.float32), 'fq2_w': xav(ks[6], dk), 'fq2_b': jnp.zeros((dk,), jnp.float32), 'fk1_w': xav(ks[7], dk), 'fk1_b': jnp.zeros((dk,), jnp.float32), 'fk2_w': xav(ks[8], dk), 'fk2_b': jnp.zeros((dk,), jnp.float32), 'norm_w': jnp.ones((dk,), jnp.float32)}
    _L0_attn_in = _L0_attn_setup()

    def _L0_ffn_setup():
        import jax, jax.numpy as jnp
        import numpy as np
        import math
        N_EMBD = 256
        N_HEAD = 16
        HEAD_DIM = N_EMBD // N_HEAD
        B, T = (2, 256)
        key = jax.random.key(seed)
        k1, k2, k3 = jax.random.split(key, 3)
        x = jax.random.normal(k1, (B, T, N_EMBD), dtype=jnp.float32)
        W_gate = jax.random.normal(k2, (N_HEAD, N_EMBD), dtype=jnp.float32) * 0.02
        W_qkv = jax.random.normal(k3, (3 * N_EMBD, N_EMBD), dtype=jnp.float32) * 0.02
        return {'x': x, 'W_gate': W_gate, 'W_qkv': W_qkv}
    _L0_ffn_in = _L0_ffn_setup()

    def _L1_attn_setup():
        import jax, jax.numpy as jnp
        import numpy as np
        H = 32
        D = 64
        BS = 32
        LAYER_IDX = 0
        NUM_LAYERS = 32
        EPS = 1e-05

        def _decay_buffers():
            base = 1.0 / 2.0 ** (8.0 / H)
            rate = base ** (jnp.arange(H, dtype=jnp.float32) + 1.0)
            factor = 1.0 - LAYER_IDX / (NUM_LAYERS - 1 + 1e-05) + 1e-05
            slope = (rate * factor)[:, None, None]
            r = jnp.arange(BS, dtype=jnp.float32) + 1.0
            query_decay = jnp.exp(-slope * r[:, None])
            key_decay = jnp.exp(-slope * (BS - r[:, None]))
            dd = r[:, None] - r[None, :]
            dd = slope * dd[None, :, :]
            dd = jnp.where(dd >= 0, -dd, -jnp.inf)
            diagonal_decay = jnp.exp(dd)[None]
            block_decay = jnp.exp(-slope * BS)
            return (slope, query_decay, key_decay, diagonal_decay, block_decay)

        def _rmsnorm(x, w):
            v = jnp.mean(x.astype(jnp.float32) ** 2, axis=-1, keepdims=True)
            return (x * jax.lax.rsqrt(v + EPS)).astype(x.dtype) * w
        key = jax.random.key(seed)
        ks = jax.random.split(key, 4)
        b, s, hid = (2, 512, 256)
        return {'hidden_states': jax.random.normal(ks[0], (b, s, hid), jnp.float32), 'qkv_w': jax.random.normal(ks[1], (3 * H * D, hid), jnp.float32) * 0.02, 'out_w': jax.random.normal(ks[2], (hid, H * D), jnp.float32) * 0.02, 'gate_w': jax.random.normal(ks[3], (H * D, hid), jnp.float32) * 0.02, 'norm_w': jnp.ones((H * D,), jnp.float32)}
    _L1_attn_in = _L1_attn_setup()

    def _L1_ffn_setup():
        import jax, jax.numpy as jnp
        import numpy as np
        B, S, D = (2, 256, 256)
        H, KV, HD = (16, 4, 128)
        E, F, TOPK = (8, 512, 2)
        THETA = 1000000.0
        EPS = 1e-05

        def rmsnorm(x, w):
            var = jnp.mean(jnp.square(x), axis=-1, keepdims=True)
            return x * jax.lax.rsqrt(var + EPS) * w

        def rope_cos_sin(seq_len):
            inv_freq = 1.0 / THETA ** (jnp.arange(0, HD, 2, dtype=jnp.float32) / HD)
            ang = jnp.arange(seq_len, dtype=jnp.float32)[:, None] * inv_freq[None, :]
            return (jnp.cos(ang)[None, :, None, :], jnp.sin(ang)[None, :, None, :])

        def apply_rope(x, cos, sin):
            x1, x2 = jnp.split(x, 2, axis=-1)
            return jnp.concatenate([x1 * cos - x2 * sin, x2 * cos + x1 * sin], axis=-1)

        def attention(x, wq, wk, wv, wo):
            b, s, _ = x.shape
            q = (x @ wq).reshape(b, s, H, HD)
            k = (x @ wk).reshape(b, s, KV, HD)
            v = (x @ wv).reshape(b, s, KV, HD)
            cos, sin = rope_cos_sin(s)
            q = apply_rope(q, cos, sin)
            k = apply_rope(k, cos, sin)
            rep = H // KV
            k = jnp.repeat(k, rep, axis=2)
            v = jnp.repeat(v, rep, axis=2)
            scores = jnp.einsum('bqhd,bkhd->bhqk', q, k) / np.sqrt(HD)
            causal = jnp.tril(jnp.ones((s, s), dtype=bool))
            scores = jnp.where(causal[None, None], scores, jnp.finfo(scores.dtype).min)
            probs = jax.nn.softmax(scores, axis=-1)
            out = jnp.einsum('bhqk,bkhd->bqhd', probs, v).reshape(b, s, H * HD)
            return out @ wo

        def moe(x, gate_w, w1, w3, w2):
            b, s, d = x.shape
            xt = x.reshape(b * s, d)
            logits = xt @ gate_w
            topv, topi = jax.lax.top_k(logits, TOPK)
            probs = jax.nn.softmax(topv, axis=-1)
            w = jnp.zeros_like(logits)
            for kk in range(TOPK):
                w = w + jax.nn.one_hot(topi[:, kk], E, dtype=logits.dtype) * probs[:, kk:kk + 1]
            out = jnp.zeros_like(xt)
            for e in range(E):
                h = jax.nn.silu(xt @ w1[e]) * (xt @ w3[e])
                out = out + w[:, e:e + 1] * (h @ w2[e])
            return out.reshape(b, s, d)
        key = jax.random.key(seed)
        ks = jax.random.split(key, 10)
        init = lambda k, shape: jax.random.normal(k, shape, jnp.float32) * 0.02
        return {'hidden_states': jax.random.normal(ks[0], (B, S, D), jnp.float32), 'norm1_w': jnp.ones((D,), jnp.float32), 'norm2_w': jnp.ones((D,), jnp.float32), 'wq': init(ks[1], (D, H * HD)), 'wk': init(ks[2], (D, KV * HD)), 'wv': init(ks[3], (D, KV * HD)), 'wo': init(ks[4], (H * HD, D)), 'gate_w': init(ks[5], (D, E)), 'w1': init(ks[6], (E, D, F)), 'w3': init(ks[7], (E, D, F)), 'w2': init(ks[8], (E, F, D))}
    _L1_ffn_in = _L1_ffn_setup()
    _d = {'L0_attn_x': _L0_attn_in['x'], 'L0_attn_wq': _L0_attn_in['wq'], 'L0_attn_wk': _L0_attn_in['wk'], 'L0_attn_wv': _L0_attn_in['wv'], 'L0_attn_wo': _L0_attn_in['wo'], 'L0_attn_fq1_w': _L0_attn_in['fq1_w'], 'L0_attn_fq1_b': _L0_attn_in['fq1_b'], 'L0_attn_fq2_w': _L0_attn_in['fq2_w'], 'L0_attn_fq2_b': _L0_attn_in['fq2_b'], 'L0_attn_fk1_w': _L0_attn_in['fk1_w'], 'L0_attn_fk1_b': _L0_attn_in['fk1_b'], 'L0_attn_fk2_w': _L0_attn_in['fk2_w'], 'L0_attn_fk2_b': _L0_attn_in['fk2_b'], 'L0_attn_norm_w': _L0_attn_in['norm_w'], 'L0_ffn_W_gate': _L0_ffn_in['W_gate'], 'L0_ffn_W_qkv': _L0_ffn_in['W_qkv'], 'L1_attn_qkv_w': _L1_attn_in['qkv_w'], 'L1_attn_out_w': _L1_attn_in['out_w'], 'L1_attn_gate_w': _L1_attn_in['gate_w'], 'L1_attn_norm_w': _L1_attn_in['norm_w'], 'L1_ffn_norm1_w': _L1_ffn_in['norm1_w'], 'L1_ffn_norm2_w': _L1_ffn_in['norm2_w'], 'L1_ffn_wq': _L1_ffn_in['wq'], 'L1_ffn_wk': _L1_ffn_in['wk'], 'L1_ffn_wv': _L1_ffn_in['wv'], 'L1_ffn_wo': _L1_ffn_in['wo'], 'L1_ffn_gate_w': _L1_ffn_in['gate_w'], 'L1_ffn_w1': _L1_ffn_in['w1'], 'L1_ffn_w3': _L1_ffn_in['w3'], 'L1_ffn_w2': _L1_ffn_in['w2']}
    _x0 = _d['L0_attn_x']
    _d['L0_attn_x'] = jax.random.normal(jax.random.fold_in(jax.random.key(seed), 1), (4, 256, 256), dtype=_x0.dtype)
    del _x0
    return _d

def reference(L0_attn_x, L0_attn_wq, L0_attn_wk, L0_attn_wv, L0_attn_wo, L0_attn_fq1_w, L0_attn_fq1_b, L0_attn_fq2_w, L0_attn_fq2_b, L0_attn_fk1_w, L0_attn_fk1_b, L0_attn_fk2_w, L0_attn_fk2_b, L0_attn_norm_w, L0_ffn_W_gate, L0_ffn_W_qkv, L1_attn_qkv_w, L1_attn_out_w, L1_attn_gate_w, L1_attn_norm_w, L1_ffn_norm1_w, L1_ffn_norm2_w, L1_ffn_wq, L1_ffn_wk, L1_ffn_wv, L1_ffn_wo, L1_ffn_gate_w, L1_ffn_w1, L1_ffn_w3, L1_ffn_w2):

    def _L0_attn_ref(x, wq, wk, wv, wo, fq1_w, fq1_b, fq2_w, fq2_b, fk1_w, fk1_b, fk2_w, fk2_b, norm_w):
        import jax, jax.numpy as jnp
        import numpy as np
        H = 16
        CHUNK = 64
        EPS = 1e-05

        def _forward(x, wq, wk, wv, wo, fq1_w, fq1_b, fq2_w, fq2_b, fk1_w, fk1_b, fk2_w, fk2_b, norm_w):
            B, L, D = x.shape
            dk = D // H

            def proj(w):
                return (x @ w.T).reshape(B, L, H, dk).transpose(0, 2, 1, 3)
            q, k, v = (proj(wq), proj(wk), proj(wv))
            q = (q @ fq1_w.T + fq1_b) * (q @ fq2_w.T + fq2_b)
            k = (k @ fk1_w.T + fk1_b) * (k @ fk2_w.T + fk2_b)
            scale = dk ** (-0.5)
            n = L // CHUNK
            qc = q.reshape(B, H, n, CHUNK, dk) * scale
            kc = k.reshape(B, H, n, CHUNK, dk)
            vc = v.reshape(B, H, n, CHUNK, dk)
            kv = jnp.einsum('bhncd,bhnce->bhnde', kc, vc)
            kv = jnp.cumsum(kv, axis=2)
            kv = jnp.concatenate([jnp.zeros_like(kv[:, :, :1]), kv[:, :, :-1]], axis=2)
            inter = jnp.einsum('bhncd,bhnde->bhnce', qc, kv)
            s = jnp.einsum('bhncd,bhnmd->bhncm', qc, kc)
            mask = jnp.tril(jnp.ones((CHUNK, CHUNK), bool))
            s = jnp.where(mask, s, 0.0)
            intra = jnp.einsum('bhncm,bhnmd->bhncd', s, vc)
            o = (inter + intra).reshape(B, H, L, dk)
            o = o * jax.lax.rsqrt(jnp.mean(o * o, axis=-1, keepdims=True) + EPS) * norm_w
            o = o.transpose(0, 2, 1, 3).reshape(B, L, D)
            return o @ wo.T
        return _forward(x, wq, wk, wv, wo, fq1_w, fq1_b, fq2_w, fq2_b, fk1_w, fk1_b, fk2_w, fk2_b, norm_w)

    def _L0_ffn_ref(x, W_gate, W_qkv):
        import jax, jax.numpy as jnp
        import numpy as np
        import math
        N_EMBD = 256
        N_HEAD = 16
        HEAD_DIM = N_EMBD // N_HEAD
        B, T = (2, 256)
        Bb, Tt, C = x.shape
        H, hd = (N_HEAD, HEAD_DIM)
        gating = jax.nn.softmax(x @ W_gate.T, axis=-1)
        idx = jnp.argmax(gating, axis=-1)
        indicator = jax.nn.one_hot(idx, H, dtype=gating.dtype)
        top1_val = jnp.max(gating, axis=-1, keepdims=True)
        gating_top1 = indicator * top1_val
        qkv = x @ W_qkv.T
        q, k, v = jnp.split(qkv, 3, axis=-1)
        k = k.reshape(Bb, Tt, H, hd)
        v = v.reshape(Bb, Tt, H, hd)
        k_shared = jnp.einsum('bth,bthd->btd', indicator, k)
        v_shared = jnp.einsum('bth,bthd->btd', gating_top1, v)
        q = q.reshape(Bb, Tt, H, hd).transpose(0, 2, 1, 3)
        att = jnp.einsum('bhqd,bkd->bhqk', q, k_shared) * (1.0 / math.sqrt(hd))
        causal = jnp.tril(jnp.ones((Tt, Tt), dtype=bool))
        att = jnp.where(causal[None, None, :, :], att, -jnp.inf)
        att = jax.nn.softmax(att, axis=-1)
        y = jnp.einsum('bhqk,bkd->bhqd', att, v_shared)
        y = y.transpose(0, 2, 1, 3).reshape(Bb, Tt, C)
        return y

    def _L1_attn_ref(hidden_states, qkv_w, out_w, gate_w, norm_w):
        import jax, jax.numpy as jnp
        import numpy as np
        H = 32
        D = 64
        BS = 32
        LAYER_IDX = 0
        NUM_LAYERS = 32
        EPS = 1e-05

        def _decay_buffers():
            base = 1.0 / 2.0 ** (8.0 / H)
            rate = base ** (jnp.arange(H, dtype=jnp.float32) + 1.0)
            factor = 1.0 - LAYER_IDX / (NUM_LAYERS - 1 + 1e-05) + 1e-05
            slope = (rate * factor)[:, None, None]
            r = jnp.arange(BS, dtype=jnp.float32) + 1.0
            query_decay = jnp.exp(-slope * r[:, None])
            key_decay = jnp.exp(-slope * (BS - r[:, None]))
            dd = r[:, None] - r[None, :]
            dd = slope * dd[None, :, :]
            dd = jnp.where(dd >= 0, -dd, -jnp.inf)
            diagonal_decay = jnp.exp(dd)[None]
            block_decay = jnp.exp(-slope * BS)
            return (slope, query_decay, key_decay, diagonal_decay, block_decay)

        def _rmsnorm(x, w):
            v = jnp.mean(x.astype(jnp.float32) ** 2, axis=-1, keepdims=True)
            return (x * jax.lax.rsqrt(v + EPS)).astype(x.dtype) * w
        b, s, hid = hidden_states.shape
        nb = s // BS
        _, qd, kd, dd, bd = _decay_buffers()
        qkv = jax.nn.silu(hidden_states @ qkv_w.T)
        qkv = qkv.reshape(b, s, H, 3 * D)
        q, k, v = jnp.split(qkv, 3, axis=-1)

        def to_blocks(t):
            return t.transpose(0, 2, 1, 3).reshape(b, H, nb, BS, D).transpose(2, 0, 1, 3, 4)
        qb, kb, vb = (to_blocks(q), to_blocks(k), to_blocks(v))
        qd_ = qd[None]
        kd_ = kd[None]
        bd_ = bd[None]

        def step(state, blk):
            qi, ki, vi = blk
            aw = jnp.einsum('bhid,bhjd->bhij', qi, ki) * dd
            intra = jnp.einsum('bhij,bhjd->bhid', aw, vi)
            inter = jnp.einsum('bhid,bhde->bhie', qi * qd_, state)
            new_state = state * bd_ + jnp.einsum('bhsd,bhse->bhde', ki * kd_, vi)
            return (new_state, intra + inter)
        state0 = jnp.zeros((b, H, D, D), hidden_states.dtype)
        _, ys = jax.lax.scan(step, state0, (qb, kb, vb))
        attn = ys.transpose(1, 2, 0, 3, 4).reshape(b, H, s, D)
        attn = attn.transpose(0, 2, 1, 3).reshape(b, s, H * D)
        attn = _rmsnorm(attn, norm_w)
        gate = jax.nn.sigmoid(hidden_states @ gate_w.T)
        return gate * attn @ out_w.T

    def _L1_ffn_ref(hidden_states, norm1_w, norm2_w, wq, wk, wv, wo, gate_w, w1, w3, w2):
        import jax, jax.numpy as jnp
        import numpy as np
        B, S, D = (2, 256, 256)
        H, KV, HD = (16, 4, 128)
        E, F, TOPK = (8, 512, 2)
        THETA = 1000000.0
        EPS = 1e-05

        def rmsnorm(x, w):
            var = jnp.mean(jnp.square(x), axis=-1, keepdims=True)
            return x * jax.lax.rsqrt(var + EPS) * w

        def rope_cos_sin(seq_len):
            inv_freq = 1.0 / THETA ** (jnp.arange(0, HD, 2, dtype=jnp.float32) / HD)
            ang = jnp.arange(seq_len, dtype=jnp.float32)[:, None] * inv_freq[None, :]
            return (jnp.cos(ang)[None, :, None, :], jnp.sin(ang)[None, :, None, :])

        def apply_rope(x, cos, sin):
            x1, x2 = jnp.split(x, 2, axis=-1)
            return jnp.concatenate([x1 * cos - x2 * sin, x2 * cos + x1 * sin], axis=-1)

        def attention(x, wq, wk, wv, wo):
            b, s, _ = x.shape
            q = (x @ wq).reshape(b, s, H, HD)
            k = (x @ wk).reshape(b, s, KV, HD)
            v = (x @ wv).reshape(b, s, KV, HD)
            cos, sin = rope_cos_sin(s)
            q = apply_rope(q, cos, sin)
            k = apply_rope(k, cos, sin)
            rep = H // KV
            k = jnp.repeat(k, rep, axis=2)
            v = jnp.repeat(v, rep, axis=2)
            scores = jnp.einsum('bqhd,bkhd->bhqk', q, k) / np.sqrt(HD)
            causal = jnp.tril(jnp.ones((s, s), dtype=bool))
            scores = jnp.where(causal[None, None], scores, jnp.finfo(scores.dtype).min)
            probs = jax.nn.softmax(scores, axis=-1)
            out = jnp.einsum('bhqk,bkhd->bqhd', probs, v).reshape(b, s, H * HD)
            return out @ wo

        def moe(x, gate_w, w1, w3, w2):
            b, s, d = x.shape
            xt = x.reshape(b * s, d)
            logits = xt @ gate_w
            topv, topi = jax.lax.top_k(logits, TOPK)
            probs = jax.nn.softmax(topv, axis=-1)
            w = jnp.zeros_like(logits)
            for kk in range(TOPK):
                w = w + jax.nn.one_hot(topi[:, kk], E, dtype=logits.dtype) * probs[:, kk:kk + 1]
            out = jnp.zeros_like(xt)
            for e in range(E):
                h = jax.nn.silu(xt @ w1[e]) * (xt @ w3[e])
                out = out + w[:, e:e + 1] * (h @ w2[e])
            return out.reshape(b, s, d)
        attn_out = attention(rmsnorm(hidden_states, norm1_w), wq, wk, wv, wo)
        h = hidden_states + attn_out
        out = h + moe(rmsnorm(h, norm2_w), gate_w, w1, w3, w2)
        return out
    x = L0_attn_x
    x = _layernorm(x + _L0_attn_ref(x, L0_attn_wq, L0_attn_wk, L0_attn_wv, L0_attn_wo, L0_attn_fq1_w, L0_attn_fq1_b, L0_attn_fq2_w, L0_attn_fq2_b, L0_attn_fk1_w, L0_attn_fk1_b, L0_attn_fk2_w, L0_attn_fk2_b, L0_attn_norm_w), axis=-1)
    x = _layernorm(x + _L0_ffn_ref(x, L0_ffn_W_gate, L0_ffn_W_qkv), axis=-1)
    x = _layernorm(x + _L1_attn_ref(x, L1_attn_qkv_w, L1_attn_out_w, L1_attn_gate_w, L1_attn_norm_w), axis=-1)
    x = _layernorm(x + _L1_ffn_ref(x, L1_ffn_norm1_w, L1_ffn_norm2_w, L1_ffn_wq, L1_ffn_wk, L1_ffn_wv, L1_ffn_wo, L1_ffn_gate_w, L1_ffn_w1, L1_ffn_w3, L1_ffn_w2), axis=-1)
    return x

_drawn_inputs = setup_inputs


def setup_inputs(seed=0):
    import zlib

    import numpy as np

    out = dict(_drawn_inputs(seed))
    spreads = {'L0_attn_fq1_b': (0.0, 0.665),
     'L0_attn_fq2_b': (0.0, 0.617),
     'L0_attn_fk1_b': (0.0, 0.551),
     'L0_attn_fk2_b': (0.0, 0.725),
     'L0_attn_norm_w': (1.0, 0.6),
     'L1_attn_norm_w': (1.0, 0.2),
     'L1_ffn_norm1_w': (1.0, 0.6),
     'L1_ffn_norm2_w': (1.0, 0.6)}
    factors = {'L0_attn_wq': 7.338,
     'L0_attn_wk': 5.827,
     'L0_attn_wv': 4.002,
     'L0_attn_wo': 4.078,
     'L0_attn_fq1_w': 6.216,
     'L0_attn_fq2_w': 8.0,
     'L0_attn_fk1_w': 8.0,
     'L0_attn_fk2_w': 5.429,
     'L1_ffn_wq': 8.0,
     'L1_ffn_wk': 8.0,
     'L1_ffn_gate_w': 6.91,
     'L1_ffn_w1': 6.185,
     'L1_ffn_w3': 6.109,
     'L1_ffn_w2': 6.122}
    for name, (base, spread) in spreads.items():
        noise = np.random.default_rng([zlib.crc32(name.encode()), seed]).standard_normal(out[name].shape)
        drawn = base * np.exp(spread * noise) if base else spread * noise
        out[name] = jnp.asarray(drawn.astype(out[name].dtype))
    for name, factor in factors.items():
        out[name] = (out[name] * factor).astype(out[name].dtype)
    return out
```

```python
from contextlib import ExitStack

import numpy as np

import concourse.bass as bass
from concourse import mybir

F32 = mybir.dt.float32
F32R = mybir.dt.float32r
BF16 = mybir.dt.bfloat16
ALU = mybir.AluOpType
ACT = mybir.ActivationFunctionType
X = mybir.AxisListType.X

P = 128
LEAD = 8
EPS = 1e-5
BATCH, SEQ, D = 4, 256, 256
TOK = BATCH * SEQ
NT = TOK // P
KD = D // P
TPB = SEQ // P
CAUSAL = 384

H0, HD0 = 16, 16
H1, HD1 = 32, 64
PAIRS = H1 // 2
HQ, HKV, HDQ = 16, 4, 128
GROUP = HQ // HKV
EXPERTS, FF = 8, 512

C_IDENT = 0
C_TRI = C_IDENT + P
C_NEG = C_TRI + CAUSAL
C_PAR = C_NEG + CAUSAL
C_IOTA = C_PAR + 2
C_END = C_IOTA + 16


class Core:

    def __init__(self, nc, dram, out, ctx):
        self.nc, self.dram, self.out, self.ctx = nc, dram, out, ctx
        self.ps = ctx.enter_context(nc.psum_tensor("ps", [P, 8, 512], F32))
        self.norm_sems, self.norm_counts = None, dict.fromkeys(
            "w_in stat_done mean_done var_ready sd_ready rstd_ready n_ready turn_ps hi_ready lo_ready stored".split(), 0)
        self.consts = self.tile(ctx, "consts", [P, C_END])
        self.ident = self.consts[:, C_IDENT:C_IDENT + P]
        self.tri = self.consts[:, C_TRI:C_TRI + CAUSAL]
        self.parity = self.consts[:, C_PAR:C_PAR + 2]
        self.iota = self.consts[:, C_IOTA:C_IOTA + 16]
        self.ident16 = self.tile(ctx, "ident16", [P, P], BF16)
        self.neg16 = self.tile(ctx, "neg16", [P, CAUSAL], BF16)
        self.warm16 = self.tile(ctx, "warm16", [P, 512], BF16)
        self.x = self.tile(ctx, "x", [P, NT, D])
        self.y = self.tile(ctx, "y", [P, NT, D])
        self.scratch = self.tile(ctx, "scratch", [P, NT, D])
        self.xT = self.tile(ctx, "xT", [P, KD, TOK])
        self.xTh = self.tile(ctx, "xTh", [P, KD, TOK], F32R)
        self.xTl = self.tile(ctx, "xTl", [P, KD, TOK], F32R)

    def tile(self, ctx, name, shape, dt=F32):
        return ctx.enter_context(self.nc.sbuf_tensor(name, shape, dt))

    def sems(self, ctx, prefix, names):
        return [self.ctx.enter_context(self.nc.semaphore(f"{prefix}_{n}")) for n in names.split()]


def give_lead(eng, sems):
    for s in sems:
        eng.sem_inc(s, LEAD)


class Chain:

    def __init__(self, eng, sem, base=0):
        self.eng, self.sem, self.base, self.n = eng, sem, base, 0

    def __call__(self, ins):
        self.n += 1
        ins.then_inc(self.sem, 1)
        self.eng.wait_ge(self.sem, self.base + self.n)


def split_product(pe, out, wh, wl, xh, xl, ks, skip=False):
    passes = [(wh, xl), (wl, xh), (wh, xh)]
    n = 0
    for k in ks:
        for w, x in passes:
            mm = pe.matmul(out, w(k), x(k), start=(n == 0), stop=(n == 3 * len(ks) - 1))
            n += 1
    return mm


def keep_warm(c, pe, out, n):
    for _ in range(n):
        pe.matmul(out, c.ident16[:], c.warm16[:], start=True, stop=True)


def layer0_linear_attention(c):
    nc, ps = c.nc, c.ps
    SLOTS = 2
    QUADS = 4
    PAD = 32
    with ExitStack() as ctx:
        def sb(name, shape, dt=F32):
            return c.tile(ctx, "a_" + name, shape, dt)

        w = sb("w", [P, 3, KD, D])
        wh = sb("wh", [P, 3, KD, D], F32R)
        wl = sb("wl", [P, 3, KD, D], F32R)
        maps = sb("maps", [P, 4, P])
        vecs = sb("vecs", [P, 5])
        wo = sb("wo", [P, KD, D])
        q_all = sb("q_all", [P, KD, TOK])
        k_all = sb("k_all", [P, KD, TOK])
        v_all = sb("v_all", [P, NT, D])
        v_pad = sb("v_pad", [P, SLOTS, TPB, H0, PAD])
        second = sb("second", [P, 3, KD, SEQ])
        q_par = sb("q_par", [P, 2, KD, SEQ])
        k_map = sb("k_map", [P, KD, SEQ])
        s_m = sb("s_m", [P, 8, CAUSAL])
        o_sb = sb("o_sb", [P, 2, 512])
        o_sq = sb("o_sq", [P, TPB, D])
        o_n = sb("o_n", [P, TPB, D])
        o_nT = sb("o_nT", [P, KD, SEQ])
        stat = sb("stat", [P, 4, TPB * H0])

        x_in, w_in, loaded = c.sems(ctx, "a", "x_in w_in loaded")
        pe_sems = p_ps, map_ps, s_ps, pv_ps, o_turned, on_turned, wo_ps = c.sems(ctx, "a", "p_ps map_ps s_ps pv_ps o_turned on_turned wo_ps")
        dve_sems = x_split, w_hi, w_split, v_copied, qmap_ready, kmap_ready, sm_ready, sum_ready, var_ready, r_ready, on_ready, oT_ready, y_ready, second_q = c.sems(
            ctx, "a", "x_split w_hi w_split v_copied qmap_ready kmap_ready sm_ready sum_ready var_ready r_ready on_ready oT_ready y_ready second_q")
        act_sems = x_hi, p_ready, second_k, o_ready, sq_ready, sd_ready = c.sems(ctx, "a", "x_hi p_ready second_k o_ready sq_ready sd_ready")
        (zeroed,) = c.sems(ctx, "a", "zeroed")
        block = ctx.enter_context(nc.Block())

        @block.sync
        def _(sp):
            for k in range(KD):
                sp.dma_start(c.xT[:, k, :], c.dram["xT"][:, k, :]).then_inc(x_in, 16)
            sp.dma_start(w[:], c.dram["w0"]).then_inc(w_in, 16)
            sp.dma_start(maps[:], c.dram["maps"]).then_inc(loaded, 16)
            sp.dma_start(vecs[:], c.dram["vecs"]).then_inc(loaded, 16)
            sp.dma_start(c.consts[:], c.dram["consts"]).then_inc(loaded, 16)
            sp.dma_start(wo[:], c.dram["wo0"]).then_inc(loaded, 16)
            sp.dma_start(c.x[:], c.dram["x"]).then_inc(loaded, 16)

        @block.gpsimd
        def _(pool):
            pool.memset(c.warm16[:], 0.0).then_inc(zeroed, 1)
            pool.memset(v_pad[:], 0.0).then_inc(zeroed, 1)

        @block.vector
        def _(dve):
            give_lead(dve, dve_sems)
            for k in range(KD):
                dve.wait_ge(x_hi, LEAD + k + 1)
                dve.tensor_tensor(c.xTl[:, k, :], c.xT[:, k, :], c.xTh[:, k, :].bitcast(F32), ALU.subtract).then_inc(x_split, 1)
            dve.wait_ge(w_in, 16)
            for n in range(3):
                dve.tensor_copy(wh[:, n], w[:, n]).then_inc(w_hi, 1)
                dve.wait_ge(w_hi, LEAD + n + 1)
                dve.tensor_tensor(wl[:, n], w[:, n], wh[:, n].bitcast(F32), ALU.subtract).then_inc(w_split, 1)
            dve.wait_ge(loaded, 16 * 5)
            dve.tensor_copy(c.ident16[:], c.ident)
            dve.tensor_copy(c.neg16[:], c.consts[:, C_NEG:C_NEG + CAUSAL])
            dve.wait_ge(p_ready, LEAD + 12)
            dve.wait_ge(zeroed, 2)
            with dve.Fori(0, BATCH // SLOTS) as i:
                def at(u):
                    return SLOTS * i + u

                def prepare(u):
                    dve.wait_ge(pv_ps, LEAD + QUADS * (SLOTS * i + u) - QUADS * SLOTS + QUADS)
                    dve.tensor_scalar(v_pad[:, u].rearrange("p t h r -> p (t h) r")[:, :, 0:HD0],
                                      v_all[:, bass.ds(at(u) * TPB, TPB), :].rearrange("p t (h d) -> p (t h) d", h=H0), 1.0, None, ALU.mult).then_inc(v_copied, 1)
                    dve.wait_ge(map_ps, LEAD + 2 * at(u) + 1)
                    for par in range(2):
                        dve.tensor_scalar(second[:, par].rearrange("p k s -> p (k s)"), ps[:, 4, :], vecs[:, 1:2],
                                          c.parity[:, par:par + 1], ALU.add, ALU.mult).then_inc(second_q, 1)
                    for par in range(2):
                        dve.wait_ge(second_q, LEAD + 2 * at(u) + par + 1)
                        dve.scalar_tensor_tensor(q_par[:, par].rearrange("p k s -> p (k s)"), ps[:, 3, :], vecs[:, 0:1],
                                                 second[:, par].rearrange("p k s -> p (k s)"), ALU.add, ALU.mult).then_inc(qmap_ready, 1)
                    dve.wait_ge(map_ps, LEAD + 2 * at(u) + 2)
                    dve.wait_ge(second_k, LEAD + at(u) + 1)
                    dve.scalar_tensor_tensor(k_map[:].rearrange("p k s -> p (k s)"), ps[:, 5, :], vecs[:, 2:3],
                                             second[:, 2].rearrange("p k s -> p (k s)"), ALU.add, ALU.mult).then_inc(kmap_ready, 1)

                def masks(u, quad):
                    for h in range(4 * quad, 4 * quad + 4):
                        dve.wait_ge(s_ps, LEAD + H0 * at(u) + h + 1)
                        dve.wait_ge(pv_ps, LEAD + QUADS * at(u) + quad - 1)
                        dve.tensor_tensor(s_m[:, h % 8, :], ps[:, 3 + h % 4, 0:CAUSAL], c.tri, ALU.mult).then_inc(sm_ready, 1)

                def moments(u):
                    dve.wait_ge(sq_ready, LEAD + TPB * (at(u) + 1))
                    dve.tensor_reduce(stat[:, 0, :], o_sq[:].rearrange("p t (h d) -> p (t h) d", h=H0), X, ALU.add).then_inc(sum_ready, 1)
                    dve.wait_ge(sum_ready, LEAD + at(u) + 1)
                    dve.tensor_scalar(stat[:, 1, :], stat[:, 0, :], 1.0 / HD0, EPS, ALU.mult, ALU.add).then_inc(var_ready, 1)

                def scale(u):
                    dve.wait_ge(sd_ready, LEAD + at(u) + 1)
                    dve.reciprocal(stat[:, 3, :], stat[:, 2, :]).then_inc(r_ready, 1)
                    dve.wait_ge(r_ready, LEAD + at(u) + 1)
                    for t in range(TPB):
                        dve.tensor_tensor(o_n[:, t, :].rearrange("p (h d) -> p h d", h=H0), ps[:, 1 + t, :].rearrange("p (h r) -> p h r", h=H0)[:, :, 0:HD0],
                                          stat[:, 3, t * H0:(t + 1) * H0].unsqueeze(2).broadcast_to((P, H0, HD0)), ALU.mult).then_inc(on_ready, 1)

                def weigh(u):
                    dve.wait_ge(on_turned, LEAD + at(u) + 1)
                    dve.tensor_scalar(o_nT[:].rearrange("p k s -> p (k s)"), ps[:, 1, :], vecs[:, 4:5], None, ALU.mult).then_inc(oT_ready, 1)

                def add(u):
                    dve.wait_ge(wo_ps, LEAD + at(u) + 1)
                    dve.tensor_tensor(c.y[:, bass.ds(at(u) * TPB, TPB), :], ps[:, 2, :].rearrange("p (t d) -> p t d", t=TPB),
                                      c.x[:, bass.ds(at(u) * TPB, TPB), :], ALU.add).then_inc(y_ready, 1)

                prepare(0)
                for quad in range(QUADS):
                    masks(0, quad)
                prepare(1)
                masks(1, 0)
                moments(0)
                masks(1, 1)
                scale(0)
                masks(1, 2)
                weigh(0)
                masks(1, 3)
                add(0)
                moments(1)
                scale(1)
                weigh(1)
                add(1)

        @block.scalar
        def _(act):
            give_lead(act, act_sems)
            for k in range(KD):
                act.wait_ge(x_in, 16 * KD)
                act.activation(c.xTh[:, k, :], c.xT[:, k, :], ACT.Copy).then_inc(x_hi, 1)
            for n in range(12):
                act.wait_ge(p_ps, LEAD + n + 1)
                if n < 8:
                    half, a, m = n // 4, n // 2 % 2, n % 2
                    dst = (q_all, k_all)[a][:, m, half * 512:(half + 1) * 512]
                else:
                    dst = v_all[:, 2 * (n - 8):2 * (n - 7), :].rearrange("p t d -> p (t d)")
                act.activation(dst, ps[:, n % 8, :], ACT.Copy).then_inc(p_ready, 1)
            with act.Fori(0, BATCH // SLOTS) as i:
                def prepare(u):
                    act.wait_ge(map_ps, LEAD + 2 * (SLOTS * i + u) + 2)
                    act.activation(second[:, 2].rearrange("p k s -> p (k s)"), ps[:, 6, :], ACT.Identity, bias=vecs[:, 3:4]).then_inc(second_k, 1)

                def outputs(u):
                    for half in range(2):
                        act.wait_ge(pv_ps, LEAD + QUADS * (SLOTS * i + u) + 2 * half + 2)
                        act.wait_ge(o_turned, LEAD + TPB * (SLOTS * i + u))
                        act.activation(o_sb[:, half, :], ps[:, 7 * half, :], ACT.Copy).then_inc(o_ready, 1)

                def squares(u):
                    for t in range(TPB):
                        act.wait_ge(o_turned, LEAD + TPB * (SLOTS * i + u) + t + 1)
                        act.wait_ge(sum_ready, LEAD + SLOTS * i + u)
                        act.activation(o_sq[:, t, :].rearrange("p (h d) -> p h d", h=H0), ps[:, 1 + t, :].rearrange("p (h r) -> p h r", h=H0)[:, :, 0:HD0],
                                       ACT.Square).then_inc(sq_ready, 1)

                def root(u):
                    act.wait_ge(var_ready, LEAD + SLOTS * i + u + 1)
                    act.activation(stat[:, 2, :], stat[:, 1, :], ACT.Sqrt).then_inc(sd_ready, 1)

                prepare(0)
                outputs(0)
                prepare(1)
                squares(0)
                root(0)
                outputs(1)
                squares(1)
                root(1)

        @block.tensor
        def _(pe):
            give_lead(pe, pe_sems)
            pe.wait_ge(x_split, LEAD + 2)
            for n in range(12):
                pe.wait_ge(w_split, LEAD + (n // 2 % 2 + 1 if n < 8 else 3))
                if n >= 8:
                    pe.wait_ge(p_ready, LEAD + n - 7)
                if n < 8:
                    half, a, m = slice(n // 4 * 512, (n // 4 + 1) * 512), n // 2 % 2, n % 2
                    mm = split_product(pe, ps[:, n % 8, :], lambda k: wh[:, a, k, m * P:(m + 1) * P], lambda k: wl[:, a, k, m * P:(m + 1) * P],
                                       lambda k: c.xTh[:, k, half], lambda k: c.xTl[:, k, half], range(KD))
                else:
                    for t in range(2):
                        tok = slice((2 * (n - 8) + t) * P, (2 * (n - 8) + t + 1) * P)
                        mm = split_product(pe, ps[:, n % 8, t * D:(t + 1) * D], lambda k: c.xTh[:, k, tok], lambda k: c.xTl[:, k, tok],
                                           lambda k: wh[:, 2, k, :], lambda k: wl[:, 2, k, :], range(KD))
                mm.then_inc(p_ps, 1)
            pe.wait_ge(p_ready, LEAD + 12)
            pe.wait_ge(loaded, 16 * 5)
            with pe.Fori(0, BATCH // SLOTS) as i:
                def at(u):
                    return SLOTS * i + u

                def prepare(u):
                    pe.wait_ge(sm_ready, LEAD + H0 * at(u))
                    for n, raw in enumerate((q_all, k_all)):
                        for f in range(2):
                            for m in range(KD):
                                mm = pe.matmul(ps[:, 3 + 2 * n + f, m * SEQ:(m + 1) * SEQ], maps[:, 2 * n + f, :], raw[:, m, bass.ds(at(u) * SEQ, SEQ)],
                                               start=True, stop=True)
                        mm.then_inc(map_ps, 1)

                def scores(u, quad):
                    if quad == 0:
                        pe.wait_ge(qmap_ready, LEAD + 2 * at(u) + 2)
                        pe.wait_ge(kmap_ready, LEAD + at(u) + 1)
                    for h in range(4 * quad, 4 * quad + 4):
                        m, g, par = h // 8, 32 * (h % 8 // 2), h % 2
                        bank = ps[:, 3 + h % 4, :]
                        if h >= 4:
                            pe.wait_ge(sm_ready, LEAD + H0 * at(u) + h - 3)
                        pe.matmul(bank[:, 0:SEQ], k_map[g:g + 32, m, 0:P], q_par[g:g + 32, par, m, :], start=True, stop=True, tile_position=(g, 0))
                        pe.matmul(bank[:, SEQ:CAUSAL], k_map[g:g + 32, m, P:SEQ], q_par[g:g + 32, par, m, P:SEQ], start=True, stop=True,
                                  tile_position=(g, 0)).then_inc(s_ps, 1)

                def values(u, quad):
                    if quad == 0:
                        pe.wait_ge(v_copied, LEAD + at(u) + 1)
                    if quad % 2 == 0:
                        pe.wait_ge(o_ready, LEAD + 2 * at(u) + quad // 2 - 1)
                    pe.wait_ge(sm_ready, LEAD + H0 * at(u) + 4 * quad + 4)
                    out = ps[:, 7 * (quad // 2), quad % 2 * SEQ:(quad % 2 + 1) * SEQ]
                    for q in range(4):
                        h = 4 * quad + q
                        pe.matmul(out[PAD * q:PAD * (q + 1), :], v_pad[:, u, 0, h, :], s_m[:, h % 8, 0:SEQ], start=True, stop=False)
                    for q in range(4):
                        h = 4 * quad + q
                        mm = pe.matmul(out[PAD * q:PAD * (q + 1), P:SEQ], v_pad[:, u, 1, h, :], s_m[:, h % 8, SEQ:CAUSAL], start=False, stop=True)
                    mm.then_inc(pv_ps, 1)

                def turn(u):
                    pe.wait_ge(o_ready, LEAD + 2 * at(u) + 2)
                    pe.wait_ge(y_ready, LEAD + at(u))
                    for t in range(TPB):
                        for j in range(4):
                            mm = pe.transpose(ps[:, 1 + t, j * P:(j + 1) * P], o_sb[:, j // 2, j % 2 * SEQ + t * P:j % 2 * SEQ + (t + 1) * P], c.ident)
                        mm.then_inc(o_turned, 1)

                def turn_back(u):
                    pe.wait_ge(on_ready, LEAD + TPB * (at(u) + 1))
                    for t in range(TPB):
                        for m in range(KD):
                            mm = pe.transpose(ps[:, 1, m * SEQ + t * P:m * SEQ + (t + 1) * P], o_n[:, t, m * P:(m + 1) * P], c.ident)
                    mm.then_inc(on_turned, 1)

                def project(u):
                    pe.wait_ge(oT_ready, LEAD + at(u) + 1)
                    for t in range(TPB):
                        for k in range(KD):
                            mm = pe.matmul(ps[:, 2, t * D:(t + 1) * D], o_nT[:, k, t * P:(t + 1) * P], wo[:, k, :], start=(k == 0), stop=(k == KD - 1))
                    mm.then_inc(wo_ps, 1)

                prepare(0)
                scores(0, 0)
                for quad in range(1, QUADS):
                    scores(0, quad)
                    values(0, quad - 1)
                values(0, QUADS - 1)
                prepare(1)
                turn(0)
                scores(1, 0)
                scores(1, 1)
                values(1, 0)
                scores(1, 2)
                turn_back(0)
                values(1, 1)
                scores(1, 3)
                values(1, 2)
                project(0)
                values(1, 3)
                turn(1)
                turn_back(1)
                project(1)


def normalise(c, tag, src, dst, rms=False, turned=None, weight=None, store=False):
    nc, ps = c.nc, c.ps
    with ExitStack() as ctx:
        def sb(name, shape, dt=F32):
            return c.tile(ctx, f"{tag}_{name}", shape, dt)

        stats = sb("stats", [P, NT, 6])
        mv = sb("mv", [P, NT, 2])
        var = sb("var", [P, NT])
        sd = sb("sd", [P, NT])
        rstd = sb("rstd", [P, NT])
        junk = sb("junk", [P, D])
        wcol = sb("wcol", [P, KD])
        names = "w_in stat_done mean_done var_ready sd_ready rstd_ready n_ready turn_ps hi_ready lo_ready stored"
        if not c.norm_sems:
            c.norm_sems = c.sems(ctx, "norm", names)
        w_in, stat_done, mean_done, var_ready, sd_ready, rstd_ready, n_ready, turn_ps, hi_ready, lo_ready, stored = c.norm_sems
        so = dict(c.norm_counts)
        block = ctx.enter_context(nc.Block())

        @block.sync
        def _(sp):
            if weight is not None:
                sp.dma_start(wcol[:], weight).then_inc(w_in, 16)
            if store:
                for t in range(NT):
                    sp.wait_ge(n_ready, so["n_ready"] + t + 1)
                    sp.dma_start(c.out[:, t, :], dst[:, t, :]).then_inc(stored, 16)
                sp.wait_ge(stored, so["stored"] + 16 * NT)

        @block.vector
        def _(dve):
            if rms:
                dve.wait_ge(stat_done, so["stat_done"] + NT)
                dve.tensor_scalar(var[:], sd[:], 1.0 / D, EPS, ALU.mult, ALU.add).then_inc(var_ready, 1)
            else:
                for t in range(NT):
                    dve.bn_stats(stats[:, t, :], src[:, t, :]).then_inc(stat_done, 1)
                dve.wait_ge(stat_done, so["stat_done"] + NT)
                for t in range(NT):
                    dve.bn_aggr(mv[:, t, :], stats[:, t, :]).then_inc(mean_done, 1)
                dve.wait_ge(mean_done, so["mean_done"] + NT)
                dve.tensor_scalar(var[:], mv[:, :, 1], EPS, None, ALU.add).then_inc(var_ready, 1)
            dve.wait_ge(sd_ready, so["sd_ready"] + 1)
            dve.reciprocal(rstd[:], sd[:]).then_inc(rstd_ready, 1)
            dve.wait_ge(rstd_ready, so["rstd_ready"] + 1)
            for t in range(NT):
                if rms:
                    dve.tensor_scalar(dst[:, t, :], src[:, t, :], rstd[:, t:t + 1], None, ALU.mult).then_inc(n_ready, 1)
                else:
                    dve.tensor_scalar(dst[:, t, :], src[:, t, :], mv[:, t, 0:1], rstd[:, t:t + 1], ALU.subtract, ALU.mult).then_inc(n_ready, 1)
            if turned in ("split", "both"):
                for n in range(4):
                    half, k = n // 2, n % 2
                    dve.wait_ge(hi_ready, so["hi_ready"] + n + 1)
                    cols = slice(half * 512, (half + 1) * 512)
                    if weight is None:
                        dve.tensor_tensor(c.xTl[:, k, cols], ps[:, n, :], c.xTh[:, k, cols].bitcast(F32), ALU.subtract).then_inc(lo_ready, 1)
                    else:
                        dve.scalar_tensor_tensor(c.xTl[:, k, cols], ps[:, n, :], wcol[:, k:k + 1], c.xTh[:, k, cols].bitcast(F32),
                                                 ALU.mult, ALU.subtract).then_inc(lo_ready, 1)

        @block.scalar
        def _(act):
            if rms:
                for t in range(NT):
                    if t >= 1:
                        act.wait_ge(stat_done, so["stat_done"] + t)
                    act.activation(junk[:], src[:, t, :], ACT.Square, accum_out=sd[:, t:t + 1]).then_inc(stat_done, 1)
            act.wait_ge(var_ready, so["var_ready"] + 1)
            act.activation(sd[:], var[:], ACT.Sqrt).then_inc(sd_ready, 1)
            if weight is not None:
                act.wait_ge(w_in, so["w_in"] + 16)
            for n in range(4 if turned else 0):
                half, k = n // 2, n % 2
                act.wait_ge(turn_ps, so["turn_ps"] + n + 1)
                if turned == "both":
                    act.activation(c.xT[:, k, half * 512:(half + 1) * 512], ps[:, n, :], ACT.Copy)
                to = (c.xT if turned == "whole" else c.xTh)[:, k, half * 512:(half + 1) * 512]
                if weight is None:
                    act.activation(to, ps[:, n, :], ACT.Copy).then_inc(hi_ready, 1)
                else:
                    act.activation(to, ps[:, n, :], ACT.Copy, scale=wcol[:, k:k + 1]).then_inc(hi_ready, 1)

        @block.tensor
        def _(pe):
            for n in range(4 if turned else 0):
                half, k = n // 2, n % 2
                pe.wait_ge(n_ready, so["n_ready"] + 4 * half + 4)
                for t in range(4):
                    mm = pe.transpose(ps[:, n, t * P:(t + 1) * P], dst[:, 4 * half + t, k * P:(k + 1) * P], c.ident)
                mm.then_inc(turn_ps, 1)

        raised = {"stat_done": NT, "mean_done": 0 if rms else NT, "var_ready": 1, "sd_ready": 1, "rstd_ready": 1, "n_ready": NT,
                  "w_in": 16 if weight is not None else 0, "turn_ps": 4 if turned else 0, "hi_ready": 4 if turned else 0,
                  "lo_ready": 4 if turned in ("split", "both") else 0, "stored": 16 * NT if store else 0}
        c.norm_counts = {n: so[n] + raised[n] for n in raised}


def layer0_gated_attention(c):
    nc, ps = c.nc, c.ps
    QKV = 3 * D
    SLOTS = 2
    ITEMS = SLOTS * H0
    QUADS = ITEMS // 4
    PAD = 32
    with ExitStack() as ctx:
        def sb(name, shape, dt=F32):
            return c.tile(ctx, "g_" + name, shape, dt)

        w = sb("w", [P, KD, QKV + H0])
        wh = sb("wh", [P, KD, QKV + H0], F32R)
        wl = sb("wl", [P, KD, QKV + H0], F32R)
        gate = sb("gate", [P, 6, NT, H0])
        gstat = sb("gstat", [P, 6, NT])
        picked = sb("picked", [P, 2, H0, HD0])
        k_tok = sb("k_tok", [P, NT, HD0])
        v_pad = sb("v_pad", [P, NT, PAD])
        k_pad = sb("k_pad", [P, NT, 2, P])
        k_all = sb("k_all", [P, 2, TOK])
        q_all = sb("q_all", [P, KD, TOK])
        q_T = sb("q_T", [P, SLOTS, KD, SEQ])
        k_T = sb("k_T", [P, SLOTS, 2, SEQ])
        v_seq = sb("v_seq", [P, SLOTS, TPB, PAD])
        neg_max = sb("neg_max", [P, 4, 2])
        probs = sb("probs", [P, 4, CAUSAL])
        probsT = sb("probsT", [P, 8, CAUSAL])
        o_sb = sb("o_sb", [P, 2, 512])
        o_tok = sb("o_tok", [P, 2, H0, HD0])
        rsum = sb("rsum", [P, 2, H0])

        (loaded,) = c.sems(ctx, "g", "loaded")
        pool_sems = (padded,) = c.sems(ctx, "g", "padded")
        pe_sems = lg_ps, kv_ps, q_ps, kT_ps, s_ps, t_ps, pv_ps, o_turned = c.sems(
            ctx, "g", "lg_ps kv_ps q_ps kT_ps s_ps t_ps pv_ps o_turned")
        dve_sems = z_ready, picked_ps, k_ready, copied, nm_ready, pT_ready, rs_ready, o_scaled, chain = c.sems(
            ctx, "g", "z_ready picked_ps k_ready copied nm_ready pT_ready rs_ready o_scaled chain")
        act_sems = e_ready, q_ready, kT_ready, p_ready, o_ready = c.sems(ctx, "g", "e_ready q_ready kT_ready p_ready o_ready")
        block = ctx.enter_context(nc.Block())

        @block.sync
        def _(sp):
            sp.dma_start(w[:], c.dram["w_gated"]).then_inc(loaded, 16)

        @block.gpsimd
        def _(pool):
            give_lead(pool, pool_sems)
            pool.memset(k_pad[:], 0.0).then_inc(padded, 1)
            pool.memset(v_pad[:], 0.0).then_inc(padded, 1)
            pool.wait_ge(padded, LEAD + 2)
            pool.memset(v_pad[:, :, HD0:HD0 + 1], 1.0).then_inc(padded, 1)

        @block.vector
        def _(dve):
            give_lead(dve, dve_sems)
            link = Chain(dve, chain, LEAD)
            dve.wait_ge(loaded, 16)
            link(dve.tensor_copy(wh[:], w[:]))
            link(dve.tensor_tensor(wl[:], w[:], wh[:].bitcast(F32), ALU.subtract))
            z, e, cand, one_hot, top_hot, eq = (gate[:, n] for n in range(6))
            nmax, esum, emax, erec, top, first = (gstat[:, n] for n in range(6))

            def wide(a):
                return a.unsqueeze(2).broadcast_to((P, NT, H0))

            dve.wait_ge(lg_ps, LEAD + 1)
            logits = ps[:, 0, 0:NT * H0].rearrange("p (t h) -> p t h", t=NT)
            link(dve.tensor_reduce(nmax, logits, X, ALU.max, negate=True))
            dve.tensor_tensor(z, logits, wide(nmax), ALU.add).then_inc(z_ready, 1)
            dve.wait_ge(e_ready, LEAD + 1)
            dve.tensor_reduce(esum, e, X, ALU.add)
            link(dve.tensor_reduce(emax, e, X, ALU.max))
            link(dve.reciprocal(erec, esum))
            dve.tensor_tensor(top, emax, erec, ALU.mult)
            link(dve.tensor_tensor(eq, e, wide(emax), ALU.is_equal))
            link(dve.scalar_tensor_tensor(cand, eq, -16.0, c.iota.unsqueeze(1).broadcast_to((P, NT, H0)), ALU.mult, ALU.add))
            link(dve.tensor_reduce(first, cand, X, ALU.min))
            link(dve.tensor_tensor(one_hot, cand, wide(first), ALU.is_equal))
            link(dve.tensor_tensor(top_hot, one_hot, wide(top), ALU.mult))
            dve.wait_ge(padded, LEAD + 3)
            for t in range(NT):
                dve.wait_ge(kv_ps, LEAD + t + 1)
                kv = ps[:, 5 + t % 3, :].rearrange("p (a h d) -> p a h d", a=2, h=H0)
                dve.tensor_tensor(picked[:, 0], kv[:, 0], one_hot[:, t, :].unsqueeze(2).broadcast_to((P, H0, HD0)), ALU.mult)
                dve.tensor_tensor(picked[:, 1], kv[:, 1], top_hot[:, t, :].unsqueeze(2).broadcast_to((P, H0, HD0)), ALU.mult).then_inc(picked_ps, 1)
                dve.wait_ge(picked_ps, LEAD + t + 1)
                dve.tensor_reduce(v_pad[:, t, 0:HD0], picked[:, 1].rearrange("p h d -> p d h"), X, ALU.add)
                link(dve.tensor_reduce(k_tok[:, t, :], picked[:, 0].rearrange("p h d -> p d h"), X, ALU.add))
                for par in range(2):
                    dst = k_pad[:, t, par, :].rearrange("p (g r) -> p g r", g=4)[:, :, par * HD0:(par + 1) * HD0]
                    dve.tensor_copy(dst, k_tok[:, t, :].unsqueeze(1).broadcast_to((P, 4, HD0))).then_inc(k_ready, 1)
            dve.wait_ge(q_ready, LEAD + 4)
            dve.wait_ge(kT_ready, LEAD + 4)
            with dve.Fori(0, BATCH // SLOTS) as i:
                dve.wait_ge(pv_ps, LEAD + QUADS * i)
                for u in range(SLOTS):
                    s = SLOTS * i + u
                    dve.tensor_scalar(q_T[:, u], q_all[:, :, bass.ds(s * SEQ, SEQ)], 1.0, None, ALU.mult)
                    dve.tensor_scalar(k_T[:, u], k_all[:, :, bass.ds(s * SEQ, SEQ)], 1.0, None, ALU.mult)
                    dve.tensor_scalar(v_seq[:, u], v_pad[:, bass.ds(s * TPB, TPB), :], 1.0, None, ALU.mult).then_inc(copied, 1)
                for n in range(ITEMS + 8):
                    if n < ITEMS:
                        dve.wait_ge(s_ps, LEAD + ITEMS * i + n + 1)
                        dve.wait_ge(p_ready, LEAD + ITEMS * i + n - 3)
                        dve.tensor_reduce(neg_max[:, n % 4, 0:1], ps[:, n % 3, 0:P], X, ALU.max, negate=True)
                        dve.tensor_reduce(neg_max[:, n % 4, 1:2], ps[:, n % 3, P:CAUSAL], X, ALU.max, negate=True).then_inc(nm_ready, 1)
                    m = n - 3
                    if 0 <= m < ITEMS:
                        dve.wait_ge(t_ps, LEAD + ITEMS * i + m + 1)
                        dve.wait_ge(pv_ps, LEAD + QUADS * i + m // 4 - 1)
                        dve.tensor_copy(probsT[:, m % 8, :], ps[:, 3 + m % 2, 0:CAUSAL]).then_inc(pT_ready, 1)
                    for u in range(SLOTS):
                        for t, at in enumerate((21, 23)):
                            if n == H0 * u + at:
                                seq = TPB * (SLOTS * i + u) + t
                                turned = ps[:, 5, :].rearrange("p (h r) -> p h r", h=H0)
                                dve.wait_ge(o_turned, LEAD + seq + 1)
                                dve.reciprocal(rsum[:, t, :], turned[:, :, HD0]).then_inc(rs_ready, 1)
                                dve.wait_ge(rs_ready, LEAD + seq + 1)
                                dve.tensor_tensor(o_tok[:, t], turned[:, :, 0:HD0], rsum[:, t, :].unsqueeze(2).broadcast_to((P, H0, HD0)), ALU.mult).then_inc(o_scaled, 1)
                                dve.wait_ge(o_scaled, LEAD + seq + 1)
                                tile = bass.ds(seq, 1)
                                dve.tensor_tensor(c.y[:, tile, :], o_tok[:, t].rearrange("p h d -> p (h d)").unsqueeze(1), c.x[:, tile, :], ALU.add)

        @block.scalar
        def _(act):
            give_lead(act, act_sems)
            act.wait_ge(z_ready, LEAD + 1)
            act.activation(gate[:, 1], gate[:, 0], ACT.Exp).then_inc(e_ready, 1)
            for n in range(4):
                act.wait_ge(q_ps, LEAD + n + 1)
                act.activation(q_all[:, n // 2, n % 2 * 512:(n % 2 + 1) * 512], ps[:, 1 + n, :], ACT.Copy, scale=float(HD0) ** -0.5).then_inc(q_ready, 1)
            for n in range(4):
                half, par = n // 2, n % 2
                act.wait_ge(kT_ps, LEAD + n + 1)
                act.activation(k_all[:, par, half * 512:(half + 1) * 512], ps[:, 1 + n, :], ACT.Copy).then_inc(kT_ready, 1)
            with act.Fori(0, BATCH // SLOTS) as i:
                for n in range(ITEMS + 5):
                    if n < ITEMS:
                        act.wait_ge(nm_ready, LEAD + ITEMS * i + n + 1)
                        act.wait_ge(t_ps, LEAD + ITEMS * i + n - 3)
                        for b, cols in enumerate((slice(0, P), slice(P, CAUSAL))):
                            ex = act.activation(probs[:, n % 4, cols], ps[:, n % 3, cols], ACT.Exp, bias=neg_max[:, n % 4, b:b + 1])
                        ex.then_inc(p_ready, 1)
                    for u in range(SLOTS):
                        for half, at in enumerate((11, 19)):
                            if n == H0 * u + at:
                                act.wait_ge(pv_ps, LEAD + QUADS * i + 4 * u + 2 * half + 2)
                                act.wait_ge(o_turned, LEAD + TPB * (SLOTS * i + u))
                                act.activation(o_sb[:, half, :], ps[:, 6 + half, :], ACT.Copy).then_inc(o_ready, 1)

        @block.tensor
        def _(pe):
            give_lead(pe, pe_sems)
            pe.wait_ge(chain, LEAD + 2)
            for t in range(NT):
                tok = slice(t * P, (t + 1) * P)
                mm = split_product(pe, ps[:, 0, t * H0:(t + 1) * H0], lambda k: c.xTh[:, k, tok], lambda k: c.xTl[:, k, tok],
                                   lambda k: wh[:, k, QKV:], lambda k: wl[:, k, QKV:], range(KD))
            mm.then_inc(lg_ps, 1)
            for n in range(4):
                m, half = n // 2, slice(n % 2 * 512, (n % 2 + 1) * 512)
                split_product(pe, ps[:, 1 + n, :], lambda k: wh[:, k, m * P:(m + 1) * P], lambda k: wl[:, k, m * P:(m + 1) * P],
                              lambda k: c.xTh[:, k, half], lambda k: c.xTl[:, k, half], range(KD)).then_inc(q_ps, 1)
            for t in range(NT):
                tok = slice(t * P, (t + 1) * P)
                if t >= 3:
                    pe.wait_ge(picked_ps, LEAD + t - 2)
                split_product(pe, ps[:, 5 + t % 3, :], lambda k: c.xTh[:, k, tok], lambda k: c.xTl[:, k, tok],
                              lambda k: wh[:, k, D:QKV], lambda k: wl[:, k, D:QKV], range(KD)).then_inc(kv_ps, 1)
            for n in range(4):
                half, par = n // 2, n % 2
                pe.wait_ge(q_ready, LEAD + n + 1)
                pe.wait_ge(k_ready, LEAD + 8 * (half + 1))
                for t in range(4):
                    mm = pe.transpose(ps[:, 1 + n, t * P:(t + 1) * P], k_pad[:, 4 * half + t, par, :], c.ident)
                mm.then_inc(kT_ps, 1)
            pe.wait_ge(kT_ready, LEAD + 4)
            pe.wait_ge(picked_ps, LEAD + NT)
            with pe.Fori(0, BATCH // SLOTS) as i:
                def scores(n):
                    u, h = n // H0, n % H0
                    m, g, par = h // 8, 32 * (h % 8 // 2), h % 2
                    bank = ps[:, n % 3, :]
                    if h == 0:
                        pe.wait_ge(copied, LEAD + SLOTS * i + u + 1)
                    pe.wait_ge(p_ready, LEAD + ITEMS * i + (n - 2 if n >= 3 else 0))
                    pe.matmul(bank[:, 0:CAUSAL], c.ident16[:], c.neg16[:], start=True, stop=False)
                    pe.matmul(bank[:, 0:P], q_T[g:g + 32, u, m, 0:P], k_T[g:g + 32, u, par, 0:P], start=False, stop=False, tile_position=(g, 0))
                    pe.matmul(bank[:, P:CAUSAL], q_T[g:g + 32, u, m, P:SEQ], k_T[g:g + 32, u, par, :], start=False, stop=True,
                              tile_position=(g, 0)).then_inc(s_ps, 1)

                def turn(n):
                    pe.wait_ge(p_ready, LEAD + ITEMS * i + n + 1)
                    pe.wait_ge(pT_ready, LEAD + ITEMS * i + n - 1)
                    for b in range(3):
                        mm = pe.transpose(ps[:, 3 + n % 2, b * P:(b + 1) * P], probs[:, n % 4, b * P:(b + 1) * P], c.ident)
                    mm.then_inc(t_ps, 1)

                def values(quad):
                    u, j = quad // 4, quad % 4
                    pe.wait_ge(pT_ready, LEAD + ITEMS * i + 4 * quad + 4)
                    if j % 2 == 0:
                        pe.wait_ge(o_ready, LEAD + 2 * (SLOTS * i + u) + j // 2 - 1)
                    out = ps[:, 6 + j // 2, j % 2 * SEQ:(j % 2 + 1) * SEQ]
                    for q in range(4):
                        pe.matmul(out[PAD * q:PAD * (q + 1), :], v_seq[:, u, 0, :], probsT[:, (4 * quad + q) % 8, 0:SEQ], start=True, stop=False)
                    for q in range(4):
                        mm = pe.matmul(out[PAD * q:PAD * (q + 1), P:SEQ], v_seq[:, u, 1, :], probsT[:, (4 * quad + q) % 8, SEQ:CAUSAL],
                                       start=False, stop=True)
                    mm.then_inc(pv_ps, 1)

                def turn_outputs(u, t):
                    pe.wait_ge(o_ready, LEAD + 2 * (SLOTS * i + u) + 2)
                    pe.wait_ge(o_scaled, LEAD + TPB * (SLOTS * i + u) + t)
                    for j in range(4):
                        mm = pe.transpose(ps[:, 5, j * P:(j + 1) * P], o_sb[:, j // 2, j % 2 * SEQ + t * P:j % 2 * SEQ + (t + 1) * P], c.ident)
                    mm.then_inc(o_turned, 1)

                keep_warm(c, pe, ps[:, 2, :], 8)
                for n in range(ITEMS + 8):
                    if n < ITEMS:
                        scores(n)
                    if 2 <= n < ITEMS + 2:
                        turn(n - 2)
                    if n >= 6 and (n - 6) % 4 == 0 and (n - 6) // 4 < QUADS:
                        values((n - 6) // 4)
                    for u in range(SLOTS):
                        if n - H0 * u in (20, 22):
                            turn_outputs(u, (n - H0 * u - 20) // 2)


def layer1_decay_attention(c):
    nc, ps = c.nc, c.ps
    WC = 4 * P
    with ExitStack() as ctx:
        def sb(name, shape, dt=F32):
            return c.tile(ctx, "d_" + name, shape, dt)

        stage = sb("stage", [P, KD, WC])
        wh = sb("wh", [P, KD, 3 * P], F32R)
        wl = sb("wl", [P, KD, 3 * P], F32R)
        wv = sb("wv", [P, KD, P])
        decay = sb("decay", [P, 2, CAUSAL])
        wo = sb("wo", [P, PAIRS, D])
        norm_w = sb("norm_w", [P, PAIRS])
        q_T = sb("q_T", [P, TOK])
        k_T = sb("k_T", [P, TOK])
        v = sb("v", [P, NT, P])
        gate = sb("gate", [P, TOK])
        s_m = sb("s_m", [P, 4, CAUSAL])
        sq = sb("sq", [P, 2, SEQ])
        sq_sum = sb("sq_sum", [P, TOK])
        gated = sb("gated", [P, BATCH, SEQ])
        zeros = sb("zeros", [P, 512])
        ones = sb("ones", [P, 1])
        stat = sb("stat", [P, 3, NT])

        loaded, stage_in, decay_in = c.sems(ctx, "d", "loaded stage_in decay_in")
        pe_sems = proj_ps, s_ps, pv_ps, op_ps = c.sems(ctx, "d", "proj_ps s_ps pv_ps op_ps")
        dve_sems = sm_ready, og_ready = c.sems(ctx, "d", "sm_ready og_ready")
        act_sems = evac, sq_ready = c.sems(ctx, "d", "evac sq_ready")
        pool_sems = w_hi, w_split, sq_added = c.sems(ctx, "d", "w_hi w_split sq_added")
        zeroed, wo_scaled, ss_ps, var_ready, sd_ready, rs_ready = c.sems(ctx, "d", "zeroed wo_scaled ss_ps var_ready sd_ready rs_ready")
        block = ctx.enter_context(nc.Block())

        @block.sync
        def _(sp):
            sp.dma_start(stage[:], c.dram["w_decay"][0]).then_inc(stage_in, 16)
            sp.dma_start(wo[:], c.dram["wo_decay"]).then_inc(loaded, 16)
            sp.dma_start(norm_w[:], c.dram["norm_decay"]).then_inc(loaded, 16)
            with sp.Fori(0, PAIRS) as i:
                sp.wait_ge(sm_ready, LEAD + 8 * i)
                sp.dma_start(decay[:], c.dram["decay"][bass.ds(i, 1)].rearrange("a p h s -> p (a h) s")).then_inc(decay_in, 16)
                sp.wait_ge(w_split, LEAD + i + 1)
                sp.dma_start(stage[:], c.dram["w_decay"][bass.ds(i + 1, 1)].rearrange("a p k n -> p (a k) n")).then_inc(stage_in, 16)

        @block.gpsimd
        def _(pool):
            give_lead(pool, pool_sems)
            pool.memset(zeros[:], 0.0).then_inc(zeroed, 1)
            pool.memset(ones[:], 1.0).then_inc(zeroed, 1)
            pool.memset(sq_sum[:], 0.0).then_inc(zeroed, 1)
            pool.wait_ge(zeroed, 3)

            def split(i, staged):
                nought = zeros[:, 0:1].unsqueeze(1)
                pool.wait_ge(stage_in, staged)
                pool.tensor_tensor(wh[:], stage[:, :, 0:3 * P], nought.broadcast_to((P, KD, 3 * P)), ALU.add).then_inc(w_hi, 1)
                pool.tensor_tensor(wv[:], stage[:, :, 3 * P:], nought.broadcast_to((P, KD, P)), ALU.add)
                pool.wait_ge(w_hi, LEAD + i + 1)
                pool.tensor_tensor(wl[:], stage[:, :, 0:3 * P], wh[:].bitcast(F32), ALU.subtract).then_inc(w_split, 1)

            split(0, 16)
            pool.wait_ge(loaded, 32)
            pool.tensor_tensor(wo[:], wo[:], norm_w[:].unsqueeze(2).broadcast_to((P, PAIRS, D)), ALU.mult).then_inc(wo_scaled, 1)
            with pool.Fori(0, PAIRS) as i:
                pool.wait_ge(proj_ps, LEAD + 8 * i + 8)
                split(i + 1, 16 * i + 32)
                for b in range(BATCH):
                    pool.wait_ge(sq_ready, LEAD + BATCH * i + b + 1)
                    pool.wait_ge(sq_added, LEAD + BATCH * i + b - 3)
                    cols = slice(b * SEQ, (b + 1) * SEQ)
                    pool.tensor_tensor(sq_sum[:, cols], sq_sum[:, cols], sq[:, b % 2, :], ALU.add).then_inc(sq_added, 1)

        @block.vector
        def _(dve):
            give_lead(dve, dve_sems)

            with dve.Fori(0, PAIRS) as i:
                def gate_out(b):
                    dve.wait_ge(pv_ps, LEAD + BATCH * i + b + 1)
                    dve.wait_ge(op_ps, LEAD + BATCH * i + b - 3)
                    if b == 0:
                        dve.wait_ge(evac, LEAD + 8 * i + 8)
                    dve.scalar_tensor_tensor(gated[:, b, :], gate[:, b * SEQ:(b + 1) * SEQ], 1.0, ps[:, 6 + b % 2, 0:SEQ],
                                             ALU.add, ALU.mult).then_inc(og_ready, 1)

                dve.wait_ge(decay_in, 16 * i + 16)
                for s in range(8):
                    dve.wait_ge(s_ps, LEAD + 8 * i + s + 1)
                    dve.wait_ge(pv_ps, LEAD + BATCH * i + s // 2 - 1)
                    dve.tensor_tensor(s_m[:, s % 4, :], ps[:, 4 + s % 2, 0:CAUSAL], decay[:, s % 2, :], ALU.mult).then_inc(sm_ready, 1)
                    if s in (3, 5, 7):
                        gate_out((s - 3) // 2)
                gate_out(3)
            dve.wait_ge(ss_ps, 1)
            dve.tensor_scalar(stat[:, 0, :], ps[:, 4, 0:NT], 1.0 / (H1 * HD1), EPS, ALU.mult, ALU.add).then_inc(var_ready, 1)
            dve.wait_ge(sd_ready, 1)
            dve.reciprocal(stat[:, 2, :], stat[:, 1, :]).then_inc(rs_ready, 1)
            dve.wait_ge(rs_ready, 1)
            dve.tensor_scalar(stat[:, 0, :], stat[:, 2, :], 0.5, None, ALU.mult).then_inc(rs_ready, 1)
            dve.wait_ge(rs_ready, 2)
            for t in range(NT):
                dve.scalar_tensor_tensor(c.y[:, t, :], ps[:, t // 2, t % 2 * D:(t % 2 + 1) * D], stat[:, 0, t:t + 1], c.x[:, t, :], ALU.mult, ALU.add)

        @block.scalar
        def _(act):
            give_lead(act, act_sems)
            with act.Fori(0, PAIRS) as i:
                for n in range(8):
                    act.wait_ge(proj_ps, LEAD + 8 * i + n + 1)
                    half = slice(n % 2 * 512, (n % 2 + 1) * 512)
                    bank = ps[:, 4 + n % 2, :]
                    if n < 4:
                        act.activation((q_T, k_T)[n // 2][:, half], bank, ACT.Silu).then_inc(evac, 1)
                    elif n >= 6:
                        act.activation(v[:, n % 2 * 4:(n % 2 + 1) * 4, :].rearrange("p t d -> p (t d)"), bank, ACT.Silu).then_inc(evac, 1)
                    else:
                        if n == 4:
                            act.wait_ge(og_ready, LEAD + BATCH * i)
                        act.activation(gate[:, half], bank, ACT.Tanh, scale=0.5).then_inc(evac, 1)
                for b in range(BATCH):
                    act.wait_ge(og_ready, LEAD + BATCH * i + b + 1)
                    act.wait_ge(sq_added, LEAD + BATCH * i + b - 1)
                    act.activation(sq[:, b % 2, :], ps[:, 6 + b % 2, 0:SEQ], ACT.Square).then_inc(sq_ready, 1)
            act.wait_ge(var_ready, 1)
            act.activation(stat[:, 1, :], stat[:, 0, :], ACT.Sqrt).then_inc(sd_ready, 1)

        @block.tensor
        def _(pe):
            give_lead(pe, pe_sems)
            pe.wait_ge(zeroed, 3)
            pe.wait_ge(wo_scaled, 1)
            for bank in range(4):
                pe.matmul(ps[:, bank, :], zeros[:, 0:P], zeros[:], start=True, stop=False, skip_group_check=True)
            with pe.Fori(0, PAIRS) as i:
                pe.wait_ge(w_split, LEAD + i + 1)
                for n in range(8):
                    bank = ps[:, 4 + n % 2, :]
                    if n < 2:
                        pe.wait_ge(sm_ready, LEAD + 8 * i + n - 1)
                    else:
                        pe.wait_ge(evac, LEAD + 8 * i + n - 1)
                    half = slice(n % 2 * 512, (n % 2 + 1) * 512)
                    if n // 2 == 3:
                        for t in range(4):
                            tok = slice((n % 2 * 4 + t) * P, (n % 2 * 4 + t + 1) * P)
                            for k in range(KD):
                                mm = pe.matmul(bank[:, t * P:(t + 1) * P], c.xT[:, k, tok], wv[:, k, :], start=(k == 0), stop=(k == KD - 1))
                    else:
                        cols = slice(n // 2 * P, (n // 2 + 1) * P)
                        mm = split_product(pe, bank, lambda k: wh[:, k, cols], lambda k: wl[:, k, cols],
                                           lambda k: c.xTh[:, k, half], lambda k: c.xTl[:, k, half], range(KD))
                    mm.then_inc(proj_ps, 1)

                def scores(s):
                    b, r = s // 2, s % 2 * HD1
                    if s == 0:
                        pe.wait_ge(evac, LEAD + 8 * i + 7)
                    elif s == 1:
                        pe.wait_ge(evac, LEAD + 8 * i + 8)
                    else:
                        pe.wait_ge(sm_ready, LEAD + 8 * i + s - 1)
                    bank = ps[:, 4 + s % 2, :]
                    rows = slice(r, r + HD1)
                    pe.matmul(bank[:, 0:SEQ], k_T[rows, b * SEQ:b * SEQ + P], q_T[rows, b * SEQ:(b + 1) * SEQ], start=True, stop=True)
                    pe.matmul(bank[:, SEQ:CAUSAL], k_T[rows, b * SEQ + P:(b + 1) * SEQ], q_T[rows, b * SEQ + P:(b + 1) * SEQ],
                              start=True, stop=True).then_inc(s_ps, 1)

                def values(b):
                    pe.wait_ge(sm_ready, LEAD + 8 * i + 2 * b + 2)
                    pe.wait_ge(sq_ready, LEAD + BATCH * i + b - 1)
                    outs = [ps[r:r + HD1, 6 + b % 2, 0:SEQ] for r in (0, HD1)]
                    for n, out in enumerate(outs):
                        pe.matmul(out, v[:, TPB * b, n * HD1:(n + 1) * HD1], s_m[:, (2 * b + n) % 4, 0:SEQ], start=True, stop=False)
                    for n, out in enumerate(outs):
                        mm = pe.matmul(out[:, P:SEQ], v[:, TPB * b + 1, n * HD1:(n + 1) * HD1], s_m[:, (2 * b + n) % 4, SEQ:CAUSAL],
                                       start=False, stop=True)
                    mm.then_inc(pv_ps, 1)

                def project(b):
                    pe.wait_ge(og_ready, LEAD + BATCH * i + b + 1)
                    for t in range(TPB):
                        mm = pe.matmul(ps[:, b, t * D:(t + 1) * D], gated[:, b, t * P:(t + 1) * P], wo[:, bass.ds(i, 1), :].rearrange("p a d -> p (a d)"),
                                       start=False, stop=False, skip_group_check=True)
                    mm.then_inc(op_ps, 1)

                for step in range(BATCH + 2):
                    if step < BATCH:
                        scores(2 * step)
                        scores(2 * step + 1)
                    if 1 <= step <= BATCH:
                        values(step - 1)
                    if step >= 2:
                        project(step - 2)
            pe.wait_ge(sq_added, LEAD + BATCH * PAIRS)
            for t in range(NT):
                mm = pe.matmul(ps[:, 4, t:t + 1], sq_sum[:, t * P:(t + 1) * P], ones[:], start=True, stop=True)
            mm.then_inc(ss_ps, 1)


def layer1_grouped_attention(c):
    nc, ps = c.nc, c.ps
    PIECES = 2 + GROUP
    with ExitStack() as ctx:
        def sb(name, shape, dt=F32):
            return c.tile(ctx, "e_" + name, shape, dt)

        stage = sb("stage", [P, PIECES, KD, P])
        wh = sb("wh", [P, PIECES, KD, P], F32R)
        wl = sb("wl", [P, PIECES, KD, P], F32R)
        wo = sb("wo", [P, HQ, D])
        rope = sb("rope", [P, 4, 512])
        k_T = sb("k_T", [P, TOK])
        v = sb("v", [P, NT, P])
        q_T = sb("q_T", [P, 2, TOK])
        by_cos = sb("by_cos", [P, 2, 512])
        by_sin = sb("by_sin", [P, 2, 512])
        neg_max = sb("neg_max", [P, 4, 2])
        sums = sb("sums", [P, 4, 2])
        rsum = sb("rsum", [P, 4, 2])
        probs = sb("probs", [P, 4, CAUSAL])
        probsT = sb("probsT", [P, 2, CAUSAL])
        o_T = sb("o_T", [P, 2, SEQ])
        zeros = sb("zeros", [P, 512])

        loaded, stage_in, zeroed = c.sems(ctx, "e", "loaded stage_in zeroed")
        pe_sems = proj_ps, s_ps, t_ps, pv_ps, wo_ps = c.sems(ctx, "e", "proj_ps s_ps t_ps pv_ps wo_ps")
        dve_sems = w_hi, w_split, turned_ps, nm_ready, rs_ready, pT_ready = c.sems(ctx, "e", "w_hi w_split turned_ps nm_ready rs_ready pT_ready")
        act_sems = v_ready, p_ready, oT_ready = c.sems(ctx, "e", "v_ready p_ready oT_ready")
        pool_sems = roped, pn_ready = c.sems(ctx, "e", "roped pn_ready")
        block = ctx.enter_context(nc.Block())
        ITEMS = GROUP * BATCH

        ring = [("k", 0), ("k", 1), ("v", 0), ("v", 1), ("q", 0), ("q", 1)]
        for t in range(ITEMS):
            ring.append(("s", t))
            if t % 4 in (1, 2) and t // 4 + 1 < GROUP:
                ring.append(("q", 2 * (t // 4 + 1) + t % 4 - 1))
        at = {key: n for n, key in enumerate(ring)}
        PROJ, ROPED = 4 + 2 * GROUP, 2 + 2 * GROUP
        proj_order = [r for r in ring if r[0] != "s"]
        roped_order = [r for r in proj_order if r[0] != "v"]

        def freed(eng, g, key):
            n = at[key] - 2
            last, before = ring[n % len(ring)], n < 0
            if last[0] == "s":
                eng.wait_ge(p_ready, LEAD + 2 * (ITEMS * g - (ITEMS if before else 0) + last[1] + 1))
            elif last[0] == "v":
                eng.wait_ge(v_ready, LEAD + 2 * g + last[1] + 1)
            else:
                eng.wait_ge(turned_ps, LEAD + ROPED * g + roped_order.index(last) + 1)

        @block.sync
        def _(sp):
            sp.dma_start(stage[:], c.dram["w_grouped"][0]).then_inc(stage_in, 16)
            sp.dma_start(rope[:], c.dram["rope"]).then_inc(loaded, 16)
            sp.dma_start(wo[:], c.dram["wo_grouped"]).then_inc(loaded, 16)
            with sp.Fori(0, HKV) as g:
                sp.wait_ge(w_split, LEAD + g + 1)
                sp.dma_start(stage[:].rearrange("p a k n -> p (a k) n"),
                             c.dram["w_grouped"][bass.ds(g + 1, 1)].rearrange("b p a k n -> p (b a k) n")).then_inc(stage_in, 16)

        @block.gpsimd
        def _(pool):
            give_lead(pool, pool_sems)
            pool.memset(zeros[:], 0.0).then_inc(zeroed, 1)
            with pool.Fori(0, HKV) as g:
                def rotate(key):
                    n = roped_order.index(key)
                    pool.wait_ge(turned_ps, LEAD + ROPED * g + n + 1)
                    half = slice(key[1] % 2 * 512, (key[1] % 2 + 1) * 512)
                    dst = k_T[:, half] if key[0] == "k" else q_T[:, key[1] // 2 % 2, half]
                    pool.tensor_tensor(dst, by_cos[:, n % 2, :], by_sin[:, n % 2, :], ALU.add).then_inc(roped, 1)

                for key in roped_order[:4]:
                    rotate(key)
                for t in range(ITEMS + 1):
                    if ("q", 2 * (t // 4 + 1) + t % 4 - 1) in at and t % 4 in (1, 2):
                        rotate(("q", 2 * (t // 4 + 1) + t % 4 - 1))
                    if t >= 1:
                        u = t - 1
                        pool.wait_ge(rs_ready, LEAD + ITEMS * g + u + 1)
                        pool.tensor_tensor(probs[:, u % 4, 0:P], probs[:, u % 4, 0:P], rsum[:, u % 4, 0:1].broadcast_to((P, P)), ALU.mult).then_inc(pn_ready, 1)
                        pool.tensor_tensor(probs[:, u % 4, P:CAUSAL], probs[:, u % 4, P:CAUSAL], rsum[:, u % 4, 1:2].broadcast_to((P, SEQ)), ALU.mult).then_inc(pn_ready, 1)

        @block.vector
        def _(dve):
            give_lead(dve, dve_sems)

            def split(g, staged):
                dve.wait_ge(stage_in, staged)
                dve.tensor_copy(wh[:], stage[:]).then_inc(w_hi, 1)
                dve.wait_ge(w_hi, LEAD + g + 1)
                dve.tensor_tensor(wl[:], stage[:], wh[:].bitcast(F32), ALU.subtract).then_inc(w_split, 1)

            split(0, 16)
            dve.wait_ge(loaded, 32)
            with dve.Fori(0, HKV) as g:
                def rotate(key):
                    n = roped_order.index(key)
                    dve.wait_ge(proj_ps, LEAD + PROJ * g + proj_order.index(key) + 1)
                    dve.wait_ge(roped, LEAD + ROPED * g + n - 1)
                    bank = ps[:, 4 + at[key] % 2, :]
                    cos, sin = (rope[:, 0], rope[:, 1]) if key[0] == "k" else (rope[:, 2], rope[:, 3])
                    dve.tensor_tensor(by_cos[:, n % 2, :], bank, cos, ALU.mult)
                    dve.tensor_tensor(by_sin[0:HDQ // 2, n % 2, :], bank[HDQ // 2:P], sin[HDQ // 2:P], ALU.mult)
                    dve.tensor_tensor(by_sin[HDQ // 2:P, n % 2, :], bank[0:HDQ // 2], sin[0:HDQ // 2], ALU.mult).then_inc(turned_ps, 1)

                for key in roped_order[:4]:
                    rotate(key)
                for t in range(ITEMS + 2):
                    if t < ITEMS:
                        dve.wait_ge(s_ps, LEAD + ITEMS * g + t + 1)
                        dve.wait_ge(p_ready, LEAD + 2 * (ITEMS * g + t) - 6)
                        bank = ps[:, 4 + at["s", t] % 2, :]
                        dve.tensor_reduce(neg_max[:, t % 4, 0:1], bank[:, 0:P], X, ALU.max, negate=True).then_inc(nm_ready, 1)
                        dve.tensor_reduce(neg_max[:, t % 4, 1:2], bank[:, P:CAUSAL], X, ALU.max, negate=True).then_inc(nm_ready, 1)
                    if t % 4 in (1, 2) and ("q", 2 * (t // 4 + 1) + t % 4 - 1) in at:
                        rotate(("q", 2 * (t // 4 + 1) + t % 4 - 1))
                    if 1 <= t <= ITEMS:
                        u = t - 1
                        dve.wait_ge(p_ready, LEAD + 2 * (ITEMS * g + u) + 2)
                        dve.wait_ge(pn_ready, LEAD + 2 * (ITEMS * g + u) - 6)
                        dve.reciprocal(rsum[:, u % 4, :], sums[:, u % 4, :]).then_inc(rs_ready, 1)
                    if t >= 2:
                        u = t - 2
                        dve.wait_ge(t_ps, LEAD + ITEMS * g + u + 1)
                        dve.wait_ge(pv_ps, LEAD + ITEMS * g + u - 1)
                        dve.tensor_copy(probsT[:, u % 2, :], ps[:, 6, 0:CAUSAL]).then_inc(pT_ready, 1)
                    if t == ITEMS - 1:
                        split(g + 1, 16 * g + 32)
            dve.wait_ge(wo_ps, LEAD + HKV * ITEMS)
            for bank in range(4):
                dve.tensor_tensor(c.y[:, 2 * bank:2 * bank + 2, :], ps[:, bank, :].rearrange("p (t d) -> p t d", t=2),
                                  c.x[:, 2 * bank:2 * bank + 2, :], ALU.add)

        @block.scalar
        def _(act):
            give_lead(act, act_sems)
            with act.Fori(0, HKV) as g:
                for n in range(2):
                    act.wait_ge(proj_ps, LEAD + PROJ * g + 3 + n)
                    act.activation(v[:, 4 * n:4 * n + 4, :].rearrange("p t d -> p (t d)"), ps[:, 4 + at["v", n] % 2, :], ACT.Copy).then_inc(v_ready, 1)
                for t in range(ITEMS + 3):
                    if t < ITEMS:
                        act.wait_ge(nm_ready, LEAD + 2 * (ITEMS * g + t) + 2)
                        act.wait_ge(t_ps, LEAD + ITEMS * g + t - 3)
                        bank = ps[:, 4 + at["s", t] % 2, :]
                        for b, cols in enumerate((slice(0, P), slice(P, CAUSAL))):
                            act.activation(probs[:, t % 4, cols], bank[:, cols], ACT.Exp, bias=neg_max[:, t % 4, b:b + 1],
                                           accum_out=sums[:, t % 4, b:b + 1]).then_inc(p_ready, 1)
                    if t >= 3:
                        u = t - 3
                        act.wait_ge(pv_ps, LEAD + ITEMS * g + u + 1)
                        act.wait_ge(wo_ps, LEAD + ITEMS * g + u - 1)
                        act.activation(o_T[:, u % 2, :], ps[:, 7, 0:SEQ], ACT.Copy).then_inc(oT_ready, 1)

        @block.tensor
        def _(pe):
            give_lead(pe, pe_sems)
            pe.wait_ge(zeroed, 1)
            for bank in range(4):
                pe.matmul(ps[:, bank, :], zeros[:, 0:P], zeros[:], start=True, stop=False, skip_group_check=True)
            pe.wait_ge(loaded, 32)
            with pe.Fori(0, HKV) as g:
                def project(key):
                    what, n = key
                    half = slice(n % 2 * 512, (n % 2 + 1) * 512)
                    bank = ps[:, 4 + at[key] % 2, :]
                    if key == ring[0]:
                        pe.wait_ge(w_split, LEAD + g + 1)
                    freed(pe, g, key)
                    if what == "v":
                        for t in range(4):
                            tok = slice((4 * n + t) * P, (4 * n + t + 1) * P)
                            mm = split_product(pe, bank[:, t * P:(t + 1) * P], lambda k: c.xTh[:, k, tok], lambda k: c.xTl[:, k, tok],
                                               lambda k: wh[:, 1, k, :], lambda k: wl[:, 1, k, :], range(KD))
                    else:
                        piece = 0 if what == "k" else 2 + n // 2
                        mm = split_product(pe, bank, lambda k: wh[:, piece, k, :], lambda k: wl[:, piece, k, :],
                                           lambda k: c.xTh[:, k, half], lambda k: c.xTl[:, k, half], range(KD))
                    mm.then_inc(proj_ps, 1)

                for key in ring[:6]:
                    project(key)
                for t in range(ITEMS + 4):
                    if t < ITEMS:
                        b = t % 4
                        if b == 0:
                            pe.wait_ge(roped, LEAD + ROPED * g + roped_order.index(("q", 2 * (t // 4) + 1)) + 1)
                        freed(pe, g, ("s", t))
                        bank, q = ps[:, 4 + at["s", t] % 2, :], q_T[:, t // 4 % 2, b * SEQ:(b + 1) * SEQ]
                        keys = k_T[:, b * SEQ:(b + 1) * SEQ]
                        pe.matmul(bank[:, 0:CAUSAL], c.ident16[:], c.neg16[:], start=True, stop=False)
                        pe.matmul(bank[:, 0:P], q[:, 0:P], keys[:, 0:P], start=False, stop=False)
                        pe.matmul(bank[:, P:CAUSAL], q[:, P:SEQ], keys, start=False, stop=True).then_inc(s_ps, 1)
                    nxt = ("q", 2 * (t // 4 + 1) + t % 4 - 1)
                    if t % 4 in (1, 2) and nxt in at:
                        project(nxt)
                    if t >= 4:
                        u = t - 4
                        pe.wait_ge(oT_ready, LEAD + ITEMS * g + u + 1)
                        for h in range(TPB):
                            mm = pe.matmul(ps[:, u % 4, h * D:(h + 1) * D], o_T[:, u % 2, h * P:(h + 1) * P],
                                           wo[:, bass.ds(g * GROUP + u // 4, 1), :].rearrange("p a d -> p (a d)"),
                                           start=False, stop=False, skip_group_check=True)
                        mm.then_inc(wo_ps, 1)
                    if 2 <= t < ITEMS + 2:
                        u = t - 2
                        pe.wait_ge(pn_ready, LEAD + 2 * (ITEMS * g + u) + 2)
                        pe.wait_ge(pT_ready, LEAD + ITEMS * g + u)
                        for n in range(3):
                            mm = pe.transpose(ps[:, 6, n * P:(n + 1) * P], probs[:, u % 4, n * P:(n + 1) * P], c.ident)
                        mm.then_inc(t_ps, 1)
                    if 3 <= t < ITEMS + 3:
                        u, b = t - 3, (t - 3) % 4
                        if u == 0:
                            pe.wait_ge(v_ready, LEAD + 2 * g + 2)
                        pe.wait_ge(pT_ready, LEAD + ITEMS * g + u + 1)
                        pe.wait_ge(oT_ready, LEAD + ITEMS * g + u)
                        out, s = ps[:, 7, 0:SEQ], probsT[:, u % 2, :]
                        pe.matmul(out, v[:, TPB * b, :], s[:, 0:SEQ], start=True, stop=False)
                        pe.matmul(out[:, P:SEQ], v[:, TPB * b + 1, :], s[:, SEQ:CAUSAL], start=False, stop=True).then_inc(pv_ps, 1)


def layer1_experts(c):
    nc, ps = c.nc, c.ps
    W1, W3, W2, WC = 0, KD * FF, 2 * KD * FF, 3 * KD * FF
    FT = FF // P
    with ExitStack() as ctx:
        def sb(name, shape, dt=F32):
            return c.tile(ctx, "f_" + name, shape, dt)

        stage = sb("stage", [P, WC])
        wh = [sb(f"wh{n}", [P, WC], F32R) for n in range(2)]
        wl = [sb(f"wl{n}", [P, WC], F32R) for n in range(2)]
        wg = sb("wg", [P, KD, EXPERTS])
        wgh = sb("wgh", [P, KD, EXPERTS], F32R)
        wgl = sb("wgl", [P, KD, EXPERTS], F32R)
        lg = sb("lg", [P, 8, NT, EXPERTS])
        gs = sb("gs", [P, 8, NT])
        weight = sb("weight", [P, EXPERTS, NT])
        act1 = sb("act1", [P, 2, 512])
        hid = sb("hid", [P, 2, 512])
        hidh = sb("hidh", [P, 2, FT, 512], F32R)
        hidl = sb("hidl", [P, 2, FT, 512], F32R)

        loaded, stage_in = c.sems(ctx, "f", "loaded stage_in")
        pe_sems = lg_ps, a_ps, b_ps, o_ps = c.sems(ctx, "f", "lg_ps a_ps b_ps o_ps")
        dve_sems = w_split, g_split, chain, d_ready, w_ready, h_ready, lo_ready, acc = c.sems(ctx, "f", "w_split g_split chain d_ready w_ready h_ready lo_ready acc")
        act_sems = w_hi, ex_ready, silu_ready, hi_ready = c.sems(ctx, "f", "w_hi ex_ready silu_ready hi_ready")
        block = ctx.enter_context(nc.Block())
        STEPS = 2 * 2 * FT

        @block.sync
        def _(sp):
            sp.dma_start(wg[:], c.dram["w_router"]).then_inc(loaded, 16)
            sp.dma_start(stage[:], c.dram["w_experts"][0]).then_inc(stage_in, 16)
            with sp.Fori(0, EXPERTS) as e:
                sp.wait_ge(w_split, LEAD + e + 1)
                sp.dma_start(stage[:], c.dram["w_experts"][bass.ds(e + 1, 1)].rearrange("a p n -> p (a n)")).then_inc(stage_in, 16)

        @block.vector
        def _(dve):
            give_lead(dve, dve_sems)
            dve.wait_ge(loaded, 16)
            link = Chain(dve, chain, LEAD)
            link(dve.tensor_copy(wgh[:], wg[:]))
            dve.tensor_tensor(wgl[:], wg[:], wgh[:].bitcast(F32), ALU.subtract).then_inc(g_split, 1)

            def split(slot, e):
                dve.wait_ge(w_hi, LEAD + e + 1)
                dve.tensor_tensor(wl[slot][:], stage[:], wh[slot][:].bitcast(F32), ALU.subtract).then_inc(w_split, 1)

            split(0, 0)
            logits, eq, cand, hot1, rest, hot2, w_1, w_2 = (lg[:, n] for n in range(8))
            m1, m2, first, diff, ex, den, p1, p2 = (gs[:, n] for n in range(8))

            def wide(a):
                return a.unsqueeze(2).broadcast_to((P, NT, EXPERTS))

            iota = c.iota[:, 0:EXPERTS].unsqueeze(1).broadcast_to((P, NT, EXPERTS))
            dve.wait_ge(lg_ps, LEAD + 1)
            link(dve.tensor_copy(logits.rearrange("p t e -> p (t e)"), ps[:, 0, 0:NT * EXPERTS]))

            def best(values, largest, hot):
                link(dve.tensor_reduce(largest, values, X, ALU.max))
                link(dve.tensor_tensor(eq, values, wide(largest), ALU.is_equal))
                link(dve.scalar_tensor_tensor(cand, eq, -16.0, iota, ALU.mult, ALU.add))
                link(dve.tensor_reduce(first, cand, X, ALU.min))
                link(dve.tensor_tensor(hot, cand, wide(first), ALU.is_equal))

            best(logits, m1, hot1)
            link(dve.scalar_tensor_tensor(rest, hot1, -1e30, logits, ALU.mult, ALU.add))
            best(rest, m2, hot2)
            dve.tensor_tensor(diff, m2, m1, ALU.subtract).then_inc(d_ready, 1)
            dve.wait_ge(ex_ready, LEAD + 1)
            link(dve.tensor_scalar(den, ex, 1.0, None, ALU.add))
            link(dve.reciprocal(p1, den))
            link(dve.tensor_tensor(p2, p1, ex, ALU.mult))
            link(dve.tensor_tensor(w_1, hot1, wide(p1), ALU.mult))
            link(dve.tensor_tensor(w_2, hot2, wide(p2), ALU.mult))
            dve.tensor_tensor(weight[:].rearrange("p e t -> p t e"), w_1, w_2, ALU.add).then_inc(w_ready, 1)
            for t in range(NT):
                dve.tensor_tensor(c.y[:, t, :], c.y[:, t, :], c.x[:, t, :], ALU.add).then_inc(acc, 1)
            dve.wait_ge(w_ready, LEAD + 1)
            with dve.Fori(0, EXPERTS // 2) as i:
                def down(s):
                    for t in range(4):
                        n = 4 * s + t
                        tok = s % 2 * 4 + t
                        dve.wait_ge(o_ps, LEAD + 16 * i + n + 1)
                        dve.wait_ge(acc, LEAD + NT + 16 * i + n - 7)
                        dve.scalar_tensor_tensor(c.y[:, tok, :], ps[:, 6 + n % 2, 0:D], weight[:, bass.ds(2 * i + s // 2, 1), tok:tok + 1].rearrange("p a b -> p (a b)"),
                                                 c.y[:, tok, :], ALU.mult, ALU.add).then_inc(acc, 1)

                for n in range(STEPS):
                    s, f = n // FT, n % FT
                    dve.wait_ge(b_ps, LEAD + STEPS * i + n + 1)
                    dve.wait_ge(silu_ready, LEAD + STEPS * i + n + 1)
                    dve.wait_ge(hi_ready, LEAD + STEPS * i + n - 1)
                    dve.tensor_tensor(hid[:, n % 2, :], act1[:, n % 2, :], ps[:, 4 + n % 2, :], ALU.mult).then_inc(h_ready, 1)
                    dve.wait_ge(hi_ready, LEAD + STEPS * i + n + 1)
                    dve.tensor_tensor(hidl[:, s % 2, f, :], hid[:, n % 2, :], hidh[:, s % 2, f, :].bitcast(F32), ALU.subtract).then_inc(lo_ready, 1)
                    if s >= 1 and f == FT - 1:
                        down(s - 1)
                    if n == 1:
                        split(1, 2 * i + 1)
                    if n == 2 * FT + FT:
                        split(0, 2 * i + 2)
                down(3)

        @block.scalar
        def _(act):
            give_lead(act, act_sems)

            def high(slot, staged):
                act.wait_ge(stage_in, staged)
                act.activation(wh[slot][:], stage[:], ACT.Copy).then_inc(w_hi, 1)

            high(0, 16)
            act.wait_ge(d_ready, LEAD + 1)
            act.activation(gs[:, 4], gs[:, 3], ACT.Exp).then_inc(ex_ready, 1)
            with act.Fori(0, EXPERTS // 2) as i:
                for n in range(STEPS):
                    s, f = n // FT, n % FT
                    if n == 1:
                        act.wait_ge(o_ps, LEAD + 16 * i)
                        high(1, 32 * i + 32)
                    if n == 2 * FT + FT:
                        act.wait_ge(o_ps, LEAD + 16 * i + 8)
                        high(0, 32 * i + 48)
                    act.wait_ge(a_ps, LEAD + STEPS * i + n + 1)
                    act.wait_ge(h_ready, LEAD + STEPS * i + n - 1)
                    act.activation(act1[:, n % 2, :], ps[:, 2 + n % 2, :], ACT.Silu).then_inc(silu_ready, 1)
                    act.wait_ge(h_ready, LEAD + STEPS * i + n + 1)
                    act.wait_ge(o_ps, LEAD + 16 * i + 4 * s - 4)
                    act.activation(hidh[:, s % 2, f, :], hid[:, n % 2, :], ACT.Copy).then_inc(hi_ready, 1)

        @block.tensor
        def _(pe):
            give_lead(pe, pe_sems)
            pe.wait_ge(g_split, LEAD + 1)
            for t in range(NT):
                tok = slice(t * P, (t + 1) * P)
                mm = split_product(pe, ps[:, 0, t * EXPERTS:(t + 1) * EXPERTS], lambda k: c.xTh[:, k, tok], lambda k: c.xTl[:, k, tok],
                                   lambda k: wgh[:, k, :], lambda k: wgl[:, k, :], range(KD))
            mm.then_inc(lg_ps, 1)
            with pe.Fori(0, EXPERTS // 2) as i:
                def up(s):
                    e, half = s // 2, slice(s % 2 * 512, (s % 2 + 1) * 512)
                    if s % 2 == 0:
                        pe.wait_ge(w_split, LEAD + 2 * i + e + 1)
                    for f in range(FT):
                        n = FT * s + f
                        for base, bank, used, done in ((W1, 2, silu_ready, a_ps), (W3, 4, h_ready, b_ps)):
                            pe.wait_ge(used, LEAD + STEPS * i + n - 1)
                            at = [slice(base + k * FF + f * P, base + k * FF + (f + 1) * P) for k in range(KD)]
                            split_product(pe, ps[:, bank + n % 2, :], lambda k: wh[e][:, at[k]], lambda k: wl[e][:, at[k]],
                                          lambda k: c.xTh[:, k, half], lambda k: c.xTl[:, k, half], range(KD)).then_inc(done, 1)

                def down(s):
                    e = s // 2
                    pe.wait_ge(lo_ready, LEAD + STEPS * i + FT * (s + 1))
                    for t in range(4):
                        n = 4 * s + t
                        pe.wait_ge(acc, LEAD + NT + 16 * i + n - 1)
                        split_product(pe, ps[:, 6 + n % 2, 0:D], lambda f: hidh[:, s % 2, f, t * P:(t + 1) * P],
                                      lambda f: hidl[:, s % 2, f, t * P:(t + 1) * P],
                                      lambda f: wh[e][:, W2 + f * D:W2 + (f + 1) * D], lambda f: wl[e][:, W2 + f * D:W2 + (f + 1) * D],
                                      range(FT)).then_inc(o_ps, 1)

                for s in range(4):
                    up(s)
                    if s >= 1:
                        down(s - 1)
                down(3)


def build(nc, dram, out):
    with ExitStack() as ctx:
        c = Core(nc, dram, out, ctx)
        layer0_linear_attention(c)
        normalise(c, "n1", c.y, c.x, turned="split")
        layer0_gated_attention(c)
        normalise(c, "n2", c.y, c.x, turned="both")
        layer1_decay_attention(c)
        normalise(c, "n3", c.y, c.x)
        normalise(c, "n4", c.x, c.scratch, rms=True, turned="split", weight=dram["norm1"])
        layer1_grouped_attention(c)
        normalise(c, "n5", c.y, c.scratch, rms=True, turned="split", weight=dram["norm2"])
        layer1_experts(c)
        normalise(c, "n6", c.y, c.x, store=True)


def blocks(wT):
    return np.ascontiguousarray(wT.reshape(wT.shape[0] // P, P, wT.shape[1]).transpose(1, 0, 2))


def constants():
    ident = np.eye(P)
    key, q = np.mgrid[0:P, 0:P]
    tri = (q >= key).astype(np.float32)
    tri3 = np.concatenate([tri, np.ones((P, P)), tri], axis=1)
    neg = np.where(key <= q, 0.0, -1e30).T
    neg3 = np.concatenate([neg, np.zeros((P, P)), neg], axis=1)
    par = np.stack([(np.arange(P) // HD0 % 2 == n) * float(HD0) ** -0.5 for n in range(2)], axis=1)
    iota = np.tile(np.arange(16.0), (P, 1))
    return np.concatenate([ident, tri3, neg3, par, iota], axis=1).astype(np.float32)


def rope_tables():
    inv = (1.0 / np.float32(1000000.0) ** (np.arange(0, HDQ, 2, dtype=np.float32) / HDQ)).astype(np.float32)
    ang = np.arange(SEQ, dtype=np.float32)[:, None] * inv[None, :]
    cos = np.concatenate([np.cos(ang), np.cos(ang)], axis=1).T
    sin = np.concatenate([np.sin(ang), -np.sin(ang)], axis=1).T
    cos, sin = np.tile(cos, (1, 2)), np.tile(sin, (1, 2))
    r = float(HDQ) ** -0.5
    return np.stack([cos, sin, cos * r, sin * r], axis=1).astype(np.float32)


def decays():
    factor = 1.0 - 0 / (32 - 1 + 1e-05) + 1e-05
    slope = (2.0 ** (-8.0 / H1)) ** (np.arange(H1) + 1.0) * factor
    dist = np.arange(SEQ)[None, :] - np.arange(P)[:, None]
    d = np.where(dist >= 0, np.exp(-slope[:, None, None] * np.maximum(dist, 0)), 0.0)
    d = np.concatenate([d, d[:, :, 0:P]], axis=2)
    return d.reshape(PAIRS, 2, P, CAUSAL).transpose(0, 2, 1, 3).astype(np.float32)


def padded(steps):
    return np.stack(steps + [np.zeros_like(steps[0])])


def kernel(**inputs):
    import concourse.bacc as bacc
    from concourse.bass_utils import run_bass_kernel_spmd

    a = {k: np.asarray(v) for k, v in inputs.items()}
    x = a["L0_attn_x"].reshape(TOK, D)
    diag = np.zeros((P, 4, P), np.float32)
    for n, name in enumerate(("fq1", "fq2", "fk1", "fk2")):
        for h in range(P // HD0):
            s = slice(h * HD0, (h + 1) * HD0)
            diag[s, n, s] = a[f"L0_attn_{name}_w"].T
    arrays = {
        "consts": constants(),
        "x": blocks(x),
        "xT": blocks(x.T),
        "w0": np.stack([blocks(a[f"L0_attn_{n}"].T) for n in ("wq", "wk", "wv")], axis=1),
        "maps": diag,
        "vecs": np.stack([np.tile(a[f"L0_attn_{n}"], P // HD0) for n in ("fq1_b", "fq2_b", "fk1_b", "fk2_b", "norm_w")], axis=1),
        "wo0": blocks(a["L0_attn_wo"].T),
        "w_gated": blocks(np.concatenate([a["L0_ffn_W_qkv"], a["L0_ffn_W_gate"]], axis=0).T),
    }
    qkv = a["L1_attn_qkv_w"].reshape(PAIRS, 2, 3, HD1, D).transpose(0, 2, 1, 3, 4).reshape(PAIRS, 3 * P, D)
    qk, v = qkv[:, :2 * P], qkv[:, 2 * P:]
    gates = a["L1_attn_gate_w"].reshape(PAIRS, P, D)
    wq, wk, wv = (a[f"L1_ffn_{n}"] for n in ("wq", "wk", "wv"))
    w1, w3, w2 = (a[f"L1_ffn_{n}"] for n in ("w1", "w3", "w2"))

    def head(w, h):
        return blocks(w[:, h * HDQ:(h + 1) * HDQ])

    arrays |= {
        "w_decay": padded([blocks(np.concatenate([qk[i], gates[i], v[i]], axis=0).T) for i in range(PAIRS)]),
        "decay": decays(),
        "wo_decay": blocks(a["L1_attn_out_w"].T),
        "norm_decay": a["L1_attn_norm_w"].reshape(PAIRS, P).T,
        "norm1": a["L1_ffn_norm1_w"].reshape(KD, P).T,
        "norm2": a["L1_ffn_norm2_w"].reshape(KD, P).T,
        "w_grouped": padded([np.stack([head(wk, g), head(wv, g)] + [head(wq, GROUP * g + j) for j in range(GROUP)], axis=1) for g in range(HKV)]),
        "wo_grouped": blocks(a["L1_ffn_wo"]),
        "rope": rope_tables(),
        "w_router": blocks(a["L1_ffn_gate_w"]),
        "w_experts": padded([np.concatenate([blocks(w[e]).reshape(P, -1) for w in (w1, w3, w2)], axis=1) for e in range(EXPERTS)]),
    }
    nc = bacc.Bacc("TRN2", target_bir_lowering=False, num_devices=1)
    dram = {}
    for name in arrays:
        arrays[name] = np.ascontiguousarray(arrays[name])
        dram[name] = nc.dram_tensor("in_" + name, arrays[name].shape, mybir.dt.from_np(arrays[name].dtype), kind="ExternalInput").ap()
    out = nc.dram_tensor("out", (TOK, D), F32, kind="ExternalOutput").ap()
    build(nc, dram, out.rearrange("(t p) d -> p t d", p=P))
    r = run_bass_kernel_spmd(nc, [{"in_" + k: v for k, v in arrays.items()}], core_ids=[0])
    return r.results[0]["out"].reshape(BATCH, SEQ, D)
```

```python
from contextlib import ExitStack

import numpy as np

import concourse.bass as bass
from concourse import mybir

F32 = mybir.dt.float32
F32R = mybir.dt.float32r
BF16 = mybir.dt.bfloat16
ALU = mybir.AluOpType
ACT = mybir.ActivationFunctionType
X = mybir.AxisListType.X

P = 128
LEAD = 8
EPS = 1e-5
BATCH, SEQ, D = 4, 256, 256
TOK = BATCH * SEQ
NT = TOK // P
KD = D // P
TPB = SEQ // P
CAUSAL = 384

H0, HD0 = 16, 16
H1, HD1 = 32, 64
PAIRS = H1 // 2
HQ, HKV, HDQ = 16, 4, 128
GROUP = HQ // HKV
EXPERTS, FF = 8, 512

C_IDENT = 0
C_TRI = C_IDENT + P
C_NEG = C_TRI + CAUSAL
C_PAR = C_NEG + CAUSAL
C_IOTA = C_PAR + 2
C_END = C_IOTA + 16


class Core:

    def __init__(self, nc, dram, out, ctx):
        self.nc, self.dram, self.out, self.ctx = nc, dram, out, ctx
        self.ps = ctx.enter_context(nc.psum_tensor("ps", [P, 8, 512], F32))
        self.norm_sems, self.norm_counts = None, dict.fromkeys(
            "w_in stat_done mean_done var_ready sd_ready rstd_ready n_ready turn_ps hi_ready lo_ready stored".split(), 0)
        self.consts = self.tile(ctx, "consts", [P, C_END])
        self.ident = self.consts[:, C_IDENT:C_IDENT + P]
        self.tri = self.consts[:, C_TRI:C_TRI + CAUSAL]
        self.parity = self.consts[:, C_PAR:C_PAR + 2]
        self.iota = self.consts[:, C_IOTA:C_IOTA + 16]
        self.ident16 = self.tile(ctx, "ident16", [P, P], BF16)
        self.neg16 = self.tile(ctx, "neg16", [P, CAUSAL], BF16)
        self.warm16 = self.tile(ctx, "warm16", [P, 512], BF16)
        self.x = self.tile(ctx, "x", [P, NT, D])
        self.y = self.tile(ctx, "y", [P, NT, D])
        self.scratch = self.tile(ctx, "scratch", [P, NT, D])
        self.w_gated = self.tile(ctx, "w_gated", [P, KD, 3 * D + H0])
        self.wh_gated = self.tile(ctx, "wh_gated", [P, KD, 3 * D + H0], F32R)
        self.wl_gated = self.tile(ctx, "wl_gated", [P, KD, 3 * D + H0], F32R)
        self.xT = self.tile(ctx, "xT", [P, KD, TOK])
        self.xTh = self.tile(ctx, "xTh", [P, KD, TOK], F32R)
        self.xTl = self.tile(ctx, "xTl", [P, KD, TOK], F32R)

    def tile(self, ctx, name, shape, dt=F32):
        return ctx.enter_context(self.nc.sbuf_tensor(name, shape, dt))

    def sems(self, ctx, prefix, names):
        return [self.ctx.enter_context(self.nc.semaphore(f"{prefix}_{n}")) for n in names.split()]


def give_lead(eng, sems):
    for s in sems:
        eng.sem_inc(s, LEAD)


class Chain:

    def __init__(self, eng, sem, base=0):
        self.eng, self.sem, self.base, self.n = eng, sem, base, 0

    def __call__(self, ins):
        self.n += 1
        ins.then_inc(self.sem, 1)
        self.eng.wait_ge(self.sem, self.base + self.n)


def split_product(pe, out, wh, wl, xh, xl, ks, skip=False):
    passes = [(wh, xl), (wl, xh), (wh, xh)]
    n = 0
    for k in ks:
        for w, x in passes:
            mm = pe.matmul(out, w(k), x(k), start=(n == 0), stop=(n == 3 * len(ks) - 1))
            n += 1
    return mm


def keep_warm(c, pe, out, n):
    for _ in range(n):
        pe.matmul(out, c.warm16[:, 0:P], c.warm16[:, 0:out.shape[1]], start=True, stop=True)


def layer0_linear_attention(c):
    nc, ps = c.nc, c.ps
    SLOTS = 2
    QUADS = 4
    PAD = 32
    with ExitStack() as ctx:
        def sb(name, shape, dt=F32):
            return c.tile(ctx, "a_" + name, shape, dt)

        w = sb("w", [P, 3, KD, D])
        wh = sb("wh", [P, 3, KD, D], F32R)
        wl = sb("wl", [P, 3, KD, D], F32R)
        maps = sb("maps", [P, 4, P])
        vecs = sb("vecs", [P, 5])
        wo = sb("wo", [P, KD, D])
        q_all = sb("q_all", [P, KD, TOK])
        k_all = sb("k_all", [P, KD, TOK])
        v_all = sb("v_all", [P, NT, D])
        v_pad = sb("v_pad", [P, SLOTS, TPB, H0, PAD])
        second = sb("second", [P, 3, KD, SEQ])
        q_par = sb("q_par", [P, 2, KD, SEQ])
        k_map = sb("k_map", [P, KD, SEQ])
        s_m = sb("s_m", [P, 8, CAUSAL])
        o_sb = sb("o_sb", [P, 2, 512])
        o_sq = sb("o_sq", [P, TPB, D])
        o_n = sb("o_n", [P, TPB, D])
        o_nT = sb("o_nT", [P, KD, SEQ])
        stat = sb("stat", [P, 4, TPB * H0])
        par_bias = sb("par_bias", [P, 2])

        x_in, w_in, loaded = c.sems(ctx, "a", "x_in w_in loaded")
        pe_sems = p_ps, map_ps, s_ps, pv_ps, o_turned, on_turned, wo_ps = c.sems(ctx, "a", "p_ps map_ps s_ps pv_ps o_turned on_turned wo_ps")
        dve_sems = x_split, w_hi, w_split, v_copied, qmap_ready, kmap_ready, sm_ready, sum_ready, var_ready, r_ready, on_ready, oT_ready, y_ready, bias_ready = c.sems(
            ctx, "a", "x_split w_hi w_split v_copied qmap_ready kmap_ready sm_ready sum_ready var_ready r_ready on_ready oT_ready y_ready bias_ready")
        act_sems = x_hi, p_ready, second_q, second_k, o_ready, sq_ready, sd_ready = c.sems(
            ctx, "a", "x_hi p_ready second_q second_k o_ready sq_ready sd_ready")
        zeroed, next_in, next_hi = c.sems(ctx, "a", "zeroed next_in next_hi")
        block = ctx.enter_context(nc.Block())

        @block.sync
        def _(sp):
            for k in range(KD):
                sp.dma_start(c.xT[:, k, :], c.dram["xT"][:, k, :]).then_inc(x_in, 16)
            sp.dma_start(w[:], c.dram["w0"]).then_inc(w_in, 16)
            sp.dma_start(maps[:], c.dram["maps"]).then_inc(loaded, 16)
            sp.dma_start(vecs[:], c.dram["vecs"]).then_inc(loaded, 16)
            sp.dma_start(c.consts[:], c.dram["consts"]).then_inc(loaded, 16)
            sp.dma_start(wo[:], c.dram["wo0"]).then_inc(loaded, 16)
            sp.dma_start(c.x[:], c.dram["x"]).then_inc(loaded, 16)
            sp.dma_start(c.w_gated[:], c.dram["w_gated"]).then_inc(next_in, 16)

        @block.gpsimd
        def _(pool):
            pool.memset(c.warm16[:], 0.0).then_inc(zeroed, 1)
            pool.memset(v_pad[:], 0.0).then_inc(zeroed, 1)
            pool.wait_ge(next_in, 16)
            pool.tensor_copy(c.wh_gated[:], c.w_gated[:]).then_inc(next_hi, 1)
            pool.wait_ge(next_hi, 1)
            pool.tensor_tensor(c.wl_gated[:], c.w_gated[:], c.wh_gated[:].bitcast(F32), ALU.subtract)

        @block.vector
        def _(dve):
            give_lead(dve, dve_sems)
            for k in range(KD):
                dve.wait_ge(x_hi, LEAD + k + 1)
                dve.tensor_tensor(c.xTl[:, k, :], c.xT[:, k, :], c.xTh[:, k, :].bitcast(F32), ALU.subtract).then_inc(x_split, 1)
            dve.wait_ge(w_in, 16)
            for n in range(3):
                dve.tensor_copy(wh[:, n], w[:, n]).then_inc(w_hi, 1)
                dve.wait_ge(w_hi, LEAD + n + 1)
                dve.tensor_tensor(wl[:, n], w[:, n], wh[:, n].bitcast(F32), ALU.subtract).then_inc(w_split, 1)
            dve.wait_ge(loaded, 16 * 5)
            for par in range(2):
                dve.tensor_tensor(par_bias[:, par:par + 1], vecs[:, 1:2], c.parity[:, par:par + 1], ALU.mult).then_inc(bias_ready, 1)
            dve.tensor_copy(c.ident16[:], c.ident)
            dve.tensor_copy(c.neg16[:], c.consts[:, C_NEG:C_NEG + CAUSAL])
            dve.wait_ge(p_ready, LEAD + 12)
            dve.wait_ge(zeroed, 2)
            with dve.Fori(0, BATCH // SLOTS) as i:
                def at(u):
                    return SLOTS * i + u

                def prepare(u):
                    dve.wait_ge(pv_ps, LEAD + QUADS * (SLOTS * i + u) - QUADS * SLOTS + QUADS)
                    dve.tensor_scalar(v_pad[:, u].rearrange("p t h r -> p (t h) r")[:, :, 0:HD0],
                                      v_all[:, bass.ds(at(u) * TPB, TPB), :].rearrange("p t (h d) -> p (t h) d", h=H0), 1.0, None, ALU.mult).then_inc(v_copied, 1)
                    dve.wait_ge(map_ps, LEAD + 2 * at(u) + 1)
                    for par in range(2):
                        dve.wait_ge(second_q, LEAD + 2 * at(u) + par + 1)
                        dve.scalar_tensor_tensor(q_par[:, par].rearrange("p k s -> p (k s)"), ps[:, 3, :], vecs[:, 0:1],
                                                 second[:, par].rearrange("p k s -> p (k s)"), ALU.add, ALU.mult).then_inc(qmap_ready, 1)
                    dve.wait_ge(map_ps, LEAD + 2 * at(u) + 2)
                    dve.wait_ge(second_k, LEAD + at(u) + 1)
                    dve.scalar_tensor_tensor(k_map[:].rearrange("p k s -> p (k s)"), ps[:, 5, :], vecs[:, 2:3],
                                             second[:, 2].rearrange("p k s -> p (k s)"), ALU.add, ALU.mult).then_inc(kmap_ready, 1)

                def masks(u, quad):
                    for h in range(4 * quad, 4 * quad + 4):
                        dve.wait_ge(s_ps, LEAD + H0 * at(u) + h + 1)
                        dve.wait_ge(pv_ps, LEAD + QUADS * at(u) + quad - 1)
                        dve.tensor_tensor(s_m[:, h % 8, :], ps[:, 3 + h % 4, 0:CAUSAL], c.tri, ALU.mult).then_inc(sm_ready, 1)

                def moments(u):
                    dve.wait_ge(sq_ready, LEAD + TPB * (at(u) + 1))
                    dve.tensor_reduce(stat[:, 0, :], o_sq[:].rearrange("p t (h d) -> p (t h) d", h=H0), X, ALU.add).then_inc(sum_ready, 1)
                    dve.wait_ge(sum_ready, LEAD + at(u) + 1)
                    dve.tensor_scalar(stat[:, 1, :], stat[:, 0, :], 1.0 / HD0, EPS, ALU.mult, ALU.add).then_inc(var_ready, 1)

                def scale(u):
                    dve.wait_ge(sd_ready, LEAD + at(u) + 1)
                    dve.reciprocal(stat[:, 3, :], stat[:, 2, :]).then_inc(r_ready, 1)
                    dve.wait_ge(r_ready, LEAD + at(u) + 1)
                    for t in range(TPB):
                        dve.tensor_tensor(o_n[:, t, :].rearrange("p (h d) -> p h d", h=H0), ps[:, 1 + t, :].rearrange("p (h r) -> p h r", h=H0)[:, :, 0:HD0],
                                          stat[:, 3, t * H0:(t + 1) * H0].unsqueeze(2).broadcast_to((P, H0, HD0)), ALU.mult).then_inc(on_ready, 1)

                def weigh(u):
                    dve.wait_ge(on_turned, LEAD + at(u) + 1)
                    dve.tensor_scalar(o_nT[:].rearrange("p k s -> p (k s)"), ps[:, 1, :], vecs[:, 4:5], None, ALU.mult).then_inc(oT_ready, 1)

                def add(u):
                    dve.wait_ge(wo_ps, LEAD + at(u) + 1)
                    dve.tensor_tensor(c.y[:, bass.ds(at(u) * TPB, TPB), :], ps[:, 2, :].rearrange("p (t d) -> p t d", t=TPB),
                                      c.x[:, bass.ds(at(u) * TPB, TPB), :], ALU.add).then_inc(y_ready, 1)

                prepare(0)
                for quad in range(QUADS):
                    masks(0, quad)
                prepare(1)
                masks(1, 0)
                moments(0)
                masks(1, 1)
                scale(0)
                masks(1, 2)
                weigh(0)
                masks(1, 3)
                add(0)
                moments(1)
                scale(1)
                weigh(1)
                add(1)

        @block.scalar
        def _(act):
            give_lead(act, act_sems)
            for k in range(KD):
                act.wait_ge(x_in, 16 * KD)
                act.activation(c.xTh[:, k, :], c.xT[:, k, :], ACT.Copy).then_inc(x_hi, 1)
            for n in range(12):
                act.wait_ge(p_ps, LEAD + n + 1)
                if n < 8:
                    half, a, m = n // 4, n // 2 % 2, n % 2
                    dst = (q_all, k_all)[a][:, m, half * 512:(half + 1) * 512]
                else:
                    dst = v_all[:, 2 * (n - 8):2 * (n - 7), :].rearrange("p t d -> p (t d)")
                act.activation(dst, ps[:, n % 8, :], ACT.Copy).then_inc(p_ready, 1)
            act.wait_ge(bias_ready, LEAD + 2)
            with act.Fori(0, BATCH // SLOTS) as i:
                def prepare(u):
                    act.wait_ge(map_ps, LEAD + 2 * (SLOTS * i + u) + 1)
                    act.wait_ge(kmap_ready, LEAD + SLOTS * i + u)
                    for par in range(2):
                        act.activation(second[:, par].rearrange("p k s -> p (k s)"), ps[:, 4, :], ACT.Identity, bias=par_bias[:, par:par + 1],
                                       scale=c.parity[:, par:par + 1]).then_inc(second_q, 1)
                    act.wait_ge(map_ps, LEAD + 2 * (SLOTS * i + u) + 2)
                    act.activation(second[:, 2].rearrange("p k s -> p (k s)"), ps[:, 6, :], ACT.Identity, bias=vecs[:, 3:4]).then_inc(second_k, 1)

                def outputs(u):
                    for half in range(2):
                        act.wait_ge(pv_ps, LEAD + QUADS * (SLOTS * i + u) + 2 * half + 2)
                        act.wait_ge(o_turned, LEAD + TPB * (SLOTS * i + u))
                        act.activation(o_sb[:, half, :], ps[:, 7 * half, :], ACT.Copy).then_inc(o_ready, 1)

                def squares(u):
                    for t in range(TPB):
                        act.wait_ge(o_turned, LEAD + TPB * (SLOTS * i + u) + t + 1)
                        act.wait_ge(sum_ready, LEAD + SLOTS * i + u)
                        act.activation(o_sq[:, t, :].rearrange("p (h d) -> p h d", h=H0), ps[:, 1 + t, :].rearrange("p (h r) -> p h r", h=H0)[:, :, 0:HD0],
                                       ACT.Square).then_inc(sq_ready, 1)

                def root(u):
                    act.wait_ge(var_ready, LEAD + SLOTS * i + u + 1)
                    act.activation(stat[:, 2, :], stat[:, 1, :], ACT.Sqrt).then_inc(sd_ready, 1)

                prepare(0)
                outputs(0)
                prepare(1)
                squares(0)
                root(0)
                outputs(1)
                squares(1)
                root(1)

        @block.tensor
        def _(pe):
            give_lead(pe, pe_sems)
            pe.wait_ge(zeroed, 1)
            keep_warm(c, pe, ps[:, 7, :], 28)
            pe.wait_ge(x_split, LEAD + 2)
            for n in range(12):
                pe.wait_ge(w_split, LEAD + (n // 2 % 2 + 1 if n < 8 else 3))
                if n >= 8:
                    pe.wait_ge(p_ready, LEAD + n - 7)
                if n < 8:
                    half, a, m = slice(n // 4 * 512, (n // 4 + 1) * 512), n // 2 % 2, n % 2
                    mm = split_product(pe, ps[:, n % 8, :], lambda k: wh[:, a, k, m * P:(m + 1) * P], lambda k: wl[:, a, k, m * P:(m + 1) * P],
                                       lambda k: c.xTh[:, k, half], lambda k: c.xTl[:, k, half], range(KD))
                else:
                    for t in range(2):
                        tok = slice((2 * (n - 8) + t) * P, (2 * (n - 8) + t + 1) * P)
                        mm = split_product(pe, ps[:, n % 8, t * D:(t + 1) * D], lambda k: c.xTh[:, k, tok], lambda k: c.xTl[:, k, tok],
                                           lambda k: wh[:, 2, k, :], lambda k: wl[:, 2, k, :], range(KD))
                mm.then_inc(p_ps, 1)
            pe.wait_ge(p_ready, LEAD + 8)
            keep_warm(c, pe, ps[:, 7, :], 8)
            pe.wait_ge(p_ready, LEAD + 12)
            pe.wait_ge(loaded, 16 * 5)
            with pe.Fori(0, BATCH // SLOTS) as i:
                def at(u):
                    return SLOTS * i + u

                def prepare(u):
                    pe.wait_ge(sm_ready, LEAD + H0 * at(u))
                    for n, raw in enumerate((q_all, k_all)):
                        for f in range(2):
                            for m in range(KD):
                                mm = pe.matmul(ps[:, 3 + 2 * n + f, m * SEQ:(m + 1) * SEQ], maps[:, 2 * n + f, :], raw[:, m, bass.ds(at(u) * SEQ, SEQ)],
                                               start=True, stop=True)
                        mm.then_inc(map_ps, 1)

                def scores(u, quad):
                    if quad == 0:
                        pe.wait_ge(qmap_ready, LEAD + 2 * at(u) + 2)
                        pe.wait_ge(kmap_ready, LEAD + at(u) + 1)
                    for h in range(4 * quad, 4 * quad + 4):
                        m, g, par = h // 8, 32 * (h % 8 // 2), h % 2
                        bank = ps[:, 3 + h % 4, :]
                        if h >= 4:
                            pe.wait_ge(sm_ready, LEAD + H0 * at(u) + h - 3)
                        keep_warm(c, pe, bank[:, 0:CAUSAL], 1)
                        pe.matmul(bank[:, 0:SEQ], k_map[g:g + 32, m, 0:P], q_par[g:g + 32, par, m, :], start=True, stop=True, tile_position=(g, 0))
                        pe.matmul(bank[:, SEQ:CAUSAL], k_map[g:g + 32, m, P:SEQ], q_par[g:g + 32, par, m, P:SEQ], start=True, stop=True,
                                  tile_position=(g, 0)).then_inc(s_ps, 1)

                def values(u, quad):
                    if quad == 0:
                        pe.wait_ge(v_copied, LEAD + at(u) + 1)
                    if quad % 2 == 0:
                        pe.wait_ge(o_ready, LEAD + 2 * at(u) + quad // 2 - 1)
                    pe.wait_ge(sm_ready, LEAD + H0 * at(u) + 4 * quad + 4)
                    out = ps[:, 7 * (quad // 2), quad % 2 * SEQ:(quad % 2 + 1) * SEQ]
                    for q in range(4):
                        h = 4 * quad + q
                        pe.matmul(out[PAD * q:PAD * (q + 1), :], v_pad[:, u, 0, h, :], s_m[:, h % 8, 0:SEQ], start=True, stop=False)
                    for q in range(4):
                        h = 4 * quad + q
                        mm = pe.matmul(out[PAD * q:PAD * (q + 1), P:SEQ], v_pad[:, u, 1, h, :], s_m[:, h % 8, SEQ:CAUSAL], start=False, stop=True)
                    mm.then_inc(pv_ps, 1)

                def turn(u):
                    pe.wait_ge(o_ready, LEAD + 2 * at(u) + 2)
                    pe.wait_ge(y_ready, LEAD + at(u))
                    for t in range(TPB):
                        for j in range(4):
                            mm = pe.transpose(ps[:, 1 + t, j * P:(j + 1) * P], o_sb[:, j // 2, j % 2 * SEQ + t * P:j % 2 * SEQ + (t + 1) * P], c.ident)
                        mm.then_inc(o_turned, 1)

                def turn_back(u):
                    pe.wait_ge(on_ready, LEAD + TPB * (at(u) + 1))
                    for t in range(TPB):
                        for m in range(KD):
                            mm = pe.transpose(ps[:, 1, m * SEQ + t * P:m * SEQ + (t + 1) * P], o_n[:, t, m * P:(m + 1) * P], c.ident)
                    mm.then_inc(on_turned, 1)

                def project(u):
                    pe.wait_ge(oT_ready, LEAD + at(u) + 1)
                    for t in range(TPB):
                        for k in range(KD):
                            mm = pe.matmul(ps[:, 2, t * D:(t + 1) * D], o_nT[:, k, t * P:(t + 1) * P], wo[:, k, :], start=(k == 0), stop=(k == KD - 1))
                    mm.then_inc(wo_ps, 1)

                prepare(0)
                keep_warm(c, pe, ps[:, 7, :], 14)
                scores(0, 0)
                for quad in range(1, QUADS):
                    scores(0, quad)
                    values(0, quad - 1)
                prepare(1)
                values(0, QUADS - 1)
                turn(0)
                keep_warm(c, pe, ps[:, 7, :], 6)
                scores(1, 0)
                scores(1, 1)
                values(1, 0)
                scores(1, 2)
                turn_back(0)
                values(1, 1)
                scores(1, 3)
                values(1, 2)
                project(0)
                values(1, 3)
                turn(1)
                keep_warm(c, pe, ps[:, 7, :], 16)
                turn_back(1)
                keep_warm(c, pe, ps[:, 7, :], 5)
                project(1)


def normalise(c, tag, src, dst, rms=False, turned=None, weight=None, store=False):
    nc, ps = c.nc, c.ps
    with ExitStack() as ctx:
        def sb(name, shape, dt=F32):
            return c.tile(ctx, f"{tag}_{name}", shape, dt)

        stats = sb("stats", [P, NT, 6])
        mv = sb("mv", [P, NT, 2])
        var = sb("var", [P, NT])
        sd = sb("sd", [P, NT])
        rstd = sb("rstd", [P, NT])
        junk = sb("junk", [P, D])
        wcol = sb("wcol", [P, KD])
        names = "w_in stat_done mean_done var_ready sd_ready rstd_ready n_ready turn_ps hi_ready lo_ready stored"
        if not c.norm_sems:
            c.norm_sems = c.sems(ctx, "norm", names)
        w_in, stat_done, mean_done, var_ready, sd_ready, rstd_ready, n_ready, turn_ps, hi_ready, lo_ready, stored = c.norm_sems
        so = dict(c.norm_counts)
        block = ctx.enter_context(nc.Block())

        @block.sync
        def _(sp):
            if weight is not None:
                sp.dma_start(wcol[:], weight).then_inc(w_in, 16)
            if store:
                for t in range(NT):
                    sp.wait_ge(n_ready, so["n_ready"] + t + 1)
                    sp.dma_start(c.out[:, t, :], dst[:, t, :]).then_inc(stored, 16)
                sp.wait_ge(stored, so["stored"] + 16 * NT)

        @block.vector
        def _(dve):
            if rms:
                dve.wait_ge(stat_done, so["stat_done"] + NT)
                dve.tensor_scalar(var[:], sd[:], 1.0 / D, EPS, ALU.mult, ALU.add).then_inc(var_ready, 1)
            else:
                for t in range(NT):
                    dve.bn_stats(stats[:, t, :], src[:, t, :]).then_inc(stat_done, 1)
                dve.wait_ge(stat_done, so["stat_done"] + NT)
                for t in range(NT):
                    dve.bn_aggr(mv[:, t, :], stats[:, t, :]).then_inc(mean_done, 1)
                dve.wait_ge(mean_done, so["mean_done"] + NT)
                dve.tensor_scalar(var[:], mv[:, :, 1], EPS, None, ALU.add).then_inc(var_ready, 1)
            dve.wait_ge(sd_ready, so["sd_ready"] + 1)
            dve.reciprocal(rstd[:], sd[:]).then_inc(rstd_ready, 1)
            dve.wait_ge(rstd_ready, so["rstd_ready"] + 1)
            for t in range(NT):
                if rms:
                    dve.tensor_scalar(dst[:, t, :], src[:, t, :], rstd[:, t:t + 1], None, ALU.mult).then_inc(n_ready, 1)
                else:
                    dve.tensor_scalar(dst[:, t, :], src[:, t, :], mv[:, t, 0:1], rstd[:, t:t + 1], ALU.subtract, ALU.mult).then_inc(n_ready, 1)
            if turned in ("split", "both"):
                for n in range(4):
                    half, k = n // 2, n % 2
                    dve.wait_ge(hi_ready, so["hi_ready"] + n + 1)
                    cols = slice(half * 512, (half + 1) * 512)
                    if weight is None:
                        dve.tensor_tensor(c.xTl[:, k, cols], ps[:, n, :], c.xTh[:, k, cols].bitcast(F32), ALU.subtract).then_inc(lo_ready, 1)
                    else:
                        dve.scalar_tensor_tensor(c.xTl[:, k, cols], ps[:, n, :], wcol[:, k:k + 1], c.xTh[:, k, cols].bitcast(F32),
                                                 ALU.mult, ALU.subtract).then_inc(lo_ready, 1)

        @block.scalar
        def _(act):
            if rms:
                for t in range(NT):
                    if t >= 1:
                        act.wait_ge(stat_done, so["stat_done"] + t)
                    act.activation(junk[:], src[:, t, :], ACT.Square, accum_out=sd[:, t:t + 1]).then_inc(stat_done, 1)
            act.wait_ge(var_ready, so["var_ready"] + 1)
            act.activation(sd[:], var[:], ACT.Sqrt).then_inc(sd_ready, 1)
            if weight is not None:
                act.wait_ge(w_in, so["w_in"] + 16)
            for n in range(4 if turned else 0):
                half, k = n // 2, n % 2
                act.wait_ge(turn_ps, so["turn_ps"] + n + 1)
                if turned == "both":
                    act.activation(c.xT[:, k, half * 512:(half + 1) * 512], ps[:, n, :], ACT.Copy)
                to = (c.xT if turned == "whole" else c.xTh)[:, k, half * 512:(half + 1) * 512]
                if weight is None:
                    act.activation(to, ps[:, n, :], ACT.Copy).then_inc(hi_ready, 1)
                else:
                    act.activation(to, ps[:, n, :], ACT.Copy, scale=wcol[:, k:k + 1]).then_inc(hi_ready, 1)

        @block.tensor
        def _(pe):
            for n in range(4 if turned else 0):
                half, k = n // 2, n % 2
                pe.wait_ge(n_ready, so["n_ready"] + 4 * half + 4)
                for t in range(4):
                    mm = pe.transpose(ps[:, n, t * P:(t + 1) * P], dst[:, 4 * half + t, k * P:(k + 1) * P], c.ident)
                mm.then_inc(turn_ps, 1)

        raised = {"stat_done": NT, "mean_done": 0 if rms else NT, "var_ready": 1, "sd_ready": 1, "rstd_ready": 1, "n_ready": NT,
                  "w_in": 16 if weight is not None else 0, "turn_ps": 4 if turned else 0, "hi_ready": 4 if turned else 0,
                  "lo_ready": 4 if turned in ("split", "both") else 0, "stored": 16 * NT if store else 0}
        c.norm_counts = {n: so[n] + raised[n] for n in raised}


def layer0_gated_attention(c):
    nc, ps = c.nc, c.ps
    QKV = 3 * D
    SLOTS = 2
    ITEMS = SLOTS * H0
    QUADS = ITEMS // 4
    PAD = 32
    with ExitStack() as ctx:
        def sb(name, shape, dt=F32):
            return c.tile(ctx, "g_" + name, shape, dt)

        wh, wl = c.wh_gated, c.wl_gated
        z_T = sb("z_T", [H0, TOK])
        gate = sb("gate", [P, 6, NT, H0])
        gstat = sb("gstat", [P, 6, NT])
        picked = sb("picked", [P, 2, H0, HD0])
        k_tok = sb("k_tok", [P, NT, HD0])
        v_pad = sb("v_pad", [P, NT, PAD])
        k_pad = sb("k_pad", [P, NT, 2, P])
        k_rows = sb("k_rows", [P, 8, TOK])
        q_all = sb("q_all", [P, KD, TOK])
        q_T = sb("q_T", [P, SLOTS, KD, SEQ])
        v_seq = sb("v_seq", [P, SLOTS, TPB, PAD])
        neg_max = sb("neg_max", [P, 4, 2])
        probs = sb("probs", [P, 4, CAUSAL])
        probsT = sb("probsT", [P, 8, CAUSAL])
        o_sb = sb("o_sb", [P, 2, 512])
        o_tok = sb("o_tok", [P, 2, H0, HD0])
        rsum = sb("rsum", [P, 2, H0])

        pool_sems = (padded,) = c.sems(ctx, "g", "padded")
        pe_sems = z_ps, lg_ps, kv_ps, q_ps, kT_ps, s_ps, t_ps, pv_ps, o_turned = c.sems(
            ctx, "g", "z_ps lg_ps kv_ps q_ps kT_ps s_ps t_ps pv_ps o_turned")
        dve_sems = z_ready, picked_ps, k_ready, copied, nm_ready, pT_ready, rs_ready, o_scaled, kT_copied, chain = c.sems(
            ctx, "g", "z_ready picked_ps k_ready copied nm_ready pT_ready rs_ready o_scaled kT_copied chain")
        act_sems = z_copied, e_ready, q_ready, kT_ready, p_ready, o_ready = c.sems(ctx, "g", "z_copied e_ready q_ready kT_ready p_ready o_ready")
        block = ctx.enter_context(nc.Block())

        @block.gpsimd
        def _(pool):
            give_lead(pool, pool_sems)
            pool.memset(k_pad[:], 0.0).then_inc(padded, 1)
            pool.memset(v_pad[:], 0.0).then_inc(padded, 1)
            pool.wait_ge(padded, LEAD + 2)
            pool.memset(v_pad[:, :, HD0:HD0 + 1], 1.0).then_inc(padded, 1)
            pool.memset(k_rows[:], 0.0).then_inc(padded, 1)

        @block.vector
        def _(dve):
            give_lead(dve, dve_sems)
            link = Chain(dve, chain, LEAD)
            z, e, cand, one_hot, top_hot, eq = (gate[:, n] for n in range(6))
            nmax, esum, emax, erec, top, first = (gstat[:, n] for n in range(6))

            def wide(a):
                return a.unsqueeze(2).broadcast_to((P, NT, H0))

            dve.wait_ge(lg_ps, LEAD + 1)
            logits = ps[:, 0, 0:NT * H0].rearrange("p (t h) -> p t h", t=NT)
            link(dve.tensor_reduce(nmax, logits, X, ALU.max, negate=True))
            dve.tensor_tensor(z, logits, wide(nmax), ALU.add).then_inc(z_ready, 1)
            dve.wait_ge(e_ready, LEAD + 1)
            dve.tensor_reduce(esum, e, X, ALU.add)
            link(dve.tensor_reduce(emax, e, X, ALU.max))
            link(dve.reciprocal(erec, esum))
            dve.tensor_tensor(top, emax, erec, ALU.mult)
            link(dve.tensor_tensor(eq, e, wide(emax), ALU.is_equal))
            link(dve.scalar_tensor_tensor(cand, eq, -16.0, c.iota.unsqueeze(1).broadcast_to((P, NT, H0)), ALU.mult, ALU.add))
            link(dve.tensor_reduce(first, cand, X, ALU.min))
            link(dve.tensor_tensor(one_hot, cand, wide(first), ALU.is_equal))
            link(dve.tensor_tensor(top_hot, one_hot, wide(top), ALU.mult))
            dve.wait_ge(padded, LEAD + 3)
            for t in range(NT):
                dve.wait_ge(kv_ps, LEAD + t + 1)
                kv = ps[:, 5 + t % 3, :].rearrange("p (a h d) -> p a h d", a=2, h=H0)
                dve.tensor_tensor(picked[:, 0], kv[:, 0], one_hot[:, t, :].unsqueeze(2).broadcast_to((P, H0, HD0)), ALU.mult)
                dve.tensor_tensor(picked[:, 1], kv[:, 1], top_hot[:, t, :].unsqueeze(2).broadcast_to((P, H0, HD0)), ALU.mult).then_inc(picked_ps, 1)
                dve.wait_ge(picked_ps, LEAD + t + 1)
                dve.tensor_reduce(v_pad[:, t, 0:HD0], picked[:, 1].rearrange("p h d -> p d h"), X, ALU.add)
                link(dve.tensor_reduce(k_tok[:, t, :], picked[:, 0].rearrange("p h d -> p d h"), X, ALU.add))
                for par in range(2):
                    dst = k_pad[:, t, par, :].rearrange("p (g r) -> p g r", g=4)[:, :, par * HD0:(par + 1) * HD0]
                    dve.tensor_copy(dst, k_tok[:, t, :].unsqueeze(1).broadcast_to((P, 4, HD0))).then_inc(k_ready, 1)
            dve.wait_ge(padded, LEAD + 4)
            for n in range(4):
                half, par = n // 2, n % 2
                dve.wait_ge(kT_ps, LEAD + n + 1)
                for g in range(2, 4):
                    rows = slice(32 * g, 32 * g + 32)
                    dve.tensor_copy(k_rows[rows, 2 * g + par, half * 512:(half + 1) * 512], ps[rows, 1 + n, :]).then_inc(kT_copied, 1)
            with dve.Fori(0, BATCH // SLOTS) as i:
                dve.wait_ge(pv_ps, LEAD + QUADS * i)
                for u in range(SLOTS):
                    s = SLOTS * i + u
                    dve.tensor_scalar(q_T[:, u], q_all[:, :, bass.ds(s * SEQ, SEQ)], 1.0, None, ALU.mult)
                    dve.tensor_scalar(v_seq[:, u], v_pad[:, bass.ds(s * TPB, TPB), :], 1.0, None, ALU.mult).then_inc(copied, 1)
                for n in range(ITEMS + 9):
                    if n < ITEMS:
                        dve.wait_ge(s_ps, LEAD + ITEMS * i + n + 1)
                        dve.wait_ge(p_ready, LEAD + ITEMS * i + n - 3)
                        dve.tensor_reduce(neg_max[:, n % 4, 0:1], ps[:, n % 3, 0:P], X, ALU.max, negate=True)
                        dve.tensor_reduce(neg_max[:, n % 4, 1:2], ps[:, n % 3, P:CAUSAL], X, ALU.max, negate=True).then_inc(nm_ready, 1)
                    m = n - 3
                    if 0 <= m < ITEMS:
                        dve.wait_ge(t_ps, LEAD + ITEMS * i + m + 1)
                        dve.wait_ge(pv_ps, LEAD + QUADS * i + m // 4 - 1)
                        dve.tensor_copy(probsT[:, m % 8, :], ps[:, 3 + m % 2, 0:CAUSAL]).then_inc(pT_ready, 1)
                    for u in range(SLOTS):
                        for t, at in enumerate((22, 24)):
                            if n == H0 * u + at:
                                seq = TPB * (SLOTS * i + u) + t
                                turned = ps[:, 5, :].rearrange("p (h r) -> p h r", h=H0)
                                dve.wait_ge(o_turned, LEAD + seq + 1)
                                dve.reciprocal(rsum[:, t, :], turned[:, :, HD0]).then_inc(rs_ready, 1)
                                dve.wait_ge(rs_ready, LEAD + seq + 1)
                                dve.tensor_tensor(o_tok[:, t], turned[:, :, 0:HD0], rsum[:, t, :].unsqueeze(2).broadcast_to((P, H0, HD0)), ALU.mult).then_inc(o_scaled, 1)
                                dve.wait_ge(o_scaled, LEAD + seq + 1)
                                tile = bass.ds(seq, 1)
                                dve.tensor_tensor(c.y[:, tile, :], o_tok[:, t].rearrange("p h d -> p (h d)").unsqueeze(1), c.x[:, tile, :], ALU.add)

        @block.scalar
        def _(act):
            give_lead(act, act_sems)
            for n in range(2):
                act.wait_ge(z_ps, LEAD + n + 1)
                act.activation(z_T[:, n * 512:(n + 1) * 512], ps[0:H0, 5 + n, :], ACT.Copy).then_inc(z_copied, 1)
            act.wait_ge(z_ready, LEAD + 1)
            act.activation(gate[:, 1], gate[:, 0], ACT.Exp).then_inc(e_ready, 1)
            for n in range(4):
                act.wait_ge(q_ps, LEAD + n + 1)
                act.activation(q_all[:, n // 2, n % 2 * 512:(n % 2 + 1) * 512], ps[:, 1 + n, :], ACT.Copy, scale=float(HD0) ** -0.5).then_inc(q_ready, 1)
            act.wait_ge(padded, LEAD + 4)
            for n in range(4):
                half, par = n // 2, n % 2
                act.wait_ge(kT_ps, LEAD + n + 1)
                for g in range(2):
                    rows = slice(32 * g, 32 * g + 32)
                    act.activation(k_rows[rows, 2 * g + par, half * 512:(half + 1) * 512], ps[rows, 1 + n, :], ACT.Copy).then_inc(kT_ready, 1)
            with act.Fori(0, BATCH // SLOTS) as i:
                for n in range(ITEMS + 5):
                    if n < ITEMS:
                        act.wait_ge(nm_ready, LEAD + ITEMS * i + n + 1)
                        act.wait_ge(t_ps, LEAD + ITEMS * i + n - 3)
                        for b, cols in enumerate((slice(0, P), slice(P, CAUSAL))):
                            ex = act.activation(probs[:, n % 4, cols], ps[:, n % 3, cols], ACT.Exp, bias=neg_max[:, n % 4, b:b + 1])
                        ex.then_inc(p_ready, 1)
                    for u in range(SLOTS):
                        for half, at in enumerate((12, 20)):
                            if n == H0 * u + at:
                                act.wait_ge(pv_ps, LEAD + QUADS * i + 4 * u + 2 * half + 2)
                                act.wait_ge(o_turned, LEAD + TPB * (SLOTS * i + u))
                                act.activation(o_sb[:, half, :], ps[:, 6 + half, :], ACT.Copy).then_inc(o_ready, 1)

        @block.tensor
        def _(pe):
            give_lead(pe, pe_sems)
            for n in range(2):
                half = slice(n * 512, (n + 1) * 512)
                split_product(pe, ps[0:H0, 5 + n, :], lambda k: wh[:, k, QKV:], lambda k: wl[:, k, QKV:],
                              lambda k: c.xTh[:, k, half], lambda k: c.xTl[:, k, half], range(KD)).then_inc(z_ps, 1)
            for n in range(4):
                if n == 1:
                    pe.wait_ge(z_copied, LEAD + 2)
                    for t in range(NT):
                        mm = pe.transpose(ps[:, 0, t * H0:(t + 1) * H0], z_T[:, t * P:(t + 1) * P], c.ident[0:H0, 0:H0])
                    mm.then_inc(lg_ps, 1)
                m, half = n // 2, slice(n % 2 * 512, (n % 2 + 1) * 512)
                split_product(pe, ps[:, 1 + n, :], lambda k: wh[:, k, m * P:(m + 1) * P], lambda k: wl[:, k, m * P:(m + 1) * P],
                              lambda k: c.xTh[:, k, half], lambda k: c.xTl[:, k, half], range(KD)).then_inc(q_ps, 1)
            for t in range(NT):
                tok = slice(t * P, (t + 1) * P)
                if t >= 3:
                    pe.wait_ge(picked_ps, LEAD + t - 2)
                split_product(pe, ps[:, 5 + t % 3, :], lambda k: c.xTh[:, k, tok], lambda k: c.xTl[:, k, tok],
                              lambda k: wh[:, k, D:QKV], lambda k: wl[:, k, D:QKV], range(KD)).then_inc(kv_ps, 1)
                if t >= NT - 2:
                    half = t - (NT - 2)
                    pe.wait_ge(q_ready, LEAD + 4)
                    pe.wait_ge(k_ready, LEAD + NT * (half + 1))
                    for par in range(2):
                        for tile in range(4):
                            mm = pe.transpose(ps[:, 1 + 2 * half + par, tile * P:(tile + 1) * P], k_pad[:, 4 * half + tile, par, :], c.ident)
                        mm.then_inc(kT_ps, 1)
            pe.wait_ge(kT_ready, LEAD + 8)
            pe.wait_ge(kT_copied, LEAD + 8)
            pe.wait_ge(picked_ps, LEAD + NT)
            with pe.Fori(0, BATCH // SLOTS) as i:
                def scores(n):
                    u, h = n // H0, n % H0
                    m, rows = h // 8, k_rows[:, h % 8, :]
                    bank = ps[:, n % 3, :]
                    if h == 0:
                        pe.wait_ge(copied, LEAD + SLOTS * i + u + 1)
                    pe.wait_ge(p_ready, LEAD + ITEMS * i + (n - 2 if n >= 3 else 0))
                    pe.matmul(bank[:, 0:CAUSAL], c.ident16[:], c.neg16[:], start=True, stop=False)
                    pe.matmul(bank[:, 0:P], q_T[:, u, m, 0:P], rows[:, bass.ds((SLOTS * i + u) * SEQ, P)], start=False, stop=False)
                    pe.matmul(bank[:, P:CAUSAL], q_T[:, u, m, P:SEQ], rows[:, bass.ds((SLOTS * i + u) * SEQ, SEQ)], start=False, stop=True).then_inc(s_ps, 1)

                def turn(n):
                    pe.wait_ge(p_ready, LEAD + ITEMS * i + n + 1)
                    pe.wait_ge(pT_ready, LEAD + ITEMS * i + n - 1)
                    for b in range(3):
                        mm = pe.transpose(ps[:, 3 + n % 2, b * P:(b + 1) * P], probs[:, n % 4, b * P:(b + 1) * P], c.ident)
                    mm.then_inc(t_ps, 1)

                def values(quad):
                    u, j = quad // 4, quad % 4
                    pe.wait_ge(pT_ready, LEAD + ITEMS * i + 4 * quad + 4)
                    if j % 2 == 0:
                        pe.wait_ge(o_ready, LEAD + 2 * (SLOTS * i + u) + j // 2 - 1)
                    out = ps[:, 6 + j // 2, j % 2 * SEQ:(j % 2 + 1) * SEQ]
                    for q in range(4):
                        pe.matmul(out[PAD * q:PAD * (q + 1), :], v_seq[:, u, 0, :], probsT[:, (4 * quad + q) % 8, 0:SEQ], start=True, stop=False)
                    for q in range(4):
                        mm = pe.matmul(out[PAD * q:PAD * (q + 1), P:SEQ], v_seq[:, u, 1, :], probsT[:, (4 * quad + q) % 8, SEQ:CAUSAL],
                                       start=False, stop=True)
                    mm.then_inc(pv_ps, 1)

                def turn_outputs(u, t):
                    pe.wait_ge(o_ready, LEAD + 2 * (SLOTS * i + u) + 2)
                    pe.wait_ge(o_scaled, LEAD + TPB * (SLOTS * i + u) + t)
                    for j in range(4):
                        mm = pe.transpose(ps[:, 5, j * P:(j + 1) * P], o_sb[:, j // 2, j % 2 * SEQ + t * P:j % 2 * SEQ + (t + 1) * P], c.ident)
                    mm.then_inc(o_turned, 1)

                keep_warm(c, pe, ps[:, 2, :], 8)
                for n in range(ITEMS + 9):
                    if n < ITEMS:
                        scores(n)
                    if 2 <= n < ITEMS + 2:
                        turn(n - 2)
                    if n >= 7 and (n - 7) % 4 == 0 and (n - 7) // 4 < QUADS:
                        values((n - 7) // 4)
                    for u in range(SLOTS):
                        if n - H0 * u in (21, 23):
                            turn_outputs(u, (n - H0 * u - 21) // 2)


def layer1_decay_attention(c, following):
    nc, ps = c.nc, c.ps
    WC = 4 * P
    with ExitStack() as ctx:
        def sb(name, shape, dt=F32):
            return c.tile(ctx, "d_" + name, shape, dt)

        stage = sb("stage", [P, KD, WC])
        wh = sb("wh", [P, KD, 3 * P], F32R)
        wl = sb("wl", [P, KD, 3 * P], F32R)
        wv = sb("wv", [P, KD, P])
        decay = sb("decay", [P, 2, CAUSAL])
        wo = sb("wo", [P, PAIRS, D])
        norm_w = sb("norm_w", [P, PAIRS])
        q_T = sb("q_T", [P, TOK])
        k_T = sb("k_T", [P, TOK])
        v = sb("v", [P, NT, P])
        gate = sb("gate", [P, TOK])
        s_m = sb("s_m", [P, 4, CAUSAL])
        sq = sb("sq", [P, 2, SEQ])
        sq_sum = sb("sq_sum", [P, TOK])
        gated = sb("gated", [P, BATCH, SEQ])
        zeros = sb("zeros", [P, 512])
        ones = sb("ones", [P, 1])
        stat = sb("stat", [P, 3, NT])

        loaded, stage_in, decay_in = c.sems(ctx, "d", "loaded stage_in decay_in")
        pe_sems = proj_ps, s_ps, pv_ps, op_ps = c.sems(ctx, "d", "proj_ps s_ps pv_ps op_ps")
        dve_sems = sm_ready, og_ready = c.sems(ctx, "d", "sm_ready og_ready")
        act_sems = evac, sq_ready = c.sems(ctx, "d", "evac sq_ready")
        pool_sems = w_hi, w_split, sq_added = c.sems(ctx, "d", "w_hi w_split sq_added")
        zeroed, wo_scaled, ss_ps, var_ready, sd_ready, rs_ready = c.sems(ctx, "d", "zeroed wo_scaled ss_ps var_ready sd_ready rs_ready")
        block = ctx.enter_context(nc.Block())

        @block.sync
        def _(sp):
            sp.dma_start(stage[:], c.dram["w_decay"][0]).then_inc(stage_in, 16)
            sp.dma_start(wo[:], c.dram["wo_decay"]).then_inc(loaded, 16)
            sp.dma_start(norm_w[:], c.dram["norm_decay"]).then_inc(loaded, 16)
            following.load(sp)
            with sp.Fori(0, PAIRS) as i:
                sp.wait_ge(sm_ready, LEAD + 8 * i)
                sp.dma_start(decay[:], c.dram["decay"][bass.ds(i, 1)].rearrange("a p h s -> p (a h) s")).then_inc(decay_in, 16)
                sp.wait_ge(w_split, LEAD + i + 1)
                sp.dma_start(stage[:], c.dram["w_decay"][bass.ds(i + 1, 1)].rearrange("a p k n -> p (a k) n")).then_inc(stage_in, 16)

        @block.gpsimd
        def _(pool):
            give_lead(pool, pool_sems)
            pool.memset(zeros[:], 0.0).then_inc(zeroed, 1)
            pool.memset(ones[:], 1.0).then_inc(zeroed, 1)
            pool.memset(sq_sum[:], 0.0).then_inc(zeroed, 1)
            pool.wait_ge(zeroed, 3)

            def split(i, staged):
                nought = zeros[:, 0:1].unsqueeze(1)
                pool.wait_ge(stage_in, staged)
                pool.tensor_tensor(wh[:], stage[:, :, 0:3 * P], nought.broadcast_to((P, KD, 3 * P)), ALU.add).then_inc(w_hi, 1)
                pool.tensor_tensor(wv[:], stage[:, :, 3 * P:], nought.broadcast_to((P, KD, P)), ALU.add)
                pool.wait_ge(w_hi, LEAD + i + 1)
                pool.tensor_tensor(wl[:], stage[:, :, 0:3 * P], wh[:].bitcast(F32), ALU.subtract).then_inc(w_split, 1)

            split(0, 16)
            pool.wait_ge(loaded, 32)
            pool.tensor_tensor(wo[:], wo[:], norm_w[:].unsqueeze(2).broadcast_to((P, PAIRS, D)), ALU.mult).then_inc(wo_scaled, 1)
            with pool.Fori(0, PAIRS) as i:
                pool.wait_ge(proj_ps, LEAD + 8 * i + 8)
                split(i + 1, 16 * i + 32)
                for b in range(BATCH):
                    pool.wait_ge(sq_ready, LEAD + BATCH * i + b + 1)
                    pool.wait_ge(sq_added, LEAD + BATCH * i + b - 3)
                    cols = slice(b * SEQ, (b + 1) * SEQ)
                    pool.tensor_tensor(sq_sum[:, cols], sq_sum[:, cols], sq[:, b % 2, :], ALU.add).then_inc(sq_added, 1)

        @block.vector
        def _(dve):
            give_lead(dve, dve_sems)
            following.split(dve)

            with dve.Fori(0, PAIRS) as i:
                def gate_out(b):
                    dve.wait_ge(pv_ps, LEAD + BATCH * i + b + 1)
                    dve.wait_ge(op_ps, LEAD + BATCH * i + b - 3)
                    if b == 0:
                        dve.wait_ge(evac, LEAD + 8 * i + 8)
                    dve.scalar_tensor_tensor(gated[:, b, :], gate[:, b * SEQ:(b + 1) * SEQ], 1.0, ps[:, 6 + b % 2, 0:SEQ],
                                             ALU.add, ALU.mult).then_inc(og_ready, 1)

                dve.wait_ge(decay_in, 16 * i + 16)
                for s in range(8):
                    dve.wait_ge(s_ps, LEAD + 8 * i + s + 1)
                    dve.wait_ge(pv_ps, LEAD + BATCH * i + s // 2 - 1)
                    dve.tensor_tensor(s_m[:, s % 4, :], ps[:, 4 + s % 2, 0:CAUSAL], decay[:, s % 2, :], ALU.mult).then_inc(sm_ready, 1)
                    if s in (3, 5, 7):
                        gate_out((s - 3) // 2)
                gate_out(3)
            dve.wait_ge(ss_ps, 1)
            dve.tensor_scalar(stat[:, 0, :], ps[:, 4, 0:NT], 1.0 / (H1 * HD1), EPS, ALU.mult, ALU.add).then_inc(var_ready, 1)
            dve.wait_ge(sd_ready, 1)
            dve.reciprocal(stat[:, 2, :], stat[:, 1, :]).then_inc(rs_ready, 1)
            dve.wait_ge(rs_ready, 1)
            dve.tensor_scalar(stat[:, 0, :], stat[:, 2, :], 0.5, None, ALU.mult).then_inc(rs_ready, 1)
            dve.wait_ge(rs_ready, 2)
            for t in range(NT):
                dve.scalar_tensor_tensor(c.y[:, t, :], ps[:, t // 2, t % 2 * D:(t % 2 + 1) * D], stat[:, 0, t:t + 1], c.x[:, t, :], ALU.mult, ALU.add)

        @block.scalar
        def _(act):
            give_lead(act, act_sems)
            with act.Fori(0, PAIRS) as i:
                for n in range(8):
                    act.wait_ge(proj_ps, LEAD + 8 * i + n + 1)
                    half = slice(n % 2 * 512, (n % 2 + 1) * 512)
                    bank = ps[:, 4 + n % 2, :]
                    if n < 4:
                        act.activation((q_T, k_T)[n // 2][:, half], bank, ACT.Silu).then_inc(evac, 1)
                    elif n >= 6:
                        act.activation(v[:, n % 2 * 4:(n % 2 + 1) * 4, :].rearrange("p t d -> p (t d)"), bank, ACT.Silu).then_inc(evac, 1)
                    else:
                        if n == 4:
                            act.wait_ge(og_ready, LEAD + BATCH * i)
                        act.activation(gate[:, half], bank, ACT.Tanh, scale=0.5).then_inc(evac, 1)
                for b in range(BATCH):
                    act.wait_ge(og_ready, LEAD + BATCH * i + b + 1)
                    act.wait_ge(sq_added, LEAD + BATCH * i + b - 1)
                    act.activation(sq[:, b % 2, :], ps[:, 6 + b % 2, 0:SEQ], ACT.Square).then_inc(sq_ready, 1)
            act.wait_ge(var_ready, 1)
            act.activation(stat[:, 1, :], stat[:, 0, :], ACT.Sqrt).then_inc(sd_ready, 1)

        @block.tensor
        def _(pe):
            give_lead(pe, pe_sems)
            pe.wait_ge(zeroed, 3)
            pe.wait_ge(wo_scaled, 1)
            for bank in range(4):
                pe.matmul(ps[:, bank, :], zeros[:, 0:P], zeros[:], start=True, stop=False, skip_group_check=True)
            with pe.Fori(0, PAIRS) as i:
                pe.wait_ge(w_split, LEAD + i + 1)
                for n in range(8):
                    bank = ps[:, 4 + n % 2, :]
                    if n < 2:
                        pe.wait_ge(sm_ready, LEAD + 8 * i + n - 1)
                    else:
                        pe.wait_ge(evac, LEAD + 8 * i + n - 1)
                    half = slice(n % 2 * 512, (n % 2 + 1) * 512)
                    if n // 2 == 3:
                        for t in range(4):
                            tok = slice((n % 2 * 4 + t) * P, (n % 2 * 4 + t + 1) * P)
                            for k in range(KD):
                                mm = pe.matmul(bank[:, t * P:(t + 1) * P], c.xT[:, k, tok], wv[:, k, :], start=(k == 0), stop=(k == KD - 1))
                    else:
                        cols = slice(n // 2 * P, (n // 2 + 1) * P)
                        mm = split_product(pe, bank, lambda k: wh[:, k, cols], lambda k: wl[:, k, cols],
                                           lambda k: c.xTh[:, k, half], lambda k: c.xTl[:, k, half], range(KD))
                    mm.then_inc(proj_ps, 1)

                def scores(s):
                    b, r = s // 2, s % 2 * HD1
                    if s == 0:
                        pe.wait_ge(evac, LEAD + 8 * i + 7)
                    elif s == 1:
                        pe.wait_ge(evac, LEAD + 8 * i + 8)
                    else:
                        pe.wait_ge(sm_ready, LEAD + 8 * i + s - 1)
                    bank = ps[:, 4 + s % 2, :]
                    rows = slice(r, r + HD1)
                    pe.matmul(bank[:, 0:SEQ], k_T[rows, b * SEQ:b * SEQ + P], q_T[rows, b * SEQ:(b + 1) * SEQ], start=True, stop=True)
                    pe.matmul(bank[:, SEQ:CAUSAL], k_T[rows, b * SEQ + P:(b + 1) * SEQ], q_T[rows, b * SEQ + P:(b + 1) * SEQ],
                              start=True, stop=True).then_inc(s_ps, 1)

                def values(b):
                    pe.wait_ge(sm_ready, LEAD + 8 * i + 2 * b + 2)
                    pe.wait_ge(sq_ready, LEAD + BATCH * i + b - 1)
                    outs = [ps[r:r + HD1, 6 + b % 2, 0:SEQ] for r in (0, HD1)]
                    for n, out in enumerate(outs):
                        pe.matmul(out, v[:, TPB * b, n * HD1:(n + 1) * HD1], s_m[:, (2 * b + n) % 4, 0:SEQ], start=True, stop=False)
                    for n, out in enumerate(outs):
                        mm = pe.matmul(out[:, P:SEQ], v[:, TPB * b + 1, n * HD1:(n + 1) * HD1], s_m[:, (2 * b + n) % 4, SEQ:CAUSAL],
                                       start=False, stop=True)
                    mm.then_inc(pv_ps, 1)

                def project(b):
                    pe.wait_ge(og_ready, LEAD + BATCH * i + b + 1)
                    for t in range(TPB):
                        mm = pe.matmul(ps[:, b, t * D:(t + 1) * D], gated[:, b, t * P:(t + 1) * P], wo[:, bass.ds(i, 1), :].rearrange("p a d -> p (a d)"),
                                       start=False, stop=False, skip_group_check=True)
                    mm.then_inc(op_ps, 1)

                for step in range(BATCH + 2):
                    if step < BATCH:
                        scores(2 * step)
                        scores(2 * step + 1)
                    if 1 <= step <= BATCH:
                        values(step - 1)
                    if step >= 2:
                        project(step - 2)
            pe.wait_ge(sq_added, LEAD + BATCH * PAIRS)
            for t in range(NT):
                mm = pe.matmul(ps[:, 4, t:t + 1], sq_sum[:, t * P:(t + 1) * P], ones[:], start=True, stop=True)
            mm.then_inc(ss_ps, 1)


class GroupedWeights:

    def __init__(self, c, ctx):
        def sb(name, shape, dt=F32):
            return c.tile(ctx, "e_" + name, shape, dt)

        self.stage = sb("stage", [P, 1 + GROUP, KD, P])
        self.wh = sb("wh", [P, 1 + GROUP, KD, P], F32R)
        self.wl = sb("wl", [P, 1 + GROUP, KD, P], F32R)
        self.wv = sb("wv", [P, KD, HKV * P])
        self.wvh = sb("wvh", [P, KD, HKV * P], F32R)
        self.wvl = sb("wvl", [P, KD, HKV * P], F32R)
        self.rope = sb("rope", [P, 4, 512])
        self.wo = sb("wo", [P, HQ, D])
        self.loaded, self.hi = c.sems(ctx, "e", "loaded hi")
        self.c = c

    def load(self, sp):
        dram = self.c.dram
        for tile, source in ((self.stage, dram["w_grouped"][0]), (self.wv, dram["wv_grouped"]), (self.rope, dram["rope"]), (self.wo, dram["wo_grouped"])):
            sp.dma_start(tile[:], source).then_inc(self.loaded, 16)

    def split(self, eng):
        eng.wait_ge(self.loaded, 64)
        eng.tensor_copy(self.wh[:], self.stage[:]).then_inc(self.hi, 1)
        eng.tensor_copy(self.wvh[:], self.wv[:]).then_inc(self.hi, 1)
        eng.wait_ge(self.hi, 2)
        eng.tensor_tensor(self.wl[:], self.stage[:], self.wh[:].bitcast(F32), ALU.subtract)
        eng.tensor_tensor(self.wvl[:], self.wv[:], self.wvh[:].bitcast(F32), ALU.subtract)


def layer1_grouped_attention(c, pre):
    nc, ps = c.nc, c.ps
    PIECES = 1 + GROUP
    with ExitStack() as ctx:
        def sb(name, shape, dt=F32):
            return c.tile(ctx, "e_" + name, shape, dt)

        stage, wh, wl, rope, wo = pre.stage, pre.wh, pre.wl, pre.rope, pre.wo
        v_all = sb("v_all", [P, NT, HKV * P])
        k_T = sb("k_T", [P, TOK])
        v = sb("v", [P, NT, P])
        q_T = sb("q_T", [P, 2, TOK])
        by_cos = sb("by_cos", [P, 2, 512])
        by_sin = sb("by_sin", [P, 2, 512])
        neg_max = sb("neg_max", [P, 4, 2])
        sums = sb("sums", [P, 4, 2])
        rsum = sb("rsum", [P, 4, 2])
        probs = sb("probs", [P, 4, CAUSAL])
        probsT = sb("probsT", [P, 2, CAUSAL])
        o_T = sb("o_T", [P, 2, SEQ])
        zeros = sb("zeros", [P, 512])

        stage_in, zeroed = c.sems(ctx, "e", "stage_in zeroed")
        pe_sems = proj_ps, v_ps, s_ps, t_ps, pv_ps, wo_ps = c.sems(ctx, "e", "proj_ps v_ps s_ps t_ps pv_ps wo_ps")
        dve_sems = w_hi, w_split, turned_ps, nm_ready, rs_ready, v_copied, pT_ready = c.sems(
            ctx, "e", "w_hi w_split turned_ps nm_ready rs_ready v_copied pT_ready")
        act_sems = v_ready, p_ready, oT_ready = c.sems(ctx, "e", "v_ready p_ready oT_ready")
        pool_sems = roped, pn_ready = c.sems(ctx, "e", "roped pn_ready")
        block = ctx.enter_context(nc.Block())
        ITEMS = GROUP * BATCH

        ring = []
        for t in range(ITEMS):
            ring.append(("s", t))
            if t % 4 in (1, 2):
                ring.append(("q", 2 * (t // 4 + 1) + t % 4 - 1))
        ring += [("k", 0), ("k", 1)]
        at = {key: n for n, key in enumerate(ring)}
        order = [r for r in ring if r[0] != "s"]
        first = [("k", 1), ("k", 0), ("q", 2 * GROUP), ("q", 2 * GROUP + 1)]
        project_at = {t: ("q", 2 * (t // 4 + 1) + t % 4 - 1) for t in range(ITEMS) if t % 4 in (1, 2)}
        project_at |= {ITEMS: ("k", 0), ITEMS + 1: ("k", 1)}
        split_at = {3: 0, 4: 1, 7: 2, 8: 3, 11: 4}

        def projected(g, key):
            return LEAD + len(first) + len(order) * g + order.index(key) + 1

        def freed(eng, g, key):
            n = at[key] - 2
            last, g = ring[n % len(ring)], g - 1 if n < 0 else g
            if last[0] == "s":
                eng.wait_ge(p_ready, LEAD + 2 * (ITEMS * g + last[1] + 1))
            else:
                eng.wait_ge(turned_ps, projected(g, last))

        def half_of(key):
            return slice(key[1] % 2 * 512, (key[1] % 2 + 1) * 512)

        @block.sync
        def _(sp):
            with sp.Fori(0, HKV) as g:
                sp.wait_ge(w_split, LEAD + PIECES * g)
                sp.dma_start(stage[:].rearrange("p a k n -> p (a k) n"),
                             c.dram["w_grouped"][bass.ds(g + 1, 1)].rearrange("b p a k n -> p (b a k) n")).then_inc(stage_in, 16)

        @block.gpsimd
        def _(pool):
            give_lead(pool, pool_sems)
            pool.memset(zeros[:], 0.0).then_inc(zeroed, 1)

            def rotate(key, count, slot):
                pool.wait_ge(turned_ps, count)
                dst = k_T[:, half_of(key)] if key[0] == "k" else q_T[:, key[1] // 2 % 2, half_of(key)]
                pool.tensor_tensor(dst, by_cos[:, slot, :], by_sin[:, slot, :], ALU.add).then_inc(roped, 1)

            for n, key in enumerate(first):
                rotate(key, LEAD + n + 1, n % 2)
            with pool.Fori(0, HKV) as g:
                for t in range(ITEMS + 2):
                    if 1 <= t <= ITEMS:
                        u = t - 1
                        pool.wait_ge(rs_ready, LEAD + ITEMS * g + u + 1)
                        pool.tensor_tensor(probs[:, u % 4, 0:P], probs[:, u % 4, 0:P], rsum[:, u % 4, 0:1].broadcast_to((P, P)), ALU.mult).then_inc(pn_ready, 1)
                        pool.tensor_tensor(probs[:, u % 4, P:CAUSAL], probs[:, u % 4, P:CAUSAL], rsum[:, u % 4, 1:2].broadcast_to((P, SEQ)), ALU.mult).then_inc(pn_ready, 1)
                    if t in project_at:
                        key = project_at[t]
                        if key == ("k", 0):
                            pool.wait_ge(s_ps, LEAD + ITEMS * g + ITEMS)
                        rotate(key, projected(g, key), order.index(key) % 2)

        @block.vector
        def _(dve):
            give_lead(dve, dve_sems)

            def rotate(key, count, slot, bank):
                dve.wait_ge(proj_ps, count)
                dve.wait_ge(roped, count - 2)
                cos, sin = (rope[:, 0], rope[:, 1]) if key[0] == "k" else (rope[:, 2], rope[:, 3])
                dve.tensor_tensor(by_cos[:, slot, :], bank, cos, ALU.mult)
                dve.tensor_tensor(by_sin[0:HDQ // 2, slot, :], bank[HDQ // 2:P], sin[HDQ // 2:P], ALU.mult)
                dve.tensor_tensor(by_sin[HDQ // 2:P, slot, :], bank[0:HDQ // 2], sin[0:HDQ // 2], ALU.mult).then_inc(turned_ps, 1)

            for n, key in enumerate(first):
                rotate(key, LEAD + n + 1, n % 2, ps[:, 4 + at[key] % 2, :])
            dve.wait_ge(v_ready, NT + LEAD)
            with dve.Fori(0, HKV) as g:
                for t in range(ITEMS + 2):
                    if t < ITEMS:
                        dve.wait_ge(s_ps, LEAD + ITEMS * g + t + 1)
                        dve.wait_ge(p_ready, LEAD + 2 * (ITEMS * g + t) - 6)
                        bank = ps[:, 4 + at["s", t] % 2, :]
                        dve.tensor_reduce(neg_max[:, t % 4, 0:1], bank[:, 0:P], X, ALU.max, negate=True).then_inc(nm_ready, 1)
                        dve.tensor_reduce(neg_max[:, t % 4, 1:2], bank[:, P:CAUSAL], X, ALU.max, negate=True).then_inc(nm_ready, 1)
                    if t == 0:
                        dve.wait_ge(pv_ps, LEAD + ITEMS * g)
                        dve.tensor_scalar(v[:], v_all[:, :, bass.ds(g * P, P)], 1.0, None, ALU.mult).then_inc(v_copied, 1)
                    if 1 <= t <= ITEMS:
                        u = t - 1
                        dve.wait_ge(p_ready, LEAD + 2 * (ITEMS * g + u) + 2)
                        dve.wait_ge(pn_ready, LEAD + 2 * (ITEMS * g + u) - 6)
                        dve.reciprocal(rsum[:, u % 4, :], sums[:, u % 4, :]).then_inc(rs_ready, 1)
                    if t in project_at:
                        key = project_at[t]
                        rotate(key, projected(g, key), order.index(key) % 2, ps[:, 4 + at[key] % 2, :])
                    if t >= 2:
                        u = t - 2
                        dve.wait_ge(t_ps, LEAD + ITEMS * g + u + 1)
                        dve.wait_ge(pv_ps, LEAD + ITEMS * g + u - 1)
                        dve.tensor_copy(probsT[:, u % 2, :], ps[:, 6, 0:CAUSAL]).then_inc(pT_ready, 1)
                    if t in split_at:
                        piece = split_at[t]
                        dve.wait_ge(stage_in, 16 * g + 16)
                        dve.tensor_copy(wh[:, piece], stage[:, piece]).then_inc(w_hi, 1)
                        dve.wait_ge(w_hi, LEAD + PIECES * g + piece + 1)
                        dve.tensor_tensor(wl[:, piece], stage[:, piece], wh[:, piece].bitcast(F32), ALU.subtract).then_inc(w_split, 1)
            dve.wait_ge(wo_ps, LEAD + HKV * ITEMS)
            for bank in range(4):
                dve.tensor_tensor(c.y[:, 2 * bank:2 * bank + 2, :], ps[:, bank, :].rearrange("p (t d) -> p t d", t=2),
                                  c.x[:, 2 * bank:2 * bank + 2, :], ALU.add)

        @block.scalar
        def _(act):
            give_lead(act, act_sems)
            for t in range(NT):
                act.wait_ge(v_ps, LEAD + t + 1)
                act.activation(v_all[:, t, :], ps[:, 6 + t % 2, :], ACT.Copy).then_inc(v_ready, 1)
            with act.Fori(0, HKV) as g:
                for t in range(ITEMS + 3):
                    if t < ITEMS:
                        act.wait_ge(nm_ready, LEAD + 2 * (ITEMS * g + t) + 2)
                        act.wait_ge(t_ps, LEAD + ITEMS * g + t - 3)
                        bank = ps[:, 4 + at["s", t] % 2, :]
                        for b, cols in enumerate((slice(0, P), slice(P, CAUSAL))):
                            act.activation(probs[:, t % 4, cols], bank[:, cols], ACT.Exp, bias=neg_max[:, t % 4, b:b + 1],
                                           accum_out=sums[:, t % 4, b:b + 1]).then_inc(p_ready, 1)
                    if t >= 3:
                        u = t - 3
                        act.wait_ge(pv_ps, LEAD + ITEMS * g + u + 1)
                        act.wait_ge(wo_ps, LEAD + ITEMS * g + u - 1)
                        act.activation(o_T[:, u % 2, :], ps[:, 7, 0:SEQ], ACT.Copy).then_inc(oT_ready, 1)

        @block.tensor
        def _(pe):
            give_lead(pe, pe_sems)

            def project(key):
                piece = 0 if key[0] == "k" else 1 + key[1] // 2 % GROUP
                half = half_of(key)
                split_product(pe, ps[:, 4 + at[key] % 2, :], lambda k: wh[:, piece, k, :], lambda k: wl[:, piece, k, :],
                              lambda k: c.xTh[:, k, half], lambda k: c.xTl[:, k, half], range(KD)).then_inc(proj_ps, 1)

            def project_v(t):
                if t >= 2:
                    pe.wait_ge(v_ready, LEAD + t - 1)
                tok = slice(t * P, (t + 1) * P)
                split_product(pe, ps[:, 6 + t % 2, :], lambda k: c.xTh[:, k, tok], lambda k: c.xTl[:, k, tok],
                              lambda k: pre.wvh[:, k, :], lambda k: pre.wvl[:, k, :], range(KD)).then_inc(v_ps, 1)

            project(first[0])
            project(first[1])
            for t in range(2):
                project_v(t)
            pe.wait_ge(zeroed, 1)
            for bank in range(4):
                pe.matmul(ps[:, bank, :], zeros[:, 0:P], zeros[:], start=True, stop=False, skip_group_check=True)
            pe.wait_ge(turned_ps, LEAD + 2)
            project(first[2])
            for t in range(2, 4):
                project_v(t)
            pe.wait_ge(turned_ps, LEAD + 3)
            project(first[3])
            for t in range(4, NT):
                project_v(t)
            pe.wait_ge(v_ready, LEAD + NT)
            with pe.Fori(0, HKV) as g:
                for t in range(ITEMS + 4):
                    if t < ITEMS:
                        b = t % 4
                        if b == 0:
                            pe.wait_ge(roped, LEAD + len(first) + len(order) * g + 2 * (t // 4))
                        freed(pe, g, ("s", t))
                        bank, q = ps[:, 4 + at["s", t] % 2, :], q_T[:, t // 4 % 2, b * SEQ:(b + 1) * SEQ]
                        keys = k_T[:, b * SEQ:(b + 1) * SEQ]
                        pe.matmul(bank[:, 0:CAUSAL], c.ident16[:], c.neg16[:], start=True, stop=False)
                        pe.matmul(bank[:, 0:P], q[:, 0:P], keys[:, 0:P], start=False, stop=False)
                        pe.matmul(bank[:, P:CAUSAL], q[:, P:SEQ], keys, start=False, stop=True).then_inc(s_ps, 1)
                    if t in project_at:
                        key = project_at[t]
                        pe.wait_ge(w_split, LEAD + PIECES * g + (2 if t >= 4 * (GROUP - 1) else 0))
                        freed(pe, g, key)
                        project(key)
                    if t >= 4:
                        u = t - 4
                        pe.wait_ge(oT_ready, LEAD + ITEMS * g + u + 1)
                        for h in range(TPB):
                            mm = pe.matmul(ps[:, u % 4, h * D:(h + 1) * D], o_T[:, u % 2, h * P:(h + 1) * P],
                                           wo[:, bass.ds(g * GROUP + u // 4, 1), :].rearrange("p a d -> p (a d)"),
                                           start=False, stop=False, skip_group_check=True)
                        mm.then_inc(wo_ps, 1)
                    if 2 <= t < ITEMS + 2:
                        u = t - 2
                        pe.wait_ge(pn_ready, LEAD + 2 * (ITEMS * g + u) + 2)
                        pe.wait_ge(pT_ready, LEAD + ITEMS * g + u)
                        for n in range(3):
                            mm = pe.transpose(ps[:, 6, n * P:(n + 1) * P], probs[:, u % 4, n * P:(n + 1) * P], c.ident)
                        mm.then_inc(t_ps, 1)
                    if 3 <= t < ITEMS + 3:
                        u, b = t - 3, (t - 3) % 4
                        if u == 0:
                            pe.wait_ge(v_copied, LEAD + g + 1)
                        pe.wait_ge(pT_ready, LEAD + ITEMS * g + u + 1)
                        pe.wait_ge(oT_ready, LEAD + ITEMS * g + u)
                        out, s = ps[:, 7, 0:SEQ], probsT[:, u % 2, :]
                        pe.matmul(out, v[:, TPB * b, :], s[:, 0:SEQ], start=True, stop=False)
                        pe.matmul(out[:, P:SEQ], v[:, TPB * b + 1, :], s[:, SEQ:CAUSAL], start=False, stop=True).then_inc(pv_ps, 1)


def layer1_experts(c):
    nc, ps = c.nc, c.ps
    W1, W3, W2, WC = 0, KD * FF, 2 * KD * FF, 3 * KD * FF
    FT = FF // P
    with ExitStack() as ctx:
        def sb(name, shape, dt=F32):
            return c.tile(ctx, "f_" + name, shape, dt)

        stage = sb("stage", [P, WC])
        wh = [sb(f"wh{n}", [P, WC], F32R) for n in range(2)]
        wl = [sb(f"wl{n}", [P, WC], F32R) for n in range(2)]
        wg = sb("wg", [P, KD, EXPERTS])
        wgh = sb("wgh", [P, KD, EXPERTS], F32R)
        wgl = sb("wgl", [P, KD, EXPERTS], F32R)
        lg = sb("lg", [P, 8, NT, EXPERTS])
        gs = sb("gs", [P, 8, NT])
        weight = sb("weight", [P, EXPERTS, NT])
        act1 = sb("act1", [P, 2, 512])
        hid = sb("hid", [P, 2, 512])
        hidh = sb("hidh", [P, 2, FT, 512], F32R)
        hidl = sb("hidl", [P, 2, FT, 512], F32R)

        loaded, stage_in = c.sems(ctx, "f", "loaded stage_in")
        pe_sems = lg_ps, a_ps, b_ps, o_ps = c.sems(ctx, "f", "lg_ps a_ps b_ps o_ps")
        dve_sems = w_split, g_split, chain, d_ready, w_ready, h_ready, lo_ready, acc = c.sems(ctx, "f", "w_split g_split chain d_ready w_ready h_ready lo_ready acc")
        act_sems = w_hi, ex_ready, silu_ready, hi_ready = c.sems(ctx, "f", "w_hi ex_ready silu_ready hi_ready")
        block = ctx.enter_context(nc.Block())
        STEPS = 2 * 2 * FT

        @block.sync
        def _(sp):
            sp.dma_start(wg[:], c.dram["w_router"]).then_inc(loaded, 16)
            sp.dma_start(stage[:], c.dram["w_experts"][0]).then_inc(stage_in, 16)
            with sp.Fori(0, EXPERTS) as e:
                sp.wait_ge(w_split, LEAD + e + 1)
                sp.dma_start(stage[:], c.dram["w_experts"][bass.ds(e + 1, 1)].rearrange("a p n -> p (a n)")).then_inc(stage_in, 16)

        @block.vector
        def _(dve):
            give_lead(dve, dve_sems)
            dve.wait_ge(loaded, 16)
            link = Chain(dve, chain, LEAD)
            link(dve.tensor_copy(wgh[:], wg[:]))
            dve.tensor_tensor(wgl[:], wg[:], wgh[:].bitcast(F32), ALU.subtract).then_inc(g_split, 1)

            def split(slot, e):
                dve.wait_ge(w_hi, LEAD + e + 1)
                dve.tensor_tensor(wl[slot][:], stage[:], wh[slot][:].bitcast(F32), ALU.subtract).then_inc(w_split, 1)

            split(0, 0)
            logits, eq, cand, hot1, rest, hot2, w_1, w_2 = (lg[:, n] for n in range(8))
            m1, m2, first, diff, ex, den, p1, p2 = (gs[:, n] for n in range(8))

            def wide(a):
                return a.unsqueeze(2).broadcast_to((P, NT, EXPERTS))

            iota = c.iota[:, 0:EXPERTS].unsqueeze(1).broadcast_to((P, NT, EXPERTS))
            dve.wait_ge(lg_ps, LEAD + 1)
            link(dve.tensor_copy(logits.rearrange("p t e -> p (t e)"), ps[:, 0, 0:NT * EXPERTS]))

            def best(values, largest, hot):
                link(dve.tensor_reduce(largest, values, X, ALU.max))
                link(dve.tensor_tensor(eq, values, wide(largest), ALU.is_equal))
                link(dve.scalar_tensor_tensor(cand, eq, -16.0, iota, ALU.mult, ALU.add))
                link(dve.tensor_reduce(first, cand, X, ALU.min))
                link(dve.tensor_tensor(hot, cand, wide(first), ALU.is_equal))

            best(logits, m1, hot1)
            link(dve.scalar_tensor_tensor(rest, hot1, -1e30, logits, ALU.mult, ALU.add))
            best(rest, m2, hot2)
            dve.tensor_tensor(diff, m2, m1, ALU.subtract).then_inc(d_ready, 1)
            dve.wait_ge(ex_ready, LEAD + 1)
            link(dve.tensor_scalar(den, ex, 1.0, None, ALU.add))
            link(dve.reciprocal(p1, den))
            link(dve.tensor_tensor(p2, p1, ex, ALU.mult))
            link(dve.tensor_tensor(w_1, hot1, wide(p1), ALU.mult))
            link(dve.tensor_tensor(w_2, hot2, wide(p2), ALU.mult))
            dve.tensor_tensor(weight[:].rearrange("p e t -> p t e"), w_1, w_2, ALU.add).then_inc(w_ready, 1)
            for t in range(NT):
                dve.tensor_tensor(c.y[:, t, :], c.y[:, t, :], c.x[:, t, :], ALU.add).then_inc(acc, 1)
            dve.wait_ge(w_ready, LEAD + 1)
            with dve.Fori(0, EXPERTS // 2) as i:
                def down(s):
                    for t in range(4):
                        n = 4 * s + t
                        tok = s % 2 * 4 + t
                        dve.wait_ge(o_ps, LEAD + 16 * i + n + 1)
                        dve.wait_ge(acc, LEAD + NT + 16 * i + n - 7)
                        dve.scalar_tensor_tensor(c.y[:, tok, :], ps[:, 6 + n % 2, 0:D], weight[:, bass.ds(2 * i + s // 2, 1), tok:tok + 1].rearrange("p a b -> p (a b)"),
                                                 c.y[:, tok, :], ALU.mult, ALU.add).then_inc(acc, 1)

                for n in range(STEPS):
                    s, f = n // FT, n % FT
                    dve.wait_ge(b_ps, LEAD + STEPS * i + n + 1)
                    dve.wait_ge(silu_ready, LEAD + STEPS * i + n + 1)
                    dve.wait_ge(hi_ready, LEAD + STEPS * i + n - 1)
                    dve.tensor_tensor(hid[:, n % 2, :], act1[:, n % 2, :], ps[:, 4 + n % 2, :], ALU.mult).then_inc(h_ready, 1)
                    dve.wait_ge(hi_ready, LEAD + STEPS * i + n + 1)
                    dve.tensor_tensor(hidl[:, s % 2, f, :], hid[:, n % 2, :], hidh[:, s % 2, f, :].bitcast(F32), ALU.subtract).then_inc(lo_ready, 1)
                    if s >= 1 and f == FT - 1:
                        down(s - 1)
                    if n == 1:
                        split(1, 2 * i + 1)
                    if n == 2 * FT + FT:
                        split(0, 2 * i + 2)
                down(3)

        @block.scalar
        def _(act):
            give_lead(act, act_sems)

            def high(slot, staged):
                act.wait_ge(stage_in, staged)
                act.activation(wh[slot][:], stage[:], ACT.Copy).then_inc(w_hi, 1)

            high(0, 16)
            act.wait_ge(d_ready, LEAD + 1)
            act.activation(gs[:, 4], gs[:, 3], ACT.Exp).then_inc(ex_ready, 1)
            with act.Fori(0, EXPERTS // 2) as i:
                for n in range(STEPS):
                    s, f = n // FT, n % FT
                    if n == 1:
                        act.wait_ge(o_ps, LEAD + 16 * i)
                        high(1, 32 * i + 32)
                    if n == 2 * FT + FT:
                        act.wait_ge(o_ps, LEAD + 16 * i + 8)
                        high(0, 32 * i + 48)
                    act.wait_ge(a_ps, LEAD + STEPS * i + n + 1)
                    act.wait_ge(h_ready, LEAD + STEPS * i + n - 1)
                    act.activation(act1[:, n % 2, :], ps[:, 2 + n % 2, :], ACT.Silu).then_inc(silu_ready, 1)
                    act.wait_ge(h_ready, LEAD + STEPS * i + n + 1)
                    act.wait_ge(o_ps, LEAD + 16 * i + 4 * s - 4)
                    act.activation(hidh[:, s % 2, f, :], hid[:, n % 2, :], ACT.Copy).then_inc(hi_ready, 1)

        @block.tensor
        def _(pe):
            give_lead(pe, pe_sems)
            pe.wait_ge(g_split, LEAD + 1)
            for t in range(NT):
                tok = slice(t * P, (t + 1) * P)
                mm = split_product(pe, ps[:, 0, t * EXPERTS:(t + 1) * EXPERTS], lambda k: c.xTh[:, k, tok], lambda k: c.xTl[:, k, tok],
                                   lambda k: wgh[:, k, :], lambda k: wgl[:, k, :], range(KD))
            mm.then_inc(lg_ps, 1)
            with pe.Fori(0, EXPERTS // 2) as i:
                def up(s):
                    e, half = s // 2, slice(s % 2 * 512, (s % 2 + 1) * 512)
                    if s % 2 == 0:
                        pe.wait_ge(w_split, LEAD + 2 * i + e + 1)
                    for f in range(FT):
                        n = FT * s + f
                        for base, bank, used, done in ((W1, 2, silu_ready, a_ps), (W3, 4, h_ready, b_ps)):
                            pe.wait_ge(used, LEAD + STEPS * i + n - 1)
                            at = [slice(base + k * FF + f * P, base + k * FF + (f + 1) * P) for k in range(KD)]
                            split_product(pe, ps[:, bank + n % 2, :], lambda k: wh[e][:, at[k]], lambda k: wl[e][:, at[k]],
                                          lambda k: c.xTh[:, k, half], lambda k: c.xTl[:, k, half], range(KD)).then_inc(done, 1)

                def down(s):
                    e = s // 2
                    pe.wait_ge(lo_ready, LEAD + STEPS * i + FT * (s + 1))
                    for t in range(4):
                        n = 4 * s + t
                        pe.wait_ge(acc, LEAD + NT + 16 * i + n - 1)
                        split_product(pe, ps[:, 6 + n % 2, 0:D], lambda f: hidh[:, s % 2, f, t * P:(t + 1) * P],
                                      lambda f: hidl[:, s % 2, f, t * P:(t + 1) * P],
                                      lambda f: wh[e][:, W2 + f * D:W2 + (f + 1) * D], lambda f: wl[e][:, W2 + f * D:W2 + (f + 1) * D],
                                      range(FT)).then_inc(o_ps, 1)

                for s in range(4):
                    up(s)
                    if s >= 1:
                        down(s - 1)
                down(3)


def build(nc, dram, out):
    with ExitStack() as ctx:
        c = Core(nc, dram, out, ctx)
        layer0_linear_attention(c)
        normalise(c, "n1", c.y, c.x, turned="split")
        layer0_gated_attention(c)
        normalise(c, "n2", c.y, c.x, turned="both")
        with ExitStack() as held:
            grouped = GroupedWeights(c, held)
            layer1_decay_attention(c, grouped)
            normalise(c, "n3", c.y, c.x)
            normalise(c, "n4", c.x, c.scratch, rms=True, turned="split", weight=dram["norm1"])
            layer1_grouped_attention(c, grouped)
        normalise(c, "n5", c.y, c.scratch, rms=True, turned="split", weight=dram["norm2"])
        layer1_experts(c)
        normalise(c, "n6", c.y, c.x, store=True)


def blocks(wT):
    return np.ascontiguousarray(wT.reshape(wT.shape[0] // P, P, wT.shape[1]).transpose(1, 0, 2))


def constants():
    ident = np.eye(P)
    key, q = np.mgrid[0:P, 0:P]
    tri = (q >= key).astype(np.float32)
    tri3 = np.concatenate([tri, np.ones((P, P)), tri], axis=1)
    neg = np.where(key <= q, 0.0, -1e30).T
    neg3 = np.concatenate([neg, np.zeros((P, P)), neg], axis=1)
    par = np.stack([(np.arange(P) // HD0 % 2 == n) * float(HD0) ** -0.5 for n in range(2)], axis=1)
    iota = np.tile(np.arange(16.0), (P, 1))
    return np.concatenate([ident, tri3, neg3, par, iota], axis=1).astype(np.float32)


def rope_tables():
    inv = (1.0 / np.float32(1000000.0) ** (np.arange(0, HDQ, 2, dtype=np.float32) / HDQ)).astype(np.float32)
    ang = np.arange(SEQ, dtype=np.float32)[:, None] * inv[None, :]
    cos = np.concatenate([np.cos(ang), np.cos(ang)], axis=1).T
    sin = np.concatenate([np.sin(ang), -np.sin(ang)], axis=1).T
    cos, sin = np.tile(cos, (1, 2)), np.tile(sin, (1, 2))
    r = float(HDQ) ** -0.5
    return np.stack([cos, sin, cos * r, sin * r], axis=1).astype(np.float32)


def decays():
    factor = 1.0 - 0 / (32 - 1 + 1e-05) + 1e-05
    slope = (2.0 ** (-8.0 / H1)) ** (np.arange(H1) + 1.0) * factor
    dist = np.arange(SEQ)[None, :] - np.arange(P)[:, None]
    d = np.where(dist >= 0, np.exp(-slope[:, None, None] * np.maximum(dist, 0)), 0.0)
    d = np.concatenate([d, d[:, :, 0:P]], axis=2)
    return d.reshape(PAIRS, 2, P, CAUSAL).transpose(0, 2, 1, 3).astype(np.float32)


def padded(steps):
    return np.stack(steps + [np.zeros_like(steps[0])])


def kernel(**inputs):
    import concourse.bacc as bacc
    from concourse.bass_utils import run_bass_kernel_spmd

    a = {k: np.asarray(v) for k, v in inputs.items()}
    x = a["L0_attn_x"].reshape(TOK, D)
    diag = np.zeros((P, 4, P), np.float32)
    for n, name in enumerate(("fq1", "fq2", "fk1", "fk2")):
        for h in range(P // HD0):
            s = slice(h * HD0, (h + 1) * HD0)
            diag[s, n, s] = a[f"L0_attn_{name}_w"].T
    arrays = {
        "consts": constants(),
        "x": blocks(x),
        "xT": blocks(x.T),
        "w0": np.stack([blocks(a[f"L0_attn_{n}"].T) for n in ("wq", "wk", "wv")], axis=1),
        "maps": diag,
        "vecs": np.stack([np.tile(a[f"L0_attn_{n}"], P // HD0) for n in ("fq1_b", "fq2_b", "fk1_b", "fk2_b", "norm_w")], axis=1),
        "wo0": blocks(a["L0_attn_wo"].T),
        "w_gated": blocks(np.concatenate([a["L0_ffn_W_qkv"], a["L0_ffn_W_gate"]], axis=0).T),
    }
    qkv = a["L1_attn_qkv_w"].reshape(PAIRS, 2, 3, HD1, D).transpose(0, 2, 1, 3, 4).reshape(PAIRS, 3 * P, D)
    qk, v = qkv[:, :2 * P], qkv[:, 2 * P:]
    gates = a["L1_attn_gate_w"].reshape(PAIRS, P, D)
    wq, wk, wv = (a[f"L1_ffn_{n}"] for n in ("wq", "wk", "wv"))
    w1, w3, w2 = (a[f"L1_ffn_{n}"] for n in ("w1", "w3", "w2"))

    def head(w, h):
        return blocks(w[:, h * HDQ:(h + 1) * HDQ])

    arrays |= {
        "w_decay": padded([blocks(np.concatenate([qk[i], gates[i], v[i]], axis=0).T) for i in range(PAIRS)]),
        "decay": decays(),
        "wo_decay": blocks(a["L1_attn_out_w"].T),
        "norm_decay": a["L1_attn_norm_w"].reshape(PAIRS, P).T,
        "norm1": a["L1_ffn_norm1_w"].reshape(KD, P).T,
        "norm2": a["L1_ffn_norm2_w"].reshape(KD, P).T,
        "w_grouped": padded([np.stack([head(wk, g)] + [head(wq, GROUP * g + j) for j in range(GROUP)], axis=1) for g in range(HKV)]),
        "wv_grouped": blocks(wv),
        "wo_grouped": blocks(a["L1_ffn_wo"]),
        "rope": rope_tables(),
        "w_router": blocks(a["L1_ffn_gate_w"]),
        "w_experts": padded([np.concatenate([blocks(w[e]).reshape(P, -1) for w in (w1, w3, w2)], axis=1) for e in range(EXPERTS)]),
    }
    nc = bacc.Bacc("TRN2", target_bir_lowering=False, num_devices=1)
    dram = {}
    for name in arrays:
        arrays[name] = np.ascontiguousarray(arrays[name])
        dram[name] = nc.dram_tensor("in_" + name, arrays[name].shape, mybir.dt.from_np(arrays[name].dtype), kind="ExternalInput").ap()
    out = nc.dram_tensor("out", (TOK, D), F32, kind="ExternalOutput").ap()
    build(nc, dram, out.rearrange("(t p) d -> p t d", p=P))
    r = run_bass_kernel_spmd(nc, [{"in_" + k: v for k, v in arrays.items()}], core_ids=[0])
    return r.results[0]["out"].reshape(BATCH, SEQ, D)
```

```python
from contextlib import ExitStack

import numpy as np

import concourse.bass as bass
from concourse import mybir

F32 = mybir.dt.float32
F32R = mybir.dt.float32r
BF16 = mybir.dt.bfloat16
ALU = mybir.AluOpType
ACT = mybir.ActivationFunctionType
X = mybir.AxisListType.X

P = 128
LEAD = 8
EPS = 1e-5
BATCH, SEQ, D = 4, 256, 256
TOK = BATCH * SEQ
NT = TOK // P
KD = D // P
TPB = SEQ // P
CAUSAL = 384

H0, HD0 = 16, 16
H1, HD1 = 32, 64
PAIRS = H1 // 2
HQ, HKV, HDQ = 16, 4, 128
GROUP = HQ // HKV
EXPERTS, FF = 8, 512

C_IDENT = 0
C_TRI = C_IDENT + P
C_NEG = C_TRI + CAUSAL
C_PAR = C_NEG + CAUSAL
C_IOTA = C_PAR + 2
C_END = C_IOTA + 16


class Core:

    def __init__(self, nc, dram, out, ctx):
        self.nc, self.dram, self.out, self.ctx = nc, dram, out, ctx
        self.ps = ctx.enter_context(nc.psum_tensor("ps", [P, 8, 512], F32))
        self.norm_sems, self.norm_counts = None, dict.fromkeys(
            "w_in stat_done mean_done var_ready sd_ready rstd_ready n_ready turn_ps hi_ready lo_ready stored".split(), 0)
        self.consts = self.tile(ctx, "consts", [P, C_END])
        self.ident = self.consts[:, C_IDENT:C_IDENT + P]
        self.tri = self.consts[:, C_TRI:C_TRI + CAUSAL]
        self.parity = self.consts[:, C_PAR:C_PAR + 2]
        self.iota = self.consts[:, C_IOTA:C_IOTA + 16]
        self.ident16 = self.tile(ctx, "ident16", [P, P], BF16)
        self.neg16 = self.tile(ctx, "neg16", [P, CAUSAL], BF16)
        self.warm16 = self.tile(ctx, "warm16", [P, 512], BF16)
        self.x = self.tile(ctx, "x", [P, NT, D])
        self.y = self.tile(ctx, "y", [P, NT, D])
        self.scratch = self.tile(ctx, "scratch", [P, NT, D])
        self.w_gated = self.tile(ctx, "w_gated", [P, KD, 3 * D + H0])
        self.wh_gated = self.tile(ctx, "wh_gated", [P, KD, 3 * D + H0], F32R)
        self.wl_gated = self.tile(ctx, "wl_gated", [P, KD, 3 * D + H0], F32R)
        self.xT = self.tile(ctx, "xT", [P, KD, TOK])
        self.xTh = self.tile(ctx, "xTh", [P, KD, TOK], F32R)
        self.xTl = self.tile(ctx, "xTl", [P, KD, TOK], F32R)

    def tile(self, ctx, name, shape, dt=F32):
        return ctx.enter_context(self.nc.sbuf_tensor(name, shape, dt))

    def sems(self, ctx, prefix, names):
        return [self.ctx.enter_context(self.nc.semaphore(f"{prefix}_{n}")) for n in names.split()]


def give_lead(eng, sems):
    for s in sems:
        eng.sem_inc(s, LEAD)


class Chain:

    def __init__(self, eng, sem, base=0):
        self.eng, self.sem, self.base, self.n = eng, sem, base, 0

    def __call__(self, ins):
        self.n += 1
        ins.then_inc(self.sem, 1)
        self.eng.wait_ge(self.sem, self.base + self.n)


def split_product(pe, out, wh, wl, xh, xl, ks):
    passes = [(wh, xl), (wl, xh), (wh, xh)]
    n = 0
    for k in ks:
        for w, x in passes:
            mm = pe.matmul(out, w(k), x(k), start=(n == 0), stop=(n == 3 * len(ks) - 1))
            n += 1
    return mm


def keep_warm(c, pe, out, n):
    for _ in range(n):
        pe.matmul(out, c.warm16[:, 0:P], c.warm16[:, 0:out.shape[1]], start=True, stop=True)


def layer0_linear_attention(c):
    nc, ps = c.nc, c.ps
    SLOTS = 2
    QUADS = 4
    PAD = 32
    with ExitStack() as ctx:
        def sb(name, shape, dt=F32):
            return c.tile(ctx, "a_" + name, shape, dt)

        w = sb("w", [P, 3, KD, D])
        wh = sb("wh", [P, 3, KD, D], F32R)
        wl = sb("wl", [P, 3, KD, D], F32R)
        maps = sb("maps", [P, 4, P])
        vecs = sb("vecs", [P, 5])
        wo = sb("wo", [P, KD, D])
        q_all = sb("q_all", [P, KD, TOK])
        k_all = sb("k_all", [P, KD, TOK])
        v_all = sb("v_all", [P, NT, D])
        v_pad = sb("v_pad", [P, SLOTS, TPB, H0, PAD])
        second = sb("second", [P, 3, KD, SEQ])
        q_par = sb("q_par", [P, 2, KD, SEQ])
        k_map = sb("k_map", [P, KD, SEQ])
        q_rows = sb("q_rows", [P, 8, KD, SEQ])
        s_m = sb("s_m", [P, 8, CAUSAL])
        o_sb = sb("o_sb", [P, 2, 512])
        o_sq = sb("o_sq", [P, TPB, D])
        o_n = sb("o_n", [P, TPB, D])
        o_nT = sb("o_nT", [P, KD, SEQ])
        stat = sb("stat", [P, 4, TPB * H0])
        par_bias = sb("par_bias", [P, 2])

        x_in, x_in_2, w_in, loaded = c.sems(ctx, "a", "x_in x_in_2 w_in loaded")
        pe_sems = p_ps, map_ps, s_ps, pv_ps, o_turned, on_turned, wo_ps = c.sems(ctx, "a", "p_ps map_ps s_ps pv_ps o_turned on_turned wo_ps")
        dve_sems = x_split, w_hi, w_split, v_copied, qmap_ready, kmap_ready, sm_ready, sum_ready, var_ready, r_ready, on_ready, oT_ready, y_ready, bias_ready = c.sems(
            ctx, "a", "x_split w_hi w_split v_copied qmap_ready kmap_ready sm_ready sum_ready var_ready r_ready on_ready oT_ready y_ready bias_ready")
        act_sems = x_hi, p_ready, qrows_ready, second_q, second_k, o_ready, sq_ready, sd_ready = c.sems(
            ctx, "a", "x_hi p_ready qrows_ready second_q second_k o_ready sq_ready sd_ready")
        zeroed, next_in, next_hi = c.sems(ctx, "a", "zeroed next_in next_hi")
        block = ctx.enter_context(nc.Block())

        @block.sync
        def _(sp):
            for n in range(2):
                half = slice(n * 512, (n + 1) * 512)
                sp.dma_start(c.xT[:, :, half], c.dram["xT"][:, :, half]).then_inc((x_in, x_in_2)[n], 16)
                if n == 0:
                    sp.dma_start(w[:], c.dram["w0"]).then_inc(w_in, 16)
            sp.dma_start(maps[:], c.dram["maps"]).then_inc(loaded, 16)
            sp.dma_start(vecs[:], c.dram["vecs"]).then_inc(loaded, 16)
            sp.dma_start(c.consts[:], c.dram["consts"]).then_inc(loaded, 16)
            sp.dma_start(wo[:], c.dram["wo0"]).then_inc(loaded, 16)
            sp.dma_start(c.x[:], c.dram["x"]).then_inc(loaded, 16)
            sp.dma_start(c.w_gated[:], c.dram["w_gated"]).then_inc(next_in, 16)

        @block.gpsimd
        def _(pool):
            pool.memset(c.warm16[:], 0.0).then_inc(zeroed, 1)
            pool.memset(v_pad[:], 0.0).then_inc(zeroed, 1)
            pool.memset(q_rows[:], 0.0).then_inc(zeroed, 1)
            pool.wait_ge(next_in, 16)
            pool.tensor_copy(c.wh_gated[:], c.w_gated[:]).then_inc(next_hi, 1)
            pool.wait_ge(next_hi, 1)
            pool.tensor_tensor(c.wl_gated[:], c.w_gated[:], c.wh_gated[:].bitcast(F32), ALU.subtract)

        @block.vector
        def _(dve):
            give_lead(dve, dve_sems)
            def low(n):
                half = slice(n * 512, (n + 1) * 512)
                dve.wait_ge(x_hi, LEAD + n + 1)
                dve.tensor_tensor(c.xTl[:, :, half], c.xT[:, :, half], c.xTh[:, :, half].bitcast(F32), ALU.subtract).then_inc(x_split, 1)

            low(0)
            dve.wait_ge(w_in, 16)
            for n in range(3):
                dve.tensor_copy(wh[:, n], w[:, n]).then_inc(w_hi, 1)
                dve.wait_ge(w_hi, LEAD + n + 1)
                dve.tensor_tensor(wl[:, n], w[:, n], wh[:, n].bitcast(F32), ALU.subtract).then_inc(w_split, 1)
                if n == 1:
                    low(1)
            dve.wait_ge(loaded, 16 * 5)
            for par in range(2):
                dve.tensor_tensor(par_bias[:, par:par + 1], vecs[:, 1:2], c.parity[:, par:par + 1], ALU.mult).then_inc(bias_ready, 1)
            dve.tensor_copy(c.ident16[:], c.ident)
            dve.tensor_copy(c.neg16[:], c.consts[:, C_NEG:C_NEG + CAUSAL])
            dve.wait_ge(p_ready, LEAD + 12)
            dve.wait_ge(zeroed, 2)
            with dve.Fori(0, BATCH // SLOTS) as i:
                def at(u):
                    return SLOTS * i + u

                def prepare(u):
                    dve.wait_ge(pv_ps, LEAD + QUADS * (SLOTS * i + u) - QUADS * SLOTS + QUADS)
                    dve.tensor_scalar(v_pad[:, u].rearrange("p t h r -> p (t h) r")[:, :, 0:HD0],
                                      v_all[:, bass.ds(at(u) * TPB, TPB), :].rearrange("p t (h d) -> p (t h) d", h=H0), 1.0, None, ALU.mult).then_inc(v_copied, 1)
                    dve.wait_ge(map_ps, LEAD + 2 * at(u) + 1)
                    for par in range(2):
                        dve.wait_ge(second_q, LEAD + 2 * at(u) + par + 1)
                        dve.wait_ge(qrows_ready, LEAD + 4 * at(u))
                        dve.scalar_tensor_tensor(q_par[:, par].rearrange("p k s -> p (k s)"), ps[:, 3, :], vecs[:, 0:1],
                                                 second[:, par].rearrange("p k s -> p (k s)"), ALU.add, ALU.mult).then_inc(qmap_ready, 1)
                    dve.wait_ge(map_ps, LEAD + 2 * at(u) + 2)
                    dve.wait_ge(second_k, LEAD + at(u) + 1)
                    dve.scalar_tensor_tensor(k_map[:].rearrange("p k s -> p (k s)"), ps[:, 5, :], vecs[:, 2:3],
                                             second[:, 2].rearrange("p k s -> p (k s)"), ALU.add, ALU.mult).then_inc(kmap_ready, 1)

                def masks(u, quad):
                    for h in range(4 * quad, 4 * quad + 4):
                        dve.wait_ge(s_ps, LEAD + H0 * at(u) + h + 1)
                        dve.wait_ge(pv_ps, LEAD + QUADS * at(u) + quad - 1)
                        dve.tensor_tensor(s_m[:, h % 8, :], ps[:, 3 + h % 4, 0:CAUSAL], c.tri, ALU.mult).then_inc(sm_ready, 1)

                def moments(u):
                    dve.wait_ge(sq_ready, LEAD + TPB * (at(u) + 1))
                    dve.tensor_reduce(stat[:, 0, :], o_sq[:].rearrange("p t (h d) -> p (t h) d", h=H0), X, ALU.add).then_inc(sum_ready, 1)
                    dve.wait_ge(sum_ready, LEAD + at(u) + 1)
                    dve.tensor_scalar(stat[:, 1, :], stat[:, 0, :], 1.0 / HD0, EPS, ALU.mult, ALU.add).then_inc(var_ready, 1)

                def scale(u):
                    dve.wait_ge(sd_ready, LEAD + at(u) + 1)
                    dve.reciprocal(stat[:, 3, :], stat[:, 2, :]).then_inc(r_ready, 1)
                    dve.wait_ge(r_ready, LEAD + at(u) + 1)
                    for t in range(TPB):
                        dve.tensor_tensor(o_n[:, t, :].rearrange("p (h d) -> p h d", h=H0), ps[:, 1 + t, :].rearrange("p (h r) -> p h r", h=H0)[:, :, 0:HD0],
                                          stat[:, 3, t * H0:(t + 1) * H0].unsqueeze(2).broadcast_to((P, H0, HD0)), ALU.mult).then_inc(on_ready, 1)

                def weigh(u):
                    dve.wait_ge(on_turned, LEAD + at(u) + 1)
                    dve.tensor_scalar(o_nT[:].rearrange("p k s -> p (k s)"), ps[:, 1, :], vecs[:, 4:5], None, ALU.mult).then_inc(oT_ready, 1)

                def add(u):
                    dve.wait_ge(wo_ps, LEAD + at(u) + 1)
                    dve.tensor_tensor(c.y[:, bass.ds(at(u) * TPB, TPB), :], ps[:, 2, :].rearrange("p (t d) -> p t d", t=TPB),
                                      c.x[:, bass.ds(at(u) * TPB, TPB), :], ALU.add).then_inc(y_ready, 1)

                prepare(0)
                for quad in range(QUADS):
                    masks(0, quad)
                prepare(1)
                masks(1, 0)
                moments(0)
                masks(1, 1)
                scale(0)
                masks(1, 2)
                weigh(0)
                masks(1, 3)
                add(0)
                moments(1)
                scale(1)
                weigh(1)
                add(1)

        @block.scalar
        def _(act):
            give_lead(act, act_sems)
            for n in range(2):
                half = slice(n * 512, (n + 1) * 512)
                act.wait_ge((x_in, x_in_2)[n], 16)
                act.activation(c.xTh[:, :, half], c.xT[:, :, half], ACT.Copy).then_inc(x_hi, 1)
            for n in range(12):
                act.wait_ge(p_ps, LEAD + n + 1)
                if n < 8:
                    half, a, m = n // 4, n // 2 % 2, n % 2
                    dst = (q_all, k_all)[a][:, m, half * 512:(half + 1) * 512]
                else:
                    dst = v_all[:, 2 * (n - 8):2 * (n - 7), :].rearrange("p t d -> p (t d)")
                act.activation(dst, ps[:, n % 8, :], ACT.Copy).then_inc(p_ready, 1)
            act.wait_ge(bias_ready, LEAD + 2)
            act.wait_ge(zeroed, 3)
            with act.Fori(0, BATCH // SLOTS) as i:
                def prepare(u):
                    act.wait_ge(map_ps, LEAD + 2 * (SLOTS * i + u) + 1)
                    act.wait_ge(kmap_ready, LEAD + SLOTS * i + u)
                    for par in range(2):
                        act.activation(second[:, par].rearrange("p k s -> p (k s)"), ps[:, 4, :], ACT.Identity, bias=par_bias[:, par:par + 1],
                                       scale=c.parity[:, par:par + 1]).then_inc(second_q, 1)
                    act.wait_ge(map_ps, LEAD + 2 * (SLOTS * i + u) + 2)
                    act.activation(second[:, 2].rearrange("p k s -> p (k s)"), ps[:, 6, :], ACT.Identity, bias=vecs[:, 3:4]).then_inc(second_k, 1)
                    act.wait_ge(qmap_ready, LEAD + 2 * (SLOTS * i + u) + 2)
                    for g in range(4):
                        rows = slice(32 * g, 32 * g + 32)
                        act.activation(q_rows[rows, 2 * g:2 * g + 2].rearrange("p h k s -> p (h k s)"), q_par[rows].rearrange("p h k s -> p (h k s)"),
                                       ACT.Copy).then_inc(qrows_ready, 1)

                def outputs(u):
                    for half in range(2):
                        act.wait_ge(pv_ps, LEAD + QUADS * (SLOTS * i + u) + 2 * half + 2)
                        act.wait_ge(o_turned, LEAD + TPB * (SLOTS * i + u))
                        act.activation(o_sb[:, half, :], ps[:, 7 * half, :], ACT.Copy).then_inc(o_ready, 1)

                def squares(u):
                    for t in range(TPB):
                        act.wait_ge(o_turned, LEAD + TPB * (SLOTS * i + u) + t + 1)
                        act.wait_ge(sum_ready, LEAD + SLOTS * i + u)
                        act.activation(o_sq[:, t, :].rearrange("p (h d) -> p h d", h=H0), ps[:, 1 + t, :].rearrange("p (h r) -> p h r", h=H0)[:, :, 0:HD0],
                                       ACT.Square).then_inc(sq_ready, 1)

                def root(u):
                    act.wait_ge(var_ready, LEAD + SLOTS * i + u + 1)
                    act.activation(stat[:, 2, :], stat[:, 1, :], ACT.Sqrt).then_inc(sd_ready, 1)

                prepare(0)
                outputs(0)
                prepare(1)
                squares(0)
                root(0)
                outputs(1)
                squares(1)
                root(1)

        @block.tensor
        def _(pe):
            give_lead(pe, pe_sems)
            pe.wait_ge(zeroed, 1)
            keep_warm(c, pe, ps[:, 7, :], 20)
            for n in range(12):
                pe.wait_ge(w_split, LEAD + (n // 2 % 2 + 1 if n < 8 else 3))
                pe.wait_ge(x_split, LEAD + (1 if n < 4 else 2))
                if n >= 8:
                    pe.wait_ge(p_ready, LEAD + n - 7)
                if n < 8:
                    half, a, m = slice(n // 4 * 512, (n // 4 + 1) * 512), n // 2 % 2, n % 2
                    mm = split_product(pe, ps[:, n % 8, :], lambda k: wh[:, a, k, m * P:(m + 1) * P], lambda k: wl[:, a, k, m * P:(m + 1) * P],
                                       lambda k: c.xTh[:, k, half], lambda k: c.xTl[:, k, half], range(KD))
                else:
                    for t in range(2):
                        tok = slice((2 * (n - 8) + t) * P, (2 * (n - 8) + t + 1) * P)
                        mm = split_product(pe, ps[:, n % 8, t * D:(t + 1) * D], lambda k: c.xTh[:, k, tok], lambda k: c.xTl[:, k, tok],
                                           lambda k: wh[:, 2, k, :], lambda k: wl[:, 2, k, :], range(KD))
                mm.then_inc(p_ps, 1)
            pe.wait_ge(p_ready, LEAD + 8)
            keep_warm(c, pe, ps[:, 7, :], 8)
            pe.wait_ge(p_ready, LEAD + 12)
            pe.wait_ge(loaded, 16 * 5)
            with pe.Fori(0, BATCH // SLOTS) as i:
                def at(u):
                    return SLOTS * i + u

                def prepare(u):
                    pe.wait_ge(sm_ready, LEAD + H0 * at(u))
                    for n, raw in enumerate((q_all, k_all)):
                        for f in range(2):
                            for m in range(KD):
                                mm = pe.matmul(ps[:, 3 + 2 * n + f, m * SEQ:(m + 1) * SEQ], maps[:, 2 * n + f, :], raw[:, m, bass.ds(at(u) * SEQ, SEQ)],
                                               start=True, stop=True)
                        mm.then_inc(map_ps, 1)

                def scores(u, quad):
                    if quad == 0:
                        pe.wait_ge(kmap_ready, LEAD + at(u) + 1)
                    pe.wait_ge(qrows_ready, LEAD + 4 * at(u) + (2 if quad == 0 else 4))
                    for h in range(4 * quad, 4 * quad + 4):
                        m, q = h // 8, q_rows[:, h % 8, h // 8, :]
                        bank = ps[:, 3 + h % 4, :]
                        if h >= 4:
                            pe.wait_ge(sm_ready, LEAD + H0 * at(u) + h - 3)
                        pe.matmul(bank[:, 0:SEQ], k_map[:, m, 0:P], q, start=True, stop=True)
                        pe.matmul(bank[:, SEQ:CAUSAL], k_map[:, m, P:SEQ], q[:, P:SEQ], start=True, stop=True).then_inc(s_ps, 1)

                def values(u, quad):
                    if quad == 0:
                        pe.wait_ge(v_copied, LEAD + at(u) + 1)
                    if quad % 2 == 0:
                        pe.wait_ge(o_ready, LEAD + 2 * at(u) + quad // 2 - 1)
                    pe.wait_ge(sm_ready, LEAD + H0 * at(u) + 4 * quad + 4)
                    out = ps[:, 7 * (quad // 2), quad % 2 * SEQ:(quad % 2 + 1) * SEQ]
                    for q in range(4):
                        h = 4 * quad + q
                        pe.matmul(out[PAD * q:PAD * (q + 1), :], v_pad[:, u, 0, h, :], s_m[:, h % 8, 0:SEQ], start=True, stop=False)
                    for q in range(4):
                        h = 4 * quad + q
                        mm = pe.matmul(out[PAD * q:PAD * (q + 1), P:SEQ], v_pad[:, u, 1, h, :], s_m[:, h % 8, SEQ:CAUSAL], start=False, stop=True)
                    mm.then_inc(pv_ps, 1)

                def turn(u):
                    pe.wait_ge(o_ready, LEAD + 2 * at(u) + 2)
                    pe.wait_ge(y_ready, LEAD + at(u))
                    for t in range(TPB):
                        for j in range(4):
                            mm = pe.transpose(ps[:, 1 + t, j * P:(j + 1) * P], o_sb[:, j // 2, j % 2 * SEQ + t * P:j % 2 * SEQ + (t + 1) * P], c.ident)
                        mm.then_inc(o_turned, 1)

                def turn_back(u):
                    pe.wait_ge(on_ready, LEAD + TPB * (at(u) + 1))
                    for t in range(TPB):
                        for m in range(KD):
                            mm = pe.transpose(ps[:, 1, m * SEQ + t * P:m * SEQ + (t + 1) * P], o_n[:, t, m * P:(m + 1) * P], c.ident)
                    mm.then_inc(on_turned, 1)

                def project(u):
                    pe.wait_ge(oT_ready, LEAD + at(u) + 1)
                    for t in range(TPB):
                        for k in range(KD):
                            mm = pe.matmul(ps[:, 2, t * D:(t + 1) * D], o_nT[:, k, t * P:(t + 1) * P], wo[:, k, :], start=(k == 0), stop=(k == KD - 1))
                    mm.then_inc(wo_ps, 1)

                prepare(0)
                keep_warm(c, pe, ps[:, 7, :], 18)
                scores(0, 0)
                for quad in range(1, QUADS):
                    scores(0, quad)
                    values(0, quad - 1)
                prepare(1)
                values(0, QUADS - 1)
                turn(0)
                keep_warm(c, pe, ps[:, 7, :], 10)
                scores(1, 0)
                scores(1, 1)
                values(1, 0)
                scores(1, 2)
                turn_back(0)
                values(1, 1)
                scores(1, 3)
                values(1, 2)
                project(0)
                values(1, 3)
                turn(1)
                keep_warm(c, pe, ps[:, 7, :], 16)
                turn_back(1)
                keep_warm(c, pe, ps[:, 7, :], 5)
                project(1)


def normalise(c, tag, src, dst, rms=False, turned=None, weight=None, store=False, following=None, rms_too=None):
    nc, ps = c.nc, c.ps
    with ExitStack() as ctx:
        def sb(name, shape, dt=F32):
            return c.tile(ctx, f"{tag}_{name}", shape, dt)

        stats = sb("stats", [P, NT, 6])
        mv = sb("mv", [P, NT, 2])
        var = sb("var", [P, NT])
        sd = sb("sd", [P, NT])
        rstd = sb("rstd", [P, NT])
        rstd2 = sb("rstd2", [P, NT])
        shift = sb("shift", [P, NT])
        junk = sb("junk", [P, D])
        wcol = sb("wcol", [P, KD])
        names = "w_in stat_done mean_done var_ready sd_ready rstd_ready n_ready turn_ps hi_ready lo_ready stored"
        if not c.norm_sems:
            c.norm_sems = c.sems(ctx, "norm", names)
        w_in, stat_done, mean_done, var_ready, sd_ready, rstd_ready, n_ready, turn_ps, hi_ready, lo_ready, stored = c.norm_sems
        so = dict(c.norm_counts)
        block = ctx.enter_context(nc.Block())

        @block.gpsimd
        def _(pool):
            if following:
                following.prepare(pool)

        @block.sync
        def _(sp):
            if weight is not None:
                sp.dma_start(wcol[:], weight).then_inc(w_in, 16)
            if following:
                following.load(sp)
            if store:
                for t in range(NT):
                    sp.wait_ge(n_ready, so["n_ready"] + t + 1)
                    sp.dma_start(c.out[:, t, :], dst[:, t, :]).then_inc(stored, 16)
                sp.wait_ge(stored, so["stored"] + 16 * NT)

        @block.vector
        def _(dve):
            if rms:
                dve.wait_ge(stat_done, so["stat_done"] + NT)
                dve.tensor_scalar(var[:], sd[:], 1.0 / D, EPS, ALU.mult, ALU.add).then_inc(var_ready, 1)
            else:
                for t in range(NT):
                    dve.bn_stats(stats[:, t, :], src[:, t, :]).then_inc(stat_done, 1)
                dve.wait_ge(stat_done, so["stat_done"] + NT)
                for t in range(NT):
                    dve.bn_aggr(mv[:, t, :], stats[:, t, :]).then_inc(mean_done, 1)
                dve.wait_ge(mean_done, so["mean_done"] + NT)
                dve.tensor_scalar(var[:], mv[:, :, 1], EPS, None, ALU.add).then_inc(var_ready, 1)
            dve.wait_ge(sd_ready, so["sd_ready"] + 1)
            dve.reciprocal(rstd[:], sd[:]).then_inc(rstd_ready, 1)
            dve.wait_ge(rstd_ready, so["rstd_ready"] + 1)
            if rms_too is not None:
                dve.scalar_tensor_tensor(shift[:], mv[:, :, 0], -1.0, rstd[:], ALU.mult, ALU.mult)
                dve.tensor_tensor(rstd2[:], rstd[:], rstd[:], ALU.mult).then_inc(rstd_ready, 1)
                dve.wait_ge(rstd_ready, so["rstd_ready"] + 2)
                dve.tensor_tensor(var[:], mv[:, :, 1], rstd2[:], ALU.mult).then_inc(rstd_ready, 1)
                dve.wait_ge(rstd_ready, so["rstd_ready"] + 3)
                dve.tensor_scalar(rstd2[:], var[:], EPS, None, ALU.add).then_inc(var_ready, 1)
                dve.wait_ge(sd_ready, so["sd_ready"] + 2)
                dve.reciprocal(rstd2[:], sd[:]).then_inc(rstd_ready, 1)
                dve.wait_ge(rstd_ready, so["rstd_ready"] + 4)
                dve.tensor_tensor(var[:], rstd[:], rstd2[:], ALU.mult).then_inc(rstd_ready, 1)
                dve.wait_ge(rstd_ready, so["rstd_ready"] + 5)
                for t in range(NT):
                    dve.tensor_scalar(rms_too[:, t, :], src[:, t, :], mv[:, t, 0:1], var[:, t:t + 1], ALU.subtract, ALU.mult).then_inc(n_ready, 1)
            for t in range(NT if rms_too is None else 0):
                if rms:
                    dve.tensor_scalar(dst[:, t, :], src[:, t, :], rstd[:, t:t + 1], None, ALU.mult).then_inc(n_ready, 1)
                else:
                    dve.tensor_scalar(dst[:, t, :], src[:, t, :], mv[:, t, 0:1], rstd[:, t:t + 1], ALU.subtract, ALU.mult).then_inc(n_ready, 1)
            if turned in ("split", "both"):
                for n in range(4):
                    half, k = n // 2, n % 2
                    dve.wait_ge(hi_ready, so["hi_ready"] + n + 1)
                    cols = slice(half * 512, (half + 1) * 512)
                    if weight is None:
                        dve.tensor_tensor(c.xTl[:, k, cols], ps[:, n, :], c.xTh[:, k, cols].bitcast(F32), ALU.subtract).then_inc(lo_ready, 1)
                    else:
                        dve.scalar_tensor_tensor(c.xTl[:, k, cols], ps[:, n, :], wcol[:, k:k + 1], c.xTh[:, k, cols].bitcast(F32),
                                                 ALU.mult, ALU.subtract).then_inc(lo_ready, 1)

        @block.scalar
        def _(act):
            if rms:
                for t in range(NT):
                    if t >= 1:
                        act.wait_ge(stat_done, so["stat_done"] + t)
                    act.activation(junk[:], src[:, t, :], ACT.Square, accum_out=sd[:, t:t + 1]).then_inc(stat_done, 1)
            act.wait_ge(var_ready, so["var_ready"] + 1)
            act.activation(sd[:], var[:], ACT.Sqrt).then_inc(sd_ready, 1)
            if rms_too is not None:
                act.wait_ge(var_ready, so["var_ready"] + 2)
                act.activation(sd[:], rstd2[:], ACT.Sqrt).then_inc(sd_ready, 1)
                for t in range(NT):
                    act.activation(dst[:, t, :], src[:, t, :], ACT.Identity, scale=rstd[:, t:t + 1], bias=shift[:, t:t + 1])
            if weight is not None:
                act.wait_ge(w_in, so["w_in"] + 16)
            for n in range(4 if turned else 0):
                half, k = n // 2, n % 2
                act.wait_ge(turn_ps, so["turn_ps"] + n + 1)
                if turned == "both":
                    act.activation(c.xT[:, k, half * 512:(half + 1) * 512], ps[:, n, :], ACT.Copy)
                to = (c.xT if turned == "whole" else c.xTh)[:, k, half * 512:(half + 1) * 512]
                if weight is None:
                    act.activation(to, ps[:, n, :], ACT.Copy).then_inc(hi_ready, 1)
                else:
                    act.activation(to, ps[:, n, :], ACT.Copy, scale=wcol[:, k:k + 1]).then_inc(hi_ready, 1)

        @block.tensor
        def _(pe):
            if turned:
                keep_warm(c, pe, ps[:, 7, :], 20)
            for n in range(4 if turned else 0):
                half, k = n // 2, n % 2
                pe.wait_ge(n_ready, so["n_ready"] + 4 * half + 4)
                for t in range(4):
                    mm = pe.transpose(ps[:, n, t * P:(t + 1) * P], (dst if rms_too is None else rms_too)[:, 4 * half + t, k * P:(k + 1) * P], c.ident)
                mm.then_inc(turn_ps, 1)
            if turned:
                keep_warm(c, pe, ps[:, 7, :], 10)

        raised = {"stat_done": NT, "mean_done": 0 if rms else NT, "var_ready": 2 if rms_too is not None else 1,
                  "sd_ready": 2 if rms_too is not None else 1, "rstd_ready": 5 if rms_too is not None else 1,
                  "n_ready": NT,
                  "w_in": 16 if weight is not None else 0, "turn_ps": 4 if turned else 0, "hi_ready": 4 if turned else 0,
                  "lo_ready": 4 if turned in ("split", "both") else 0, "stored": 16 * NT if store else 0}
        c.norm_counts = {n: so[n] + raised[n] for n in raised}


def layer0_gated_attention(c, following):
    nc, ps = c.nc, c.ps
    QKV = 3 * D
    SLOTS = 2
    ITEMS = SLOTS * H0
    QUADS = ITEMS // 4
    PAD = 32
    with ExitStack() as ctx:
        def sb(name, shape, dt=F32):
            return c.tile(ctx, "g_" + name, shape, dt)

        wh, wl = c.wh_gated, c.wl_gated
        z_T = sb("z_T", [H0, TOK])
        gate = sb("gate", [P, 6, NT, H0])
        gstat = sb("gstat", [P, 6, NT])
        picked = sb("picked", [P, 2, H0, HD0])
        k_tok = sb("k_tok", [P, NT, HD0])
        v_pad = sb("v_pad", [P, NT, PAD])
        k_pad = c.scratch[:].rearrange("p t (a n) -> p t a n", a=2)
        k_rows = sb("k_rows", [P, 8, TOK])
        q_all = c.xT
        q_T = sb("q_T", [P, SLOTS, KD, SEQ])
        v_seq = sb("v_seq", [P, SLOTS, TPB, PAD])
        neg_max = sb("neg_max", [P, 4, 2])
        probs = sb("probs", [P, 4, CAUSAL])
        probsT = sb("probsT", [P, 8, CAUSAL])
        o_sb = sb("o_sb", [P, 2, 512])
        o_tok = sb("o_tok", [P, 2, H0, HD0])
        rsum = sb("rsum", [P, 2, H0])
        table = sb("table", [P, 1])

        pool_sems = (padded,) = c.sems(ctx, "g", "padded")
        pe_sems = z_ps, lg_ps, kv_ps, q_ps, kT_ps, s_ps, t_ps, pv_ps, o_turned = c.sems(
            ctx, "g", "z_ps lg_ps kv_ps q_ps kT_ps s_ps t_ps pv_ps o_turned")
        dve_sems = z_ready, picked_ps, k_ready, copied, nm_ready, pT_ready, rs_ready, o_scaled, kT_copied, chain = c.sems(
            ctx, "g", "z_ready picked_ps k_ready copied nm_ready pT_ready rs_ready o_scaled kT_copied chain")
        act_sems = z_copied, e_ready, q_ready, kT_ready, p_ready, o_ready = c.sems(ctx, "g", "z_copied e_ready q_ready kT_ready p_ready o_ready")
        block = ctx.enter_context(nc.Block())

        @block.sync
        def _(sp):
            following.load(sp)

        @block.gpsimd
        def _(pool):
            give_lead(pool, pool_sems)
            pool.memset(c.scratch[:], 0.0).then_inc(padded, 1)
            pool.memset(v_pad[:], 0.0).then_inc(padded, 1)
            pool.wait_ge(padded, LEAD + 2)
            pool.memset(v_pad[:, :, HD0:HD0 + 1], 1.0).then_inc(padded, 1)
            pool.memset(k_rows[:], 0.0).then_inc(padded, 1)
            following.prepare(pool)

        @block.vector
        def _(dve):
            give_lead(dve, dve_sems)
            link = Chain(dve, chain, LEAD)
            z, e, cand, one_hot, top_hot, eq = (gate[:, n] for n in range(6))
            nmax, esum, emax, erec, top, first = (gstat[:, n] for n in range(6))

            def wide(a):
                return a.unsqueeze(2).broadcast_to((P, NT, H0))

            dve.wait_ge(lg_ps, LEAD + 1)
            logits = ps[:, 0, 0:NT * H0].rearrange("p (t h) -> p t h", t=NT)
            link(dve.tensor_reduce(nmax, logits, X, ALU.max, negate=True))
            dve.tensor_tensor(z, logits, wide(nmax), ALU.add).then_inc(z_ready, 1)
            dve.wait_ge(e_ready, LEAD + 1)
            dve.tensor_reduce(esum, e, X, ALU.add)
            link(dve.tensor_reduce(emax, e, X, ALU.max))
            link(dve.reciprocal(erec, esum))
            dve.tensor_tensor(top, emax, erec, ALU.mult)
            link(dve.tensor_tensor(eq, e, wide(emax), ALU.is_equal))
            link(dve.scalar_tensor_tensor(cand, eq, -16.0, c.iota.unsqueeze(1).broadcast_to((P, NT, H0)), ALU.mult, ALU.add))
            link(dve.tensor_reduce(first, cand, X, ALU.min))
            link(dve.tensor_tensor(one_hot, cand, wide(first), ALU.is_equal))
            link(dve.tensor_tensor(top_hot, one_hot, wide(top), ALU.mult))
            dve.wait_ge(padded, LEAD + 3)
            for t in range(NT):
                dve.wait_ge(kv_ps, LEAD + t + 1)
                kv = ps[:, 5 + t % 3, :].rearrange("p (a h d) -> p a h d", a=2, h=H0)
                dve.tensor_tensor(picked[:, 0], kv[:, 0], one_hot[:, t, :].unsqueeze(2).broadcast_to((P, H0, HD0)), ALU.mult)
                dve.tensor_tensor(picked[:, 1], kv[:, 1], top_hot[:, t, :].unsqueeze(2).broadcast_to((P, H0, HD0)), ALU.mult).then_inc(picked_ps, 1)
                dve.wait_ge(picked_ps, LEAD + t + 1)
                dve.tensor_reduce(v_pad[:, t, 0:HD0], picked[:, 1].rearrange("p h d -> p d h"), X, ALU.add)
                link(dve.tensor_reduce(k_tok[:, t, :], picked[:, 0].rearrange("p h d -> p d h"), X, ALU.add))
                for par in range(2):
                    dst = k_pad[:, t, par, :].rearrange("p (g r) -> p g r", g=4)[:, :, par * HD0:(par + 1) * HD0]
                    dve.tensor_copy(dst, k_tok[:, t, :].unsqueeze(1).broadcast_to((P, 4, HD0))).then_inc(k_ready, 1)
            dve.wait_ge(padded, LEAD + 4)
            for n in range(4):
                half, par = n // 2, n % 2
                dve.wait_ge(kT_ps, LEAD + n + 1)
                for g in range(2, 4) if half else ():
                    rows = slice(32 * g, 32 * g + 32)
                    dve.tensor_copy(k_rows[rows, 2 * g + par, half * 512:(half + 1) * 512], ps[rows, 1 + n, :]).then_inc(kT_copied, 1)
            with dve.Fori(0, BATCH // SLOTS) as i:
                dve.wait_ge(pv_ps, LEAD + QUADS * i)
                for u in range(SLOTS):
                    s = SLOTS * i + u
                    dve.tensor_scalar(q_T[:, u], q_all[:, :, bass.ds(s * SEQ, SEQ)], 1.0, None, ALU.mult)
                    dve.tensor_scalar(v_seq[:, u], v_pad[:, bass.ds(s * TPB, TPB), :], 1.0, None, ALU.mult).then_inc(copied, 1)
                for n in range(ITEMS + 9):
                    if n < ITEMS:
                        dve.wait_ge(s_ps, LEAD + ITEMS * i + n + 1)
                        dve.wait_ge(p_ready, LEAD + ITEMS * i + n - 3)
                        dve.tensor_reduce(neg_max[:, n % 4, 0:1], ps[:, n % 3, 0:P], X, ALU.max, negate=True)
                        dve.tensor_reduce(neg_max[:, n % 4, 1:2], ps[:, n % 3, P:CAUSAL], X, ALU.max, negate=True).then_inc(nm_ready, 1)
                    m = n - 3
                    if 0 <= m < ITEMS:
                        dve.wait_ge(t_ps, LEAD + ITEMS * i + m + 1)
                        dve.wait_ge(pv_ps, LEAD + QUADS * i + m // 4 - 1)
                        dve.tensor_copy(probsT[:, m % 8, :], ps[:, 3 + m % 2, 0:CAUSAL]).then_inc(pT_ready, 1)
                    for u in range(SLOTS):
                        for t, at in enumerate((22, 24)):
                            if n == H0 * u + at:
                                seq = TPB * (SLOTS * i + u) + t
                                turned = ps[:, 5, :].rearrange("p (h r) -> p h r", h=H0)
                                dve.wait_ge(o_turned, LEAD + seq + 1)
                                dve.reciprocal(rsum[:, t, :], turned[:, :, HD0]).then_inc(rs_ready, 1)
                                dve.wait_ge(rs_ready, LEAD + seq + 1)
                                dve.tensor_tensor(o_tok[:, t], turned[:, :, 0:HD0], rsum[:, t, :].unsqueeze(2).broadcast_to((P, H0, HD0)), ALU.mult).then_inc(o_scaled, 1)
                                dve.wait_ge(o_scaled, LEAD + seq + 1)
                                tile = bass.ds(seq, 1)
                                dve.tensor_tensor(c.y[:, tile, :], o_tok[:, t].rearrange("p h d -> p (h d)").unsqueeze(1), c.x[:, tile, :], ALU.add)

        @block.scalar
        def _(act):
            give_lead(act, act_sems)
            for n in range(2):
                act.wait_ge(z_ps, LEAD + n + 1)
                act.activation(z_T[:, n * 512:(n + 1) * 512], ps[0:H0, 5 + n, :], ACT.Copy).then_inc(z_copied, 1)
            act.wait_ge(z_ready, LEAD + 1)
            act.activation(gate[:, 1], gate[:, 0], ACT.Exp).then_inc(e_ready, 1)
            for n in range(4):
                act.wait_ge(q_ps, LEAD + n + 1)
                act.activation(q_all[:, n // 2, n % 2 * 512:(n % 2 + 1) * 512], ps[:, 1 + n, :], ACT.Copy, scale=float(HD0) ** -0.5).then_inc(q_ready, 1)
            act.wait_ge(padded, LEAD + 4)
            for n in range(4):
                half, par = n // 2, n % 2
                act.wait_ge(kT_ps, LEAD + n + 1)
                for g in range(2 if half else 4):
                    rows = slice(32 * g, 32 * g + 32)
                    act.activation(k_rows[rows, 2 * g + par, half * 512:(half + 1) * 512], ps[rows, 1 + n, :], ACT.Copy).then_inc(kT_ready, 1)
            with act.Fori(0, BATCH // SLOTS) as i:
                act.activation(table[:], c.iota[:, 0:1], ACT.Exp)
                for n in range(ITEMS + 5):
                    if n < ITEMS:
                        act.wait_ge(nm_ready, LEAD + ITEMS * i + n + 1)
                        act.wait_ge(t_ps, LEAD + ITEMS * i + n - 3)
                        for b, cols in enumerate((slice(0, P), slice(P, CAUSAL))):
                            ex = act.activation(probs[:, n % 4, cols], ps[:, n % 3, cols], ACT.Exp, bias=neg_max[:, n % 4, b:b + 1])
                        ex.then_inc(p_ready, 1)
                    for u in range(SLOTS):
                        for half, at in enumerate((12, 20)):
                            if n == H0 * u + at:
                                act.wait_ge(pv_ps, LEAD + QUADS * i + 4 * u + 2 * half + 2)
                                act.wait_ge(o_turned, LEAD + TPB * (SLOTS * i + u))
                                act.activation(o_sb[:, half, :], ps[:, 6 + half, :], ACT.Copy).then_inc(o_ready, 1)

        @block.tensor
        def _(pe):
            give_lead(pe, pe_sems)
            for n in range(2):
                half = slice(n * 512, (n + 1) * 512)
                split_product(pe, ps[0:H0, 5 + n, :], lambda k: wh[:, k, QKV:], lambda k: wl[:, k, QKV:],
                              lambda k: c.xTh[:, k, half], lambda k: c.xTl[:, k, half], range(KD)).then_inc(z_ps, 1)
            for n in range(4):
                if n == 1:
                    pe.wait_ge(z_copied, LEAD + 2)
                    for t in range(NT):
                        mm = pe.transpose(ps[:, 0, t * H0:(t + 1) * H0], z_T[:, t * P:(t + 1) * P], c.ident[0:H0, 0:H0])
                    mm.then_inc(lg_ps, 1)
                m, half = n // 2, slice(n % 2 * 512, (n % 2 + 1) * 512)
                split_product(pe, ps[:, 1 + n, :], lambda k: wh[:, k, m * P:(m + 1) * P], lambda k: wl[:, k, m * P:(m + 1) * P],
                              lambda k: c.xTh[:, k, half], lambda k: c.xTl[:, k, half], range(KD)).then_inc(q_ps, 1)
            for t in range(NT):
                tok = slice(t * P, (t + 1) * P)
                if t >= 3:
                    pe.wait_ge(picked_ps, LEAD + t - 2)
                split_product(pe, ps[:, 5 + t % 3, :], lambda k: c.xTh[:, k, tok], lambda k: c.xTl[:, k, tok],
                              lambda k: wh[:, k, D:QKV], lambda k: wl[:, k, D:QKV], range(KD)).then_inc(kv_ps, 1)
                if t >= NT - 2:
                    half = t - (NT - 2)
                    pe.wait_ge(q_ready, LEAD + 4)
                    if half:
                        keep_warm(c, pe, ps[:, 0, :], 20)
                    pe.wait_ge(k_ready, LEAD + NT * (half + 1))
                    for par in range(2):
                        for tile in range(4):
                            mm = pe.transpose(ps[:, 1 + 2 * half + par, tile * P:(tile + 1) * P], k_pad[:, 4 * half + tile, par, :], c.ident)
                        mm.then_inc(kT_ps, 1)
            keep_warm(c, pe, ps[:, 0, :], 8)
            pe.wait_ge(kT_ready, LEAD + 12)
            pe.wait_ge(kT_copied, LEAD + 4)
            pe.wait_ge(picked_ps, LEAD + NT)
            with pe.Fori(0, BATCH // SLOTS) as i:
                def scores(n):
                    u, h = n // H0, n % H0
                    m, rows = h // 8, k_rows[:, h % 8, :]
                    bank = ps[:, n % 3, :]
                    if h == 0:
                        pe.wait_ge(copied, LEAD + SLOTS * i + u + 1)
                    pe.wait_ge(p_ready, LEAD + ITEMS * i + (n - 2 if n >= 3 else 0))
                    pe.matmul(bank[:, 0:CAUSAL], c.ident16[:], c.neg16[:], start=True, stop=False)
                    pe.matmul(bank[:, 0:P], q_T[:, u, m, 0:P], rows[:, bass.ds((SLOTS * i + u) * SEQ, P)], start=False, stop=False)
                    pe.matmul(bank[:, P:CAUSAL], q_T[:, u, m, P:SEQ], rows[:, bass.ds((SLOTS * i + u) * SEQ, SEQ)], start=False, stop=True).then_inc(s_ps, 1)

                def turn(n):
                    pe.wait_ge(p_ready, LEAD + ITEMS * i + n + 1)
                    pe.wait_ge(pT_ready, LEAD + ITEMS * i + n - 1)
                    for b in range(3):
                        mm = pe.transpose(ps[:, 3 + n % 2, b * P:(b + 1) * P], probs[:, n % 4, b * P:(b + 1) * P], c.ident)
                    mm.then_inc(t_ps, 1)

                def values(quad):
                    u, j = quad // 4, quad % 4
                    pe.wait_ge(pT_ready, LEAD + ITEMS * i + 4 * quad + 4)
                    if j % 2 == 0:
                        pe.wait_ge(o_ready, LEAD + 2 * (SLOTS * i + u) + j // 2 - 1)
                    out = ps[:, 6 + j // 2, j % 2 * SEQ:(j % 2 + 1) * SEQ]
                    for q in range(4):
                        pe.matmul(out[PAD * q:PAD * (q + 1), :], v_seq[:, u, 0, :], probsT[:, (4 * quad + q) % 8, 0:SEQ], start=True, stop=False)
                    for q in range(4):
                        mm = pe.matmul(out[PAD * q:PAD * (q + 1), P:SEQ], v_seq[:, u, 1, :], probsT[:, (4 * quad + q) % 8, SEQ:CAUSAL],
                                       start=False, stop=True)
                    mm.then_inc(pv_ps, 1)

                def turn_outputs(u, t):
                    pe.wait_ge(o_ready, LEAD + 2 * (SLOTS * i + u) + 2)
                    pe.wait_ge(o_scaled, LEAD + TPB * (SLOTS * i + u) + t)
                    for j in range(4):
                        mm = pe.transpose(ps[:, 5, j * P:(j + 1) * P], o_sb[:, j // 2, j % 2 * SEQ + t * P:j % 2 * SEQ + (t + 1) * P], c.ident)
                    mm.then_inc(o_turned, 1)

                keep_warm(c, pe, ps[:, 2, :], 8)
                for n in range(ITEMS + 9):
                    if n < ITEMS:
                        scores(n)
                    if 2 <= n < ITEMS + 2:
                        turn(n - 2)
                    if n >= 7 and (n - 7) % 4 == 0 and (n - 7) // 4 < QUADS:
                        values((n - 7) // 4)
                    for u in range(SLOTS):
                        if n - H0 * u in (21, 23):
                            turn_outputs(u, (n - H0 * u - 21) // 2)


class DecayWeights:
    PROJ = KD * 4 * P

    def __init__(self, c, ctx):
        def sb(name, shape, dt=F32):
            return c.tile(ctx, "d_" + name, shape, dt)

        self.c = c
        self.stage = sb("stage", [P, self.PROJ + D + 1])
        self.wh = sb("wh", [P, KD, 3 * P], F32R)
        self.wl = sb("wl", [P, KD, 3 * P], F32R)
        self.wv = sb("wv", [P, KD, P])
        self.wo = sb("wo", [P, D])
        self.wo_hi = sb("wo_hi", [P, D], F32R)
        self.wo_lo = sb("wo_lo", [P, D], F32R)
        self.nought = sb("nought", [P, 1])
        self.loaded, self.zeroed, self.w_hi, self.w_split, self.wo_scaled, self.wo_high, self.wo_split = c.sems(
            ctx, "d", "loaded zeroed w_hi w_split wo_scaled wo_high wo_split")

    def load(self, sp):
        sp.dma_start(self.stage[:], self.c.dram["w_decay"][0]).then_inc(self.loaded, 16)

    def split(self, pool, n):
        nought = self.nought[:].unsqueeze(1)
        stage = self.stage[:, 0:self.PROJ].rearrange("p (k n) -> p k n", k=KD)
        pool.tensor_tensor(self.wh[:], stage[:, :, 0:3 * P], nought.broadcast_to((P, KD, 3 * P)), ALU.add).then_inc(self.w_hi, 1)
        pool.tensor_tensor(self.wv[:], stage[:, :, 3 * P:], nought.broadcast_to((P, KD, P)), ALU.add)
        pool.wait_ge(self.w_hi, n)
        pool.tensor_tensor(self.wl[:], stage[:, :, 0:3 * P], self.wh[:].bitcast(F32), ALU.subtract).then_inc(self.w_split, 1)

    def split_out(self, pool, n):
        norm_w = self.stage[:, self.PROJ + D:].broadcast_to((P, D))
        pool.tensor_tensor(self.wo[:], self.stage[:, self.PROJ:self.PROJ + D], norm_w, ALU.mult).then_inc(self.wo_scaled, 1)
        pool.wait_ge(self.wo_scaled, n)
        pool.tensor_tensor(self.wo_hi[:], self.wo[:], self.nought[:].broadcast_to((P, D)), ALU.add).then_inc(self.wo_high, 1)
        pool.wait_ge(self.wo_high, n)
        pool.tensor_tensor(self.wo_lo[:], self.wo[:], self.wo_hi[:].bitcast(F32), ALU.subtract).then_inc(self.wo_split, 1)

    def prepare(self, pool):
        pool.memset(self.nought[:], 0.0).then_inc(self.zeroed, 1)
        pool.wait_ge(self.zeroed, 1)
        pool.wait_ge(self.loaded, 16)
        self.split(pool, 1)
        self.split_out(pool, 1)


def layer1_decay_attention(c, pre, following):
    nc, ps = c.nc, c.ps
    with ExitStack() as ctx:
        def sb(name, shape, dt=F32):
            return c.tile(ctx, "d_" + name, shape, dt)

        stage, wh, wl, wv, w_split = pre.stage, pre.wh, pre.wl, pre.wv, pre.w_split
        gated_hi = sb("gated_hi", [P, BATCH, SEQ], F32R)
        gated_lo = sb("gated_lo", [P, BATCH, SEQ], F32R)
        q_hi, q_lo = (w[:].rearrange("p k n -> p (k n)")[:, 0:TOK] for w in (c.wh_gated, c.wl_gated))
        k_hi, k_lo = (w[:].rearrange("p k n -> p (k n)")[:, TOK:TOK + BATCH * P].rearrange("p (b n) -> p b n", b=BATCH) for w in (c.wh_gated, c.wl_gated))
        decay = sb("decay", [P, 2, CAUSAL])
        q_T = sb("q_T", [P, TOK])
        k_T = sb("k_T", [P, TOK])
        v = sb("v", [P, NT, P])
        gate = sb("gate", [P, TOK])
        s_m = sb("s_m", [P, 4, CAUSAL])
        sq = sb("sq", [P, 2, SEQ])
        sq_sum = sb("sq_sum", [P, TOK])
        gated = sb("gated", [P, BATCH, SEQ])
        ones = sb("ones", [P, 1])
        stat = sb("stat", [P, 3, NT])

        def first_keys(tile, half):
            return tile[:, half * 512:(half + 1) * 512].rearrange("p (b n) -> p b n", b=2)[:, :, 0:P]

        stage_in, decay_in = c.sems(ctx, "d", "stage_in decay_in")
        pe_sems = proj_ps, s_ps, pv_ps, op_ps = c.sems(ctx, "d", "proj_ps s_ps pv_ps op_ps")
        dve_sems = sm_ready, og_ready, qk_lo, out_lo = c.sems(ctx, "d", "sm_ready og_ready qk_lo out_lo")
        act_sems = evac, sq_ready, qk_hi, out_hi = c.sems(ctx, "d", "evac sq_ready qk_hi out_hi")
        pool_sems = (sq_added,) = c.sems(ctx, "d", "sq_added")
        zeroed, ss_ps, var_ready, sd_ready, rs_ready = c.sems(ctx, "d", "zeros ss_ps var_ready sd_ready rs_ready")
        block = ctx.enter_context(nc.Block())

        @block.sync
        def _(sp):
            sp.dma_start(decay[:], c.dram["decay"][0]).then_inc(decay_in, 16)
            sp.dma_start(stage[:], c.dram["w_decay"][1]).then_inc(stage_in, 16)
            with sp.Fori(0, PAIRS - 1) as i:
                sp.wait_ge(sm_ready, LEAD + 8 * i + 8)
                sp.dma_start(decay[:], c.dram["decay"][bass.ds(i + 1, 1)].rearrange("a p h s -> p (a h) s")).then_inc(decay_in, 16)
                sp.wait_ge(pre.wo_split, i + 2)
                sp.dma_start(stage[:], c.dram["w_decay"][bass.ds(i + 2, 1)].rearrange("a p n -> p (a n)")).then_inc(stage_in, 16)

        @block.gpsimd
        def _(pool):
            give_lead(pool, pool_sems)
            pool.memset(ones[:], 1.0).then_inc(zeroed, 1)
            pool.memset(sq_sum[:], 0.0).then_inc(zeroed, 1)
            pool.wait_ge(zeroed, 2)
            with pool.Fori(0, PAIRS) as i:
                pool.wait_ge(proj_ps, LEAD + 8 * i + 8)
                pool.wait_ge(stage_in, 16 * i + 16)
                pre.split(pool, i + 2)
                for b in range(BATCH):
                    pool.wait_ge(sq_ready, LEAD + BATCH * i + b + 1)
                    pool.wait_ge(sq_added, LEAD + BATCH * i + b - 3)
                    cols = slice(b * SEQ, (b + 1) * SEQ)
                    pool.tensor_tensor(sq_sum[:, cols], sq_sum[:, cols], sq[:, b % 2, :], ALU.add).then_inc(sq_added, 1)
                pool.wait_ge(op_ps, LEAD + BATCH * (i + 1))
                pre.split_out(pool, i + 2)

        @block.vector
        def _(dve):
            give_lead(dve, dve_sems)
            following.split(dve)
            with dve.Fori(0, PAIRS) as i:
                def gate_out(b):
                    dve.wait_ge(pv_ps, LEAD + BATCH * i + b + 1)
                    dve.wait_ge(op_ps, LEAD + BATCH * i + b - 3)
                    if b == 0:
                        dve.wait_ge(evac, LEAD + 8 * i + 8)
                    dve.scalar_tensor_tensor(gated[:, b, :], gate[:, b * SEQ:(b + 1) * SEQ], 1.0, ps[:, 6 + b % 2, 0:SEQ],
                                             ALU.add, ALU.mult).then_inc(og_ready, 1)

                def low_out(b):
                    dve.wait_ge(out_hi, LEAD + BATCH * i + b + 1)
                    dve.tensor_tensor(gated_lo[:, b, :], gated[:, b, :], gated_hi[:, b, :].bitcast(F32), ALU.subtract).then_inc(out_lo, 1)

                for n in range(4):
                    dve.wait_ge(qk_hi, LEAD + 4 * i + n + 1)
                    half = slice(n % 2 * 512, (n % 2 + 1) * 512)
                    if n < 2:
                        dve.tensor_tensor(q_lo[:, half], q_T[:, half], q_hi[:, half].bitcast(F32), ALU.subtract).then_inc(qk_lo, 1)
                    else:
                        two = slice(2 * (n - 2), 2 * (n - 1))
                        dve.tensor_tensor(k_lo[:, two, :], first_keys(k_T, n - 2), k_hi[:, two, :].bitcast(F32), ALU.subtract).then_inc(qk_lo, 1)
                dve.wait_ge(decay_in, 16 * i + 16)
                for s in range(8):
                    dve.wait_ge(s_ps, LEAD + 8 * i + s + 1)
                    dve.wait_ge(pv_ps, LEAD + BATCH * i + s // 2 - 1)
                    dve.tensor_tensor(s_m[:, s % 4, :], ps[:, 4 + s % 2, 0:CAUSAL], decay[:, s % 2, :], ALU.mult).then_inc(sm_ready, 1)
                    if s in (4, 6):
                        low_out((s - 4) // 2)
                    if s in (3, 5, 7):
                        gate_out((s - 3) // 2)
                low_out(2)
                gate_out(3)
                low_out(3)
            dve.wait_ge(ss_ps, 1)
            dve.tensor_scalar(stat[:, 0, :], ps[:, 4, 0:NT], 1.0 / (H1 * HD1), EPS, ALU.mult, ALU.add).then_inc(var_ready, 1)
            dve.wait_ge(sd_ready, 1)
            dve.reciprocal(stat[:, 2, :], stat[:, 1, :]).then_inc(rs_ready, 1)
            dve.wait_ge(rs_ready, 1)
            dve.tensor_scalar(stat[:, 0, :], stat[:, 2, :], 0.5, None, ALU.mult).then_inc(rs_ready, 1)
            dve.wait_ge(rs_ready, 2)
            for t in range(NT):
                dve.scalar_tensor_tensor(c.y[:, t, :], ps[:, t // 2, t % 2 * D:(t % 2 + 1) * D], stat[:, 0, t:t + 1], c.x[:, t, :], ALU.mult, ALU.add)

        @block.scalar
        def _(act):
            give_lead(act, act_sems)
            with act.Fori(0, PAIRS) as i:
                act.wait_ge(op_ps, LEAD + BATCH * i)
                for n in range(8):
                    act.wait_ge(proj_ps, LEAD + 8 * i + n + 1)
                    half = slice(n % 2 * 512, (n % 2 + 1) * 512)
                    bank = ps[:, 4 + n % 2, :]
                    if n < 4:
                        act.activation((q_T, k_T)[n // 2][:, half], bank, ACT.Silu).then_inc(evac, 1)
                        act.wait_ge(evac, LEAD + 8 * i + n + 1)
                        if n < 2:
                            act.activation(q_hi[:, half], q_T[:, half], ACT.Copy).then_inc(qk_hi, 1)
                        else:
                            act.activation(k_hi[:, 2 * (n - 2):2 * (n - 1), :], first_keys(k_T, n - 2), ACT.Copy).then_inc(qk_hi, 1)
                    elif n >= 6:
                        act.activation(v[:, n % 2 * 4:(n % 2 + 1) * 4, :].rearrange("p t d -> p (t d)"), bank, ACT.Silu).then_inc(evac, 1)
                    else:
                        if n == 4:
                            act.wait_ge(og_ready, LEAD + BATCH * i)
                        act.activation(gate[:, half], bank, ACT.Tanh, scale=0.5).then_inc(evac, 1)
                for b in range(BATCH):
                    act.wait_ge(og_ready, LEAD + BATCH * i + b + 1)
                    act.activation(gated_hi[:, b, :], gated[:, b, :], ACT.Copy).then_inc(out_hi, 1)
                    act.wait_ge(sq_added, LEAD + BATCH * i + b - 1)
                    act.activation(sq[:, b % 2, :], ps[:, 6 + b % 2, 0:SEQ], ACT.Square).then_inc(sq_ready, 1)
            act.wait_ge(var_ready, 1)
            act.activation(stat[:, 1, :], stat[:, 0, :], ACT.Sqrt).then_inc(sd_ready, 1)

        @block.tensor
        def _(pe):
            give_lead(pe, pe_sems)
            for bank in range(4):
                pe.matmul(ps[:, bank, :], c.warm16[:, 0:P], c.warm16[:], start=True, stop=False, skip_group_check=True)
            with pe.Fori(0, PAIRS) as i:
                pe.wait_ge(w_split, i + 1)
                for n in range(8):
                    bank = ps[:, 4 + n % 2, :]
                    if n < 2:
                        pe.wait_ge(sm_ready, LEAD + 8 * i + n - 1)
                    else:
                        pe.wait_ge(evac, LEAD + 8 * i + n - 1)
                    half = slice(n % 2 * 512, (n % 2 + 1) * 512)
                    if n // 2 == 3:
                        for t in range(4):
                            tok = slice((n % 2 * 4 + t) * P, (n % 2 * 4 + t + 1) * P)
                            for k in range(KD):
                                mm = pe.matmul(bank[:, t * P:(t + 1) * P], c.xT[:, k, tok], wv[:, k, :], start=(k == 0), stop=(k == KD - 1))
                    else:
                        cols = slice(n // 2 * P, (n // 2 + 1) * P)
                        mm = split_product(pe, bank, lambda k: wh[:, k, cols], lambda k: wl[:, k, cols],
                                           lambda k: c.xTh[:, k, half], lambda k: c.xTl[:, k, half], range(KD))
                    mm.then_inc(proj_ps, 1)

                def scores(s):
                    b, r = s // 2, s % 2 * HD1
                    if s == 0:
                        pe.wait_ge(evac, LEAD + 8 * i + 7)
                    elif s == 1:
                        pe.wait_ge(evac, LEAD + 8 * i + 8)
                    else:
                        pe.wait_ge(sm_ready, LEAD + 8 * i + s - 1)
                    bank = ps[:, 4 + s % 2, :]
                    rows = slice(r, r + HD1)
                    if s == 0:
                        pe.wait_ge(qk_lo, LEAD + 4 * i + 4)
                    queries = slice(b * SEQ, (b + 1) * SEQ)
                    for n, (k, q) in enumerate(((k_hi, q_lo), (k_lo, q_hi), (k_hi, q_hi))):
                        pe.matmul(bank[:, 0:SEQ], k[rows, b, :], q[rows, queries], start=(n == 0), stop=(n == 2))
                    pe.matmul(bank[:, SEQ:CAUSAL], k_T[rows, b * SEQ + P:(b + 1) * SEQ], q_T[rows, b * SEQ + P:(b + 1) * SEQ],
                              start=True, stop=True).then_inc(s_ps, 1)

                def values(b):
                    pe.wait_ge(sm_ready, LEAD + 8 * i + 2 * b + 2)
                    pe.wait_ge(sq_ready, LEAD + BATCH * i + b - 1)
                    outs = [ps[r:r + HD1, 6 + b % 2, 0:SEQ] for r in (0, HD1)]
                    for n, out in enumerate(outs):
                        pe.matmul(out, v[:, TPB * b, n * HD1:(n + 1) * HD1], s_m[:, (2 * b + n) % 4, 0:SEQ], start=True, stop=False)
                    for n, out in enumerate(outs):
                        mm = pe.matmul(out[:, P:SEQ], v[:, TPB * b + 1, n * HD1:(n + 1) * HD1], s_m[:, (2 * b + n) % 4, SEQ:CAUSAL],
                                       start=False, stop=True)
                    mm.then_inc(pv_ps, 1)

                def project(b):
                    if b == 0:
                        pe.wait_ge(pre.wo_split, i + 1)
                    for o, ws, ready in ((gated_hi, (pre.wo_lo, pre.wo_hi), out_hi), (gated_lo, (pre.wo_hi,), out_lo)):
                        pe.wait_ge(ready, LEAD + BATCH * i + b + 1)
                        for t in range(TPB):
                            for w in ws:
                                mm = pe.matmul(ps[:, b, t * D:(t + 1) * D], o[:, b, t * P:(t + 1) * P], w[:], start=False, stop=False, skip_group_check=True)
                    mm.then_inc(op_ps, 1)

                for step in range(BATCH + 2):
                    if step < BATCH:
                        scores(2 * step)
                        scores(2 * step + 1)
                    if 1 <= step <= BATCH:
                        values(step - 1)
                    if step >= 2:
                        project(step - 2)
            pe.wait_ge(sq_added, LEAD + BATCH * PAIRS)
            pe.wait_ge(zeroed, 2)
            for t in range(NT):
                mm = pe.matmul(ps[:, 4, t:t + 1], sq_sum[:, t * P:(t + 1) * P], ones[:], start=True, stop=True)
            mm.then_inc(ss_ps, 1)


class GroupedWeights:

    def __init__(self, c, ctx):
        def sb(name, shape, dt=F32):
            return c.tile(ctx, "e_" + name, shape, dt)

        self.stage = sb("stage", [P, 1 + GROUP, KD, P])
        self.wh = sb("wh", [P, 1 + GROUP, KD, P], F32R)
        self.wl = sb("wl", [P, 1 + GROUP, KD, P], F32R)
        self.wv = sb("wv", [P, KD, HKV * P])
        self.wvh = sb("wvh", [P, KD, HKV * P], F32R)
        self.wvl = sb("wvl", [P, KD, HKV * P], F32R)
        self.rope = sb("rope", [P, 4, 512])
        self.loaded, self.tables_in, self.hi = c.sems(ctx, "e", "loaded tables_in hi")
        self.c = c

    def load(self, sp):
        dram = self.c.dram
        for tile, source in ((self.stage, dram["w_grouped"][0]), (self.wv, dram["wv_grouped"])):
            sp.dma_start(tile[:], source).then_inc(self.loaded, 16)
        sp.dma_start(self.rope[:], dram["rope"]).then_inc(self.tables_in, 16)

    def prepare(self, pool):
        pass

    def split(self, eng):
        eng.wait_ge(self.loaded, 32)
        eng.tensor_copy(self.wh[:], self.stage[:]).then_inc(self.hi, 1)
        eng.tensor_copy(self.wvh[:], self.wv[:]).then_inc(self.hi, 1)
        eng.wait_ge(self.hi, 2)
        eng.tensor_tensor(self.wl[:], self.stage[:], self.wh[:].bitcast(F32), ALU.subtract)
        eng.tensor_tensor(self.wvl[:], self.wv[:], self.wvh[:].bitcast(F32), ALU.subtract)


def layer1_grouped_attention(c, pre, spent):
    nc, ps = c.nc, c.ps
    PIECES = 1 + GROUP
    with ExitStack() as ctx:
        def sb(name, shape, dt=F32):
            return c.tile(ctx, "e_" + name, shape, dt)

        stage, wh, wl, rope = pre.stage, pre.wh, pre.wl, pre.rope
        wo = sb("wo", [P, GROUP, D])
        wo_hi = sb("wo_hi", [P, GROUP, D], F32R)
        wo_lo = sb("wo_lo", [P, GROUP, D], F32R)
        v_all = sb("v_all", [P, NT, HKV * P])
        k_T = spent.stage[:, 0:TOK]
        v = sb("v", [P, NT, P])
        q_T = sb("q_T", [P, 2, TOK])
        by_cos = sb("by_cos", [P, 2, 512])
        by_sin = sb("by_sin", [P, 2, 512])
        neg_max = sb("neg_max", [P, 4, 2])
        sums = sb("sums", [P, 4, 2])
        rsum = sb("rsum", [P, 4, 2])
        probs = sb("probs", [P, 4, CAUSAL])
        probsT = sb("probsT", [P, 2, CAUSAL])
        o_hi = sb("o_hi", [P, 2, SEQ], F32R)
        o_lo = sb("o_lo", [P, 2, SEQ], F32R)
        table = sb("table", [P, 1])

        stage_in, wo_in = c.sems(ctx, "e", "stage_in wo_in")
        pe_sems = proj_ps, v_ps, s_ps, t_ps, pv_ps, wo_ps = c.sems(ctx, "e", "proj_ps v_ps s_ps t_ps pv_ps wo_ps")
        dve_sems = w_hi, w_split, turned_ps, nm_ready, rs_ready, v_copied, pT_ready, wo_high, wo_split, o_low = c.sems(
            ctx, "e", "w_hi w_split turned_ps nm_ready rs_ready v_copied pT_ready wo_high wo_split o_low")
        act_sems = v_ready, p_ready, o_high = c.sems(ctx, "e", "v_ready p_ready o_high")
        pool_sems = roped, pn_ready = c.sems(ctx, "e", "roped pn_ready")
        block = ctx.enter_context(nc.Block())
        ITEMS = GROUP * BATCH

        ring = []
        for t in range(ITEMS):
            ring.append(("s", t))
            if t % 4 in (1, 2):
                ring.append(("q", 2 * (t // 4 + 1) + t % 4 - 1))
        ring += [("k", 0), ("k", 1)]
        at = {key: n for n, key in enumerate(ring)}
        order = [r for r in ring if r[0] != "s"]
        first = [("k", 1), ("k", 0), ("q", 2 * GROUP), ("q", 2 * GROUP + 1)]
        project_at = {t: ("q", 2 * (t // 4 + 1) + t % 4 - 1) for t in range(ITEMS) if t % 4 in (1, 2)}
        project_at |= {ITEMS: ("k", 0), ITEMS + 1: ("k", 1)}
        split_at = {3: 0, 4: 1, 7: 2, 8: 3, 11: 4}
        split_out_at = {5: 3, 9: 0, 12: 1, ITEMS: 2}

        def projected(g, key):
            return LEAD + len(first) + len(order) * g + order.index(key) + 1

        def freed(eng, g, key):
            n = at[key] - 2
            last, g = ring[n % len(ring)], g - 1 if n < 0 else g
            if last[0] == "s":
                eng.wait_ge(p_ready, LEAD + 2 * (ITEMS * g + last[1] + 1))
            else:
                eng.wait_ge(turned_ps, projected(g, last))

        def half_of(key):
            return slice(key[1] % 2 * 512, (key[1] % 2 + 1) * 512)

        @block.sync
        def _(sp):
            sp.dma_start(wo[:], c.dram["wo_grouped"][0]).then_inc(wo_in, 16)
            with sp.Fori(0, HKV) as g:
                sp.wait_ge(w_split, LEAD + PIECES * g)
                sp.dma_start(stage[:].rearrange("p a k n -> p (a k) n"),
                             c.dram["w_grouped"][bass.ds(g + 1, 1)].rearrange("b p a k n -> p (b a k) n")).then_inc(stage_in, 16)
                sp.wait_ge(wo_split, LEAD + GROUP * (g + 1))
                sp.dma_start(wo[:], c.dram["wo_grouped"][bass.ds(g + 1, 1)].rearrange("b p h d -> p (b h) d")).then_inc(wo_in, 16)

        @block.gpsimd
        def _(pool):
            give_lead(pool, pool_sems)

            def rotate(key, count, slot):
                pool.wait_ge(turned_ps, count)
                dst = k_T[:, half_of(key)] if key[0] == "k" else q_T[:, key[1] // 2 % 2, half_of(key)]
                pool.tensor_tensor(dst, by_cos[:, slot, :], by_sin[:, slot, :], ALU.add).then_inc(roped, 1)

            for n, key in enumerate(first):
                rotate(key, LEAD + n + 1, n % 2)
            with pool.Fori(0, HKV) as g:
                for t in range(ITEMS + 2):
                    if 1 <= t <= ITEMS:
                        u = t - 1
                        pool.wait_ge(rs_ready, LEAD + ITEMS * g + u + 1)
                        pool.tensor_tensor(probs[:, u % 4, 0:P], probs[:, u % 4, 0:P], rsum[:, u % 4, 0:1].broadcast_to((P, P)), ALU.mult).then_inc(pn_ready, 1)
                        pool.tensor_tensor(probs[:, u % 4, P:CAUSAL], probs[:, u % 4, P:CAUSAL], rsum[:, u % 4, 1:2].broadcast_to((P, SEQ)), ALU.mult).then_inc(pn_ready, 1)
                    if t in project_at:
                        key = project_at[t]
                        if key == ("k", 0):
                            pool.wait_ge(s_ps, LEAD + ITEMS * g + ITEMS)
                        rotate(key, projected(g, key), order.index(key) % 2)

        @block.vector
        def _(dve):
            give_lead(dve, dve_sems)

            def rotate(key, count, slot, bank):
                dve.wait_ge(proj_ps, count)
                dve.wait_ge(roped, count - 2)
                cos, sin = (rope[:, 0], rope[:, 1]) if key[0] == "k" else (rope[:, 2], rope[:, 3])
                dve.tensor_tensor(by_cos[:, slot, :], bank, cos, ALU.mult)
                dve.tensor_tensor(by_sin[0:HDQ // 2, slot, :], bank[HDQ // 2:P], sin[HDQ // 2:P], ALU.mult)
                dve.tensor_tensor(by_sin[HDQ // 2:P, slot, :], bank[0:HDQ // 2], sin[0:HDQ // 2], ALU.mult).then_inc(turned_ps, 1)

            dve.wait_ge(pre.tables_in, 16)
            def split_out(head, n):
                dve.tensor_copy(wo_hi[:, head], wo[:, head]).then_inc(wo_high, 1)
                dve.wait_ge(wo_high, LEAD + n)
                dve.tensor_tensor(wo_lo[:, head], wo[:, head], wo_hi[:, head].bitcast(F32), ALU.subtract).then_inc(wo_split, 1)

            for n, key in enumerate(first):
                rotate(key, LEAD + n + 1, n % 2, ps[:, 4 + at[key] % 2, :])
            dve.wait_ge(wo_in, 16)
            for head in range(GROUP - 1):
                split_out(head, head + 1)
            dve.wait_ge(v_ready, NT + LEAD)
            with dve.Fori(0, HKV) as g:
                for t in range(ITEMS + 3):
                    if t < ITEMS:
                        dve.wait_ge(s_ps, LEAD + ITEMS * g + t + 1)
                        dve.wait_ge(p_ready, LEAD + 2 * (ITEMS * g + t) - 6)
                        bank = ps[:, 4 + at["s", t] % 2, :]
                        dve.tensor_reduce(neg_max[:, t % 4, 0:1], bank[:, 0:P], X, ALU.max, negate=True).then_inc(nm_ready, 1)
                        dve.tensor_reduce(neg_max[:, t % 4, 1:2], bank[:, P:CAUSAL], X, ALU.max, negate=True).then_inc(nm_ready, 1)
                    if 1 <= t <= ITEMS:
                        u = t - 1
                        dve.wait_ge(p_ready, LEAD + 2 * (ITEMS * g + u) + 2)
                        dve.wait_ge(pn_ready, LEAD + 2 * (ITEMS * g + u) - 6)
                        dve.reciprocal(rsum[:, u % 4, :], sums[:, u % 4, :]).then_inc(rs_ready, 1)
                    if t == 1:
                        dve.wait_ge(pv_ps, LEAD + ITEMS * g)
                        dve.tensor_scalar(v[:], v_all[:, :, bass.ds(g * P, P)], 1.0, None, ALU.mult).then_inc(v_copied, 1)
                    if t in project_at:
                        key = project_at[t]
                        rotate(key, projected(g, key), order.index(key) % 2, ps[:, 4 + at[key] % 2, :])
                    if 2 <= t < ITEMS + 2 and t not in project_at:
                        u = t - 2
                        dve.wait_ge(t_ps, LEAD + ITEMS * g + u + 1)
                        dve.wait_ge(pv_ps, LEAD + ITEMS * g + u - 1)
                        dve.tensor_copy(probsT[:, u % 2, :], ps[:, 6, 0:CAUSAL]).then_inc(pT_ready, 1)
                    if t >= 3:
                        u = t - 3
                        dve.wait_ge(o_high, LEAD + ITEMS * g + u + 1)
                        dve.wait_ge(wo_ps, LEAD + ITEMS * g + u - 1)
                        dve.tensor_tensor(o_lo[:, u % 2, :], ps[:, 7, 0:SEQ], o_hi[:, u % 2, :].bitcast(F32), ALU.subtract).then_inc(o_low, 1)
                    if t in split_out_at:
                        head = split_out_at[t]
                        n = list(split_out_at).index(t)
                        dve.wait_ge(wo_in, 16 * g + (16 if n == 0 else 32))
                        dve.wait_ge(wo_ps, LEAD + ITEMS * g + (0 if n == 0 else 4 * (head + 1)))
                        split_out(head, GROUP * g + GROUP + n)
                    if t in split_at:
                        piece = split_at[t]
                        dve.wait_ge(stage_in, 16 * g + 16)
                        dve.tensor_copy(wh[:, piece], stage[:, piece]).then_inc(w_hi, 1)
                        dve.wait_ge(w_hi, LEAD + PIECES * g + piece + 1)
                        dve.tensor_tensor(wl[:, piece], stage[:, piece], wh[:, piece].bitcast(F32), ALU.subtract).then_inc(w_split, 1)
            dve.wait_ge(wo_ps, LEAD + HKV * ITEMS)
            for bank in range(4):
                dve.tensor_tensor(c.y[:, 2 * bank:2 * bank + 2, :], ps[:, bank, :].rearrange("p (t d) -> p t d", t=2),
                                  c.x[:, 2 * bank:2 * bank + 2, :], ALU.add)

        @block.scalar
        def _(act):
            give_lead(act, act_sems)
            for t in range(NT):
                act.wait_ge(v_ps, LEAD + t + 1)
                act.activation(v_all[:, t, :], ps[:, 6 + t % 2, :], ACT.Copy).then_inc(v_ready, 1)
            with act.Fori(0, HKV) as g:
                act.activation(table[:], c.iota[:, 0:1], ACT.Exp)
                for t in range(ITEMS + 3):
                    if t < ITEMS:
                        act.wait_ge(nm_ready, LEAD + 2 * (ITEMS * g + t) + 2)
                        act.wait_ge(t_ps, LEAD + ITEMS * g + t - 3)
                        bank = ps[:, 4 + at["s", t] % 2, :]
                        for b, cols in enumerate((slice(0, P), slice(P, CAUSAL))):
                            act.activation(probs[:, t % 4, cols], bank[:, cols], ACT.Exp, bias=neg_max[:, t % 4, b:b + 1],
                                           accum_out=sums[:, t % 4, b:b + 1]).then_inc(p_ready, 1)
                    if t >= 2 and t in project_at:
                        u = t - 2
                        act.wait_ge(t_ps, LEAD + ITEMS * g + u + 1)
                        act.wait_ge(pv_ps, LEAD + ITEMS * g + u - 1)
                        act.activation(probsT[:, u % 2, :], ps[:, 6, 0:CAUSAL], ACT.Copy).then_inc(pT_ready, 1)
                    if t >= 3:
                        u = t - 3
                        act.wait_ge(pv_ps, LEAD + ITEMS * g + u + 1)
                        act.wait_ge(wo_ps, LEAD + ITEMS * g + u - 1)
                        act.activation(o_hi[:, u % 2, :], ps[:, 7, 0:SEQ], ACT.Copy).then_inc(o_high, 1)

        @block.tensor
        def _(pe):
            give_lead(pe, pe_sems)

            def project(key):
                piece = 0 if key[0] == "k" else 1 + key[1] // 2 % GROUP
                half = half_of(key)
                split_product(pe, ps[:, 4 + at[key] % 2, :], lambda k: wh[:, piece, k, :], lambda k: wl[:, piece, k, :],
                              lambda k: c.xTh[:, k, half], lambda k: c.xTl[:, k, half], range(KD)).then_inc(proj_ps, 1)

            def project_v(t):
                if t >= 2:
                    pe.wait_ge(v_ready, LEAD + t - 1)
                tok = slice(t * P, (t + 1) * P)
                split_product(pe, ps[:, 6 + t % 2, :], lambda k: c.xTh[:, k, tok], lambda k: c.xTl[:, k, tok],
                              lambda k: pre.wvh[:, k, :], lambda k: pre.wvl[:, k, :], range(KD)).then_inc(v_ps, 1)

            project(first[0])
            project(first[1])
            for t in range(2):
                project_v(t)
            for bank in range(4):
                pe.matmul(ps[:, bank, :], c.warm16[:, 0:P], c.warm16[:], start=True, stop=False, skip_group_check=True)
            pe.wait_ge(turned_ps, LEAD + 2)
            project(first[2])
            for t in range(2, 4):
                project_v(t)
            pe.wait_ge(turned_ps, LEAD + 3)
            project(first[3])
            for t in range(4, NT):
                project_v(t)
            pe.wait_ge(v_ready, LEAD + NT)
            with pe.Fori(0, HKV) as g:
                for t in range(ITEMS + 4):
                    if t < ITEMS:
                        b = t % 4
                        if b == 0:
                            pe.wait_ge(roped, LEAD + len(first) + len(order) * g + 2 * (t // 4))
                        freed(pe, g, ("s", t))
                        bank, q = ps[:, 4 + at["s", t] % 2, :], q_T[:, t // 4 % 2, b * SEQ:(b + 1) * SEQ]
                        keys = k_T[:, b * SEQ:(b + 1) * SEQ]
                        pe.matmul(bank[:, 0:CAUSAL], c.ident16[:], c.neg16[:], start=True, stop=False)
                        pe.matmul(bank[:, 0:P], q[:, 0:P], keys[:, 0:P], start=False, stop=False)
                        pe.matmul(bank[:, P:CAUSAL], q[:, P:SEQ], keys, start=False, stop=True).then_inc(s_ps, 1)
                    if t in project_at:
                        key = project_at[t]
                        pe.wait_ge(w_split, LEAD + PIECES * g + (2 if t >= 4 * (GROUP - 1) else 0))
                        freed(pe, g, key)
                        project(key)
                    if t >= 4:
                        u = t - 4
                        if u % 4 == 0:
                            pe.wait_ge(wo_split, LEAD + GROUP * g + (GROUP if u // 4 == GROUP - 1 else GROUP - 1))
                        for o, ws, ready in ((o_hi, (wo_lo, wo_hi), o_high), (o_lo, (wo_hi,), o_low)):
                            pe.wait_ge(ready, LEAD + ITEMS * g + u + 1)
                            for h in range(TPB):
                                for w in ws:
                                    mm = pe.matmul(ps[:, u % 4, h * D:(h + 1) * D], o[:, u % 2, h * P:(h + 1) * P], w[:, u // 4, :],
                                                   start=False, stop=False, skip_group_check=True)
                        mm.then_inc(wo_ps, 1)
                    if 2 <= t < ITEMS + 2:
                        u = t - 2
                        pe.wait_ge(pn_ready, LEAD + 2 * (ITEMS * g + u) + 2)
                        pe.wait_ge(pT_ready, LEAD + ITEMS * g + u)
                        for n in range(3):
                            mm = pe.transpose(ps[:, 6, n * P:(n + 1) * P], probs[:, u % 4, n * P:(n + 1) * P], c.ident)
                        mm.then_inc(t_ps, 1)
                    if 3 <= t < ITEMS + 3:
                        u, b = t - 3, (t - 3) % 4
                        if u == 0:
                            pe.wait_ge(v_copied, LEAD + g + 1)
                        pe.wait_ge(pT_ready, LEAD + ITEMS * g + u + 1)
                        pe.wait_ge(o_low, LEAD + ITEMS * g + u)
                        out, s = ps[:, 7, 0:SEQ], probsT[:, u % 2, :]
                        pe.matmul(out, v[:, TPB * b, :], s[:, 0:SEQ], start=True, stop=False)
                        pe.matmul(out[:, P:SEQ], v[:, TPB * b + 1, :], s[:, SEQ:CAUSAL], start=False, stop=True).then_inc(pv_ps, 1)


class ExpertWeights:
    W1, W3, W2, WC = 0, KD * FF, 2 * KD * FF, 3 * KD * FF

    def __init__(self, c, ctx):
        def sb(name, shape, dt=F32):
            return c.tile(ctx, "f_" + name, shape, dt)

        self.c = c
        self.stage = sb("stage", [P, self.WC])
        self.wh = [sb(f"wh{n}", [P, self.WC], F32R) for n in range(2)]
        self.wl = [sb(f"wl{n}", [P, self.WC], F32R) for n in range(2)]
        self.wg = sb("wg", [P, KD, EXPERTS])
        self.wgh = sb("wgh", [P, KD, EXPERTS], F32R)
        self.wgl = sb("wgl", [P, KD, EXPERTS], F32R)
        self.nought = sb("nought", [P, 1])
        self.loaded, self.rest_in, self.hi, self.w_hi, self.w_split, self.w2_split = c.sems(ctx, "f", "loaded rest_in hi w_hi w_split w2_split")

    def load(self, sp):
        sp.dma_start(self.wg[:], self.c.dram["w_router"]).then_inc(self.loaded, 16)
        for start in (self.W1, self.W3, self.W2):
            part = slice(start, start + KD * FF)
            sp.dma_start(self.stage[:, part], self.c.dram["w_experts"][0][:, part]).then_inc(self.loaded if start == self.W1 else self.rest_in, 16)

    def split(self, pool, slot, n, cols, done):
        nought = self.nought[:].broadcast_to((P, cols.stop - cols.start))
        pool.tensor_tensor(self.wh[slot][:, cols], self.stage[:, cols], nought, ALU.add).then_inc(self.w_hi, 1)
        pool.wait_ge(self.w_hi, n)
        pool.tensor_tensor(self.wl[slot][:, cols], self.stage[:, cols], self.wh[slot][:, cols].bitcast(F32), ALU.subtract).then_inc(done, 1)

    def prepare(self, pool):
        pool.memset(self.nought[:], 0.0).then_inc(self.hi, 1)
        pool.wait_ge(self.hi, 1)
        pool.wait_ge(self.loaded, 32)
        pool.tensor_copy(self.wgh[:], self.wg[:]).then_inc(self.hi, 1)
        pool.wait_ge(self.hi, 2)
        pool.tensor_tensor(self.wgl[:], self.wg[:], self.wgh[:].bitcast(F32), ALU.subtract)
        self.split(pool, 0, 1, slice(self.W1, self.W1 + KD * FF), self.w_split)


def layer1_experts(c, pre):
    nc, ps = c.nc, c.ps
    W1, W3, W2, WC = pre.W1, pre.W3, pre.W2, pre.WC
    FT = FF // P
    with ExitStack() as ctx:
        def sb(name, shape, dt=F32):
            return c.tile(ctx, "f_" + name, shape, dt)

        stage, wh, wl, wgh, wgl, w_split, w2_split = pre.stage, pre.wh, pre.wl, pre.wgh, pre.wgl, pre.w_split, pre.w2_split
        z_T = sb("z_T", [EXPERTS, TOK])
        lg = sb("lg", [P, 8, NT, EXPERTS])
        gs = sb("gs", [P, 8, NT])
        weight = sb("weight", [P, EXPERTS, NT])
        act1 = sb("act1", [P, 2, 512])
        hid = sb("hid", [P, 2, 512])
        hidh = sb("hidh", [P, 2, FT, 512], F32R)
        hidl = sb("hidl", [P, 2, FT, 512], F32R)

        (stage_in,) = c.sems(ctx, "f", "stage_in")
        pe_sems = z_ps, lg_ps, a_ps, b_ps, o_ps = c.sems(ctx, "f", "z_ps lg_ps a_ps b_ps o_ps")
        dve_sems = chain, d_ready, w_ready, h_ready, lo_ready, acc = c.sems(ctx, "f", "chain d_ready w_ready h_ready lo_ready acc")
        act_sems = z_copied, ex_ready, silu_ready, hi_ready = c.sems(ctx, "f", "z_copied ex_ready silu_ready hi_ready")
        block = ctx.enter_context(nc.Block())
        STEPS = 2 * 2 * FT

        @block.sync
        def _(sp):
            sp.wait_ge(w2_split, 1)
            with sp.Fori(0, EXPERTS) as e:
                sp.wait_ge(w_split, e + 2)
                sp.dma_start(stage[:], c.dram["w_experts"][bass.ds(e + 1, 1)].rearrange("a p n -> p (a n)")).then_inc(stage_in, 16)

        @block.gpsimd
        def _(pool):
            pool.wait_ge(pre.rest_in, 32)
            pre.split(pool, 0, 2, slice(W3, W3 + KD * FF), w_split)
            pre.split(pool, 0, 3, slice(W2, W2 + KD * FF), w2_split)
            with pool.Fori(0, EXPERTS // 2) as i:
                for slot, expert in ((1, 1), (0, 2)):
                    pool.wait_ge(o_ps, LEAD + 16 * i + 8 * (expert - 1))
                    pool.wait_ge(stage_in, 32 * i + 16 * expert)
                    pre.split(pool, slot, 2 * i + expert + 3, slice(0, WC), w_split)

        @block.vector
        def _(dve):
            give_lead(dve, dve_sems)
            link = Chain(dve, chain, LEAD)
            logits, eq, cand, hot1, rest, hot2, w_1, w_2 = (lg[:, n] for n in range(8))
            m1, m2, first, diff, ex, den, p1, p2 = (gs[:, n] for n in range(8))

            def wide(a):
                return a.unsqueeze(2).broadcast_to((P, NT, EXPERTS))

            iota = c.iota[:, 0:EXPERTS].unsqueeze(1).broadcast_to((P, NT, EXPERTS))
            dve.wait_ge(lg_ps, LEAD + 1)
            link(dve.tensor_copy(logits.rearrange("p t e -> p (t e)"), ps[:, 0, 0:NT * EXPERTS]))

            def best(values, largest, hot):
                link(dve.tensor_reduce(largest, values, X, ALU.max))
                link(dve.tensor_tensor(eq, values, wide(largest), ALU.is_equal))
                link(dve.scalar_tensor_tensor(cand, eq, -16.0, iota, ALU.mult, ALU.add))
                link(dve.tensor_reduce(first, cand, X, ALU.min))
                link(dve.tensor_tensor(hot, cand, wide(first), ALU.is_equal))

            best(logits, m1, hot1)
            link(dve.scalar_tensor_tensor(rest, hot1, -1e30, logits, ALU.mult, ALU.add))
            best(rest, m2, hot2)
            dve.tensor_tensor(diff, m2, m1, ALU.subtract).then_inc(d_ready, 1)
            dve.wait_ge(ex_ready, LEAD + 1)
            link(dve.tensor_scalar(den, ex, 1.0, None, ALU.add))
            link(dve.reciprocal(p1, den))
            link(dve.tensor_tensor(p2, p1, ex, ALU.mult))
            link(dve.tensor_tensor(w_1, hot1, wide(p1), ALU.mult))
            link(dve.tensor_tensor(w_2, hot2, wide(p2), ALU.mult))
            dve.tensor_tensor(weight[:].rearrange("p e t -> p t e"), w_1, w_2, ALU.add).then_inc(w_ready, 1)
            for t in range(NT):
                dve.tensor_tensor(c.y[:, t, :], c.y[:, t, :], c.x[:, t, :], ALU.add).then_inc(acc, 1)
            dve.wait_ge(w_ready, LEAD + 1)
            with dve.Fori(0, EXPERTS // 2) as i:
                def down(s):
                    for t in range(4):
                        n = 4 * s + t
                        tok = s % 2 * 4 + t
                        dve.wait_ge(o_ps, LEAD + 16 * i + n + 1)
                        dve.wait_ge(acc, LEAD + NT + 16 * i + n - 7)
                        dve.scalar_tensor_tensor(c.y[:, tok, :], ps[:, 6 + n % 2, 0:D], weight[:, bass.ds(2 * i + s // 2, 1), tok:tok + 1].rearrange("p a b -> p (a b)"),
                                                 c.y[:, tok, :], ALU.mult, ALU.add).then_inc(acc, 1)

                for n in range(STEPS):
                    s, f = n // FT, n % FT
                    dve.wait_ge(b_ps, LEAD + STEPS * i + n + 1)
                    dve.wait_ge(silu_ready, LEAD + STEPS * i + n + 1)
                    dve.wait_ge(hi_ready, LEAD + STEPS * i + n - 1)
                    dve.tensor_tensor(hid[:, n % 2, :], act1[:, n % 2, :], ps[:, 4 + n % 2, :], ALU.mult).then_inc(h_ready, 1)
                    dve.wait_ge(hi_ready, LEAD + STEPS * i + n + 1)
                    dve.tensor_tensor(hidl[:, s % 2, f, :], hid[:, n % 2, :], hidh[:, s % 2, f, :].bitcast(F32), ALU.subtract).then_inc(lo_ready, 1)
                    if s >= 1 and f == FT - 1:
                        down(s - 1)
                down(3)

        @block.scalar
        def _(act):
            give_lead(act, act_sems)
            for n in range(2):
                act.wait_ge(z_ps, LEAD + n + 1)
                act.activation(z_T[:, n * 512:(n + 1) * 512], ps[0:EXPERTS, n, :], ACT.Copy).then_inc(z_copied, 1)
            act.wait_ge(d_ready, LEAD + 1)
            act.activation(gs[:, 4], gs[:, 3], ACT.Exp).then_inc(ex_ready, 1)
            with act.Fori(0, EXPERTS // 2) as i:
                for n in range(STEPS):
                    s, f = n // FT, n % FT
                    act.wait_ge(a_ps, LEAD + STEPS * i + n + 1)
                    act.wait_ge(h_ready, LEAD + STEPS * i + n - 1)
                    act.activation(act1[:, n % 2, :], ps[:, 2 + n % 2, :], ACT.Silu).then_inc(silu_ready, 1)
                    act.wait_ge(h_ready, LEAD + STEPS * i + n + 1)
                    act.wait_ge(o_ps, LEAD + 16 * i + 4 * s - 4)
                    act.activation(hidh[:, s % 2, f, :], hid[:, n % 2, :], ACT.Copy).then_inc(hi_ready, 1)

        @block.tensor
        def _(pe):
            give_lead(pe, pe_sems)
            for n in range(2):
                half = slice(n * 512, (n + 1) * 512)
                split_product(pe, ps[0:EXPERTS, n, :], lambda k: wgh[:, k, :], lambda k: wgl[:, k, :],
                              lambda k: c.xTh[:, k, half], lambda k: c.xTl[:, k, half], range(KD)).then_inc(z_ps, 1)
            keep_warm(c, pe, ps[:, 2, :], 8)
            pe.wait_ge(z_copied, LEAD + 2)
            for t in range(NT):
                mm = pe.transpose(ps[:, 0, t * EXPERTS:(t + 1) * EXPERTS], z_T[:, t * P:(t + 1) * P], c.ident[0:EXPERTS, 0:EXPERTS])
            mm.then_inc(lg_ps, 1)
            pe.wait_ge(w_split, 2)
            with pe.Fori(0, EXPERTS // 2) as i:
                def up(s):
                    e, half = s // 2, slice(s % 2 * 512, (s % 2 + 1) * 512)
                    if s % 2 == 0:
                        pe.wait_ge(w_split, 2 * i + e + 2)
                    for f in range(FT):
                        n = FT * s + f
                        for base, bank, used, done in ((W1, 2, silu_ready, a_ps), (W3, 4, h_ready, b_ps)):
                            pe.wait_ge(used, LEAD + STEPS * i + n - 1)
                            at = [slice(base + k * FF + f * P, base + k * FF + (f + 1) * P) for k in range(KD)]
                            split_product(pe, ps[:, bank + n % 2, :], lambda k: wh[e][:, at[k]], lambda k: wl[e][:, at[k]],
                                          lambda k: c.xTh[:, k, half], lambda k: c.xTl[:, k, half], range(KD)).then_inc(done, 1)

                def down(s):
                    e = s // 2
                    if s == 0:
                        pe.wait_ge(w2_split, 1)
                    pe.wait_ge(lo_ready, LEAD + STEPS * i + FT * (s + 1))
                    for t in range(4):
                        n = 4 * s + t
                        pe.wait_ge(acc, LEAD + NT + 16 * i + n - 1)
                        split_product(pe, ps[:, 6 + n % 2, 0:D], lambda f: hidh[:, s % 2, f, t * P:(t + 1) * P],
                                      lambda f: hidl[:, s % 2, f, t * P:(t + 1) * P],
                                      lambda f: wh[e][:, W2 + f * D:W2 + (f + 1) * D], lambda f: wl[e][:, W2 + f * D:W2 + (f + 1) * D],
                                      range(FT)).then_inc(o_ps, 1)

                for s in range(4):
                    up(s)
                    if s >= 1:
                        down(s - 1)
                down(3)


def build(nc, dram, out):
    with ExitStack() as ctx:
        c = Core(nc, dram, out, ctx)
        layer0_linear_attention(c)
        normalise(c, "n1", c.y, c.x, turned="split")
        with ExitStack() as held:
            decay = DecayWeights(c, held)
            layer0_gated_attention(c, decay)
            grouped = GroupedWeights(c, held)
            normalise(c, "n2", c.y, c.x, turned="both", following=grouped)
            layer1_decay_attention(c, decay, grouped)
            normalise(c, "n3", c.y, c.x, turned="split", weight=dram["norm1"], rms_too=c.scratch)
            layer1_grouped_attention(c, grouped, decay)
        with ExitStack() as held:
            experts = ExpertWeights(c, held)
            normalise(c, "n5", c.y, c.scratch, rms=True, turned="split", weight=dram["norm2"], following=experts)
            layer1_experts(c, experts)
        normalise(c, "n6", c.y, c.x, store=True)


def blocks(wT):
    return np.ascontiguousarray(wT.reshape(wT.shape[0] // P, P, wT.shape[1]).transpose(1, 0, 2))


def constants():
    ident = np.eye(P)
    key, q = np.mgrid[0:P, 0:P]
    tri = (q >= key).astype(np.float32)
    tri3 = np.concatenate([tri, np.ones((P, P)), tri], axis=1)
    neg = np.where(key <= q, 0.0, -1e30).T
    neg3 = np.concatenate([neg, np.zeros((P, P)), neg], axis=1)
    par = np.stack([(np.arange(P) // HD0 % 2 == n) * float(HD0) ** -0.5 for n in range(2)], axis=1)
    iota = np.tile(np.arange(16.0), (P, 1))
    return np.concatenate([ident, tri3, neg3, par, iota], axis=1).astype(np.float32)


def rope_tables():
    inv = (1.0 / np.float32(1000000.0) ** (np.arange(0, HDQ, 2, dtype=np.float32) / HDQ)).astype(np.float32)
    ang = np.arange(SEQ, dtype=np.float32)[:, None] * inv[None, :]
    cos = np.concatenate([np.cos(ang), np.cos(ang)], axis=1).T
    sin = np.concatenate([np.sin(ang), -np.sin(ang)], axis=1).T
    cos, sin = np.tile(cos, (1, 2)), np.tile(sin, (1, 2))
    r = float(HDQ) ** -0.5
    return np.stack([cos, sin, cos * r, sin * r], axis=1).astype(np.float32)


def decays():
    factor = 1.0 - 0 / (32 - 1 + 1e-05) + 1e-05
    slope = (2.0 ** (-8.0 / H1)) ** (np.arange(H1) + 1.0) * factor
    dist = np.arange(SEQ)[None, :] - np.arange(P)[:, None]
    d = np.where(dist >= 0, np.exp(-slope[:, None, None] * np.maximum(dist, 0)), 0.0)
    d = np.concatenate([d, d[:, :, 0:P]], axis=2)
    return d.reshape(PAIRS, 2, P, CAUSAL).transpose(0, 2, 1, 3).astype(np.float32)


def padded(steps):
    return np.stack(steps + [np.zeros_like(steps[0])])


def kernel(**inputs):
    import concourse.bacc as bacc
    from concourse.bass_utils import run_bass_kernel_spmd

    a = {k: np.asarray(v) for k, v in inputs.items()}
    x = a["L0_attn_x"].reshape(TOK, D)
    diag = np.zeros((P, 4, P), np.float32)
    for n, name in enumerate(("fq1", "fq2", "fk1", "fk2")):
        for h in range(P // HD0):
            s = slice(h * HD0, (h + 1) * HD0)
            diag[s, n, s] = a[f"L0_attn_{name}_w"].T
    arrays = {
        "consts": constants(),
        "x": blocks(x),
        "xT": blocks(x.T),
        "w0": np.stack([blocks(a[f"L0_attn_{n}"].T) for n in ("wq", "wk", "wv")], axis=1),
        "maps": diag,
        "vecs": np.stack([np.tile(a[f"L0_attn_{n}"], P // HD0) for n in ("fq1_b", "fq2_b", "fk1_b", "fk2_b", "norm_w")], axis=1),
        "wo0": blocks(a["L0_attn_wo"].T),
        "w_gated": blocks(np.concatenate([a["L0_ffn_W_qkv"], a["L0_ffn_W_gate"]], axis=0).T),
    }
    qkv = a["L1_attn_qkv_w"].reshape(PAIRS, 2, 3, HD1, D).transpose(0, 2, 1, 3, 4).reshape(PAIRS, 3 * P, D)
    qk, v = qkv[:, :2 * P], qkv[:, 2 * P:]
    gates = a["L1_attn_gate_w"].reshape(PAIRS, P, D)
    wo_decay, norm_decay = a["L1_attn_out_w"].T.reshape(PAIRS, P, D), a["L1_attn_norm_w"].reshape(PAIRS, P, 1)
    wq, wk, wv = (a[f"L1_ffn_{n}"] for n in ("wq", "wk", "wv"))
    w1, w3, w2 = (a[f"L1_ffn_{n}"] for n in ("w1", "w3", "w2"))

    def head(w, h):
        return blocks(w[:, h * HDQ:(h + 1) * HDQ])

    arrays |= {
        "w_decay": padded([np.concatenate([blocks(np.concatenate([qk[i], gates[i], v[i]], axis=0).T).reshape(P, -1), wo_decay[i], norm_decay[i]], axis=1)
                           for i in range(PAIRS)]),
        "decay": decays(),
        "norm1": a["L1_ffn_norm1_w"].reshape(KD, P).T,
        "norm2": a["L1_ffn_norm2_w"].reshape(KD, P).T,
        "w_grouped": padded([np.stack([head(wk, g)] + [head(wq, GROUP * g + j) for j in range(GROUP)], axis=1) for g in range(HKV)]),
        "wv_grouped": blocks(wv),
        "wo_grouped": padded([blocks(a["L1_ffn_wo"])[:, GROUP * g:GROUP * (g + 1)] for g in range(HKV)]),
        "rope": rope_tables(),
        "w_router": blocks(a["L1_ffn_gate_w"]),
        "w_experts": padded([np.concatenate([blocks(w[e]).reshape(P, -1) for w in (w1, w3, w2)], axis=1) for e in range(EXPERTS)]),
    }
    nc = bacc.Bacc("TRN2", target_bir_lowering=False, num_devices=1)
    dram = {}
    for name in arrays:
        arrays[name] = np.ascontiguousarray(arrays[name])
        dram[name] = nc.dram_tensor("in_" + name, arrays[name].shape, mybir.dt.from_np(arrays[name].dtype), kind="ExternalInput").ap()
    out = nc.dram_tensor("out", (TOK, D), F32, kind="ExternalOutput").ap()
    build(nc, dram, out.rearrange("(t p) d -> p t d", p=P))
    r = run_bass_kernel_spmd(nc, [{"in_" + k: v for k, v in arrays.items()}], core_ids=[0])
    return r.results[0]["out"].reshape(BATCH, SEQ, D)
```
